# Optimizing a Trainium2 kernel written in Bass

```python
import numpy as np
import jax
import jax.numpy as jnp

def _softmax(x, axis=-1):
    return jax.nn.softmax(x, axis=axis)

def _gelu(x):
    return jax.nn.gelu(x, approximate=True)

def _silu(x):
    return jax.nn.silu(x)

def _sigmoid(x):
    return jax.nn.sigmoid(x)

def _layernorm(x, axis=-1, eps=1e-05):
    m = jnp.mean(x, axis=axis, keepdims=True)
    v = jnp.var(x, axis=axis, keepdims=True)
    return (x - m) / jnp.sqrt(v + eps)

def _scatter_add(tgt, idx, src, axis=0):
    return tgt.at[idx].add(src)

def _segment_sum(src, seg, n):
    return jax.ops.segment_sum(src, seg, n)
kernel_name = 'mk_flamingo_gated_d2_seqx_r4_f86d08'

def setup_inputs(seed: int=0):
    np.random.seed(seed)
    _w = jnp.asarray

    def _rec_inputs():
        import jax
        import jax.numpy as jnp
        _rk = jax.random.key(seed)
        x = -0.0003929 + 0.9999 * jax.random.normal(jax.random.fold_in(_rk, 1), (16, 100, 256), jnp.float32)
        _lenS = 100 - jax.random.randint(jax.random.fold_in(_rk, 7), (16,), 0, max(1, 100 // 4) + 1, jnp.int32)
        _lenS2 = 361 - jax.random.randint(jax.random.fold_in(_rk, 8), (16,), 0, max(1, 361 // 4) + 1, jnp.int32)
        _ctx_768P = jax.random.normal(jax.random.fold_in(_rk, 11), (16, 16, 192), jnp.float32)
        _ctx_768c = jax.random.dirichlet(jax.random.fold_in(_rk, 511), 0.3 * jnp.ones((16,), jnp.float32), (16, 361))
        _ctx_768t = jnp.einsum('bsk,bkd->bsd', _ctx_768c, _ctx_768P)
        _ctx_768t = _ctx_768t * jax.lax.rsqrt(jnp.mean(jnp.square(_ctx_768t)) + 1e-12) * 0.953939
        ctx_768 = -0.00055796 + 0.999787 * (_ctx_768t + 0.3 * jax.random.normal(jax.random.fold_in(_rk, 611), (16, 361, 192), jnp.float32))
        _g = jax.random.normal(jax.random.fold_in(_rk, 9001), (2, 2), jnp.float32)
        _g = jnp.sign(_g) * jnp.maximum(jnp.abs(_g), 1.0) + (_g == 0) * 1.0
        g_xattn = _g[0]
        g_ffn = _g[1]
        return (x, ctx_768, g_xattn, g_ffn)
    x, ctx_768, g_xattn, g_ffn = _rec_inputs()

    def _L0_xattn_setup():
        import jax, jax.numpy as jnp
        import numpy as np
        IMAGE_DIM = 256
        TEXT_DIM = 192
        NUM_HEADS = 16
        HEAD_DIM = IMAGE_DIM // NUM_HEADS
        key = jax.random.key(seed)
        ks = jax.random.split(key, 14)
        B, N, M = (4, 1024, 128)
        s_img = 1.0 / np.sqrt(IMAGE_DIM)
        s_txt = 1.0 / np.sqrt(TEXT_DIM)
        s_ff = 1.0 / np.sqrt(2 * IMAGE_DIM)
        return {'x': jax.random.normal(ks[0], (B, N, IMAGE_DIM), jnp.float32), 'y': jax.random.normal(ks[1], (B, M, TEXT_DIM), jnp.float32), 'Wq': jax.random.normal(ks[2], (IMAGE_DIM, IMAGE_DIM), jnp.float32) * s_img, 'bq': jax.random.normal(ks[3], (IMAGE_DIM,), jnp.float32) * s_img, 'Wk': jax.random.normal(ks[4], (TEXT_DIM, IMAGE_DIM), jnp.float32) * s_txt, 'bk': jax.random.normal(ks[5], (IMAGE_DIM,), jnp.float32) * s_txt, 'Wv': jax.random.normal(ks[6], (TEXT_DIM, IMAGE_DIM), jnp.float32) * s_txt, 'bv': jax.random.normal(ks[7], (IMAGE_DIM,), jnp.float32) * s_txt, 'W1': jax.random.normal(ks[8], (IMAGE_DIM, 2 * IMAGE_DIM), jnp.float32) * s_img, 'b1': jax.random.normal(ks[9], (2 * IMAGE_DIM,), jnp.float32) * s_img, 'W2': jax.random.normal(ks[10], (2 * IMAGE_DIM, IMAGE_DIM), jnp.float32) * s_ff, 'b2': jax.random.normal(ks[11], (IMAGE_DIM,), jnp.float32) * s_ff}
    _L0_xattn_all = _L0_xattn_setup()
    _L0_xattn_in = {k: v for k, v in _L0_xattn_all.items() if k in ('Wq', 'bq', 'Wk', 'bk', 'Wv', 'bv', 'W1', 'b1', 'W2', 'b2')}
    del _L0_xattn_all

    def _L0_ffn_setup():
        import jax, jax.numpy as jnp
        import numpy as np
        H = 8
        QD = 64
        HALF = QD // 2
        DIMS = (32, 32)
        TOPK = 16
        DTK = 4
        EPS_BN = 1e-05
        EPS_NORM = 1e-12

        def _l2norm(x):
            n = jnp.linalg.norm(x, axis=-1, keepdims=True)
            return x / jnp.maximum(n, EPS_NORM)
        key = jax.random.key(seed)
        ks = jax.random.split(key, 6)
        B, S, D, O, E = (2, 128, 256, 256, 256)
        hidden_states = jax.random.normal(ks[0], (B, S, D), jnp.float32)
        Wq = jax.random.normal(ks[1], (D, H * QD), jnp.float32) * 0.02
        bq = jnp.zeros((H * QD,), jnp.float32)
        bn_gamma = jnp.ones((QD,), jnp.float32)
        bn_beta = jnp.zeros((QD,), jnp.float32)
        sub_key0 = jax.random.normal(ks[2], (DIMS[0], HALF), jnp.float32) * 0.02
        sub_key1 = jax.random.normal(ks[3], (DIMS[1], HALF), jnp.float32) * 0.02
        expert_down = jax.random.normal(ks[4], (E, D), jnp.float32) * 0.02
        expert_up = jax.random.normal(ks[5], (E, O), jnp.float32) * 0.02
        return {'hidden_states': hidden_states, 'Wq': Wq, 'bq': bq, 'bn_gamma': bn_gamma, 'bn_beta': bn_beta, 'sub_key0': sub_key0, 'sub_key1': sub_key1, 'expert_down': expert_down, 'expert_up': expert_up}
    _L0_ffn_all = _L0_ffn_setup()
    _L0_ffn_in = {k: v for k, v in _L0_ffn_all.items() if k in ('Wq', 'bq', 'bn_gamma', 'bn_beta', 'sub_key0', 'sub_key1', 'expert_down', 'expert_up')}
    del _L0_ffn_all

    def _L1_xattn_setup():
        import jax, jax.numpy as jnp
        import numpy as np
        HEADS = 8
        DIM_HEAD = 64
        QUERY_DIM = 256
        CONTEXT_DIM = 192
        INNER = HEADS * DIM_HEAD
        key = jax.random.key(seed)
        ks = jax.random.split(key, 7)
        B, Sq, Skv = (4, 1024, 256)
        x = jax.random.normal(ks[0], (B, Sq, QUERY_DIM), dtype=jnp.float32)
        context = jax.random.normal(ks[1], (B, Skv, CONTEXT_DIM), dtype=jnp.float32)
        Wq = jax.random.normal(ks[2], (QUERY_DIM, INNER), dtype=jnp.float32) * QUERY_DIM ** (-0.5)
        Wk = jax.random.normal(ks[3], (CONTEXT_DIM, INNER), dtype=jnp.float32) * CONTEXT_DIM ** (-0.5)
        Wv = jax.random.normal(ks[4], (CONTEXT_DIM, INNER), dtype=jnp.float32) * CONTEXT_DIM ** (-0.5)
        Wo = jax.random.normal(ks[5], (INNER, QUERY_DIM), dtype=jnp.float32) * INNER ** (-0.5)
        bo = jax.random.normal(ks[6], (QUERY_DIM,), dtype=jnp.float32) * 0.01
        return {'x': x, 'context': context, 'Wq': Wq, 'Wk': Wk, 'Wv': Wv, 'Wo': Wo, 'bo': bo}
    _L1_xattn_all = _L1_xattn_setup()
    _L1_xattn_in = {k: v for k, v in _L1_xattn_all.items() if k in ('Wq', 'Wk', 'Wv', 'Wo', 'bo')}
    del _L1_xattn_all

    def _L1_ffn_setup():
        import jax, jax.numpy as jnp
        import numpy as np
        A, M, H = (4, 256, 256)
        E, N = (8, 1024)
        key = jax.random.key(seed)
        kx, k1, k2 = jax.random.split(key, 3)
        x = jax.random.normal(kx, (A, M, H), dtype=jnp.float32)
        w1 = jax.random.normal(k1, (E, H, N), dtype=jnp.float32) * 0.02
        w2 = jax.random.normal(k2, (E, N, H), dtype=jnp.float32) * 0.02
        return {'x': x, 'w1': w1, 'w2': w2}
    _L1_ffn_all = _L1_ffn_setup()
    _L1_ffn_in = {k: v for k, v in _L1_ffn_all.items() if k in ('w1', 'w2')}
    del _L1_ffn_all
    return {'x': x, 'ctx_768': ctx_768, 'g_xattn': g_xattn, 'g_ffn': g_ffn, 'L0_xattn_Wq': _L0_xattn_in['Wq'], 'L0_xattn_bq': _L0_xattn_in['bq'], 'L0_xattn_Wk': _L0_xattn_in['Wk'], 'L0_xattn_bk': _L0_xattn_in['bk'], 'L0_xattn_Wv': _L0_xattn_in['Wv'], 'L0_xattn_bv': _L0_xattn_in['bv'], 'L0_xattn_W1': _L0_xattn_in['W1'], 'L0_xattn_b1': _L0_xattn_in['b1'], 'L0_xattn_W2': _L0_xattn_in['W2'], 'L0_xattn_b2': _L0_xattn_in['b2'], 'L0_ffn_Wq': _L0_ffn_in['Wq'], 'L0_ffn_bq': _L0_ffn_in['bq'], 'L0_ffn_bn_gamma': _L0_ffn_in['bn_gamma'], 'L0_ffn_bn_beta': _L0_ffn_in['bn_beta'], 'L0_ffn_sub_key0': _L0_ffn_in['sub_key0'], 'L0_ffn_sub_key1': _L0_ffn_in['sub_key1'], 'L0_ffn_expert_down': _L0_ffn_in['expert_down'], 'L0_ffn_expert_up': _L0_ffn_in['expert_up'], 'L1_xattn_Wq': _L1_xattn_in['Wq'], 'L1_xattn_Wk': _L1_xattn_in['Wk'], 'L1_xattn_Wv': _L1_xattn_in['Wv'], 'L1_xattn_Wo': _L1_xattn_in['Wo'], 'L1_xattn_bo': _L1_xattn_in['bo'], 'L1_ffn_w1': _L1_ffn_in['w1'], 'L1_ffn_w2': _L1_ffn_in['w2']}

def reference(x, ctx_768, g_xattn, g_ffn, L0_xattn_Wq, L0_xattn_bq, L0_xattn_Wk, L0_xattn_bk, L0_xattn_Wv, L0_xattn_bv, L0_xattn_W1, L0_xattn_b1, L0_xattn_W2, L0_xattn_b2, L0_ffn_Wq, L0_ffn_bq, L0_ffn_bn_gamma, L0_ffn_bn_beta, L0_ffn_sub_key0, L0_ffn_sub_key1, L0_ffn_expert_down, L0_ffn_expert_up, L1_xattn_Wq, L1_xattn_Wk, L1_xattn_Wv, L1_xattn_Wo, L1_xattn_bo, L1_ffn_w1, L1_ffn_w2):
    import jax
    import jax.numpy as jnp

    def _L0_xattn_ref(x, y, Wq, bq, Wk, bk, Wv, bv, W1, b1, W2, b2):
        import jax, jax.numpy as jnp
        import numpy as np
        IMAGE_DIM = 256
        TEXT_DIM = 192
        NUM_HEADS = 16
        HEAD_DIM = IMAGE_DIM // NUM_HEADS
        B, N, _ = x.shape
        M = y.shape[1]
        q = (x @ Wq + bq).reshape(B, N, NUM_HEADS, HEAD_DIM)
        k = (y @ Wk + bk).reshape(B, M, NUM_HEADS, HEAD_DIM)
        v = (y @ Wv + bv).reshape(B, M, NUM_HEADS, HEAD_DIM)
        scale = 1.0 / np.sqrt(HEAD_DIM)
        scores = jnp.einsum('bnhd,bmhd->bhnm', q, k) * scale
        attn = jax.nn.softmax(scores, axis=-1)
        out = jnp.einsum('bhnm,bmhd->bnhd', attn, v).reshape(B, N, IMAGE_DIM)
        h = jax.nn.relu(out @ W1 + b1)
        return h @ W2 + b2

    def _L0_ffn_ref(hidden_states, Wq, bq, bn_gamma, bn_beta, sub_key0, sub_key1, expert_down, expert_up):
        import jax, jax.numpy as jnp
        import numpy as np
        H = 8
        QD = 64
        HALF = QD // 2
        DIMS = (32, 32)
        TOPK = 16
        DTK = 4
        EPS_BN = 1e-05
        EPS_NORM = 1e-12

        def _l2norm(x):
            n = jnp.linalg.norm(x, axis=-1, keepdims=True)
            return x / jnp.maximum(n, EPS_NORM)
        B, S, D = hidden_states.shape
        q = (hidden_states @ Wq + bq).reshape(B, S, H, QD)
        mean = q.mean(axis=(0, 1, 2))
        var = q.var(axis=(0, 1, 2))
        q = (q - mean) / jnp.sqrt(var + EPS_BN) * bn_gamma + bn_beta
        q0 = _l2norm(q[..., :HALF])
        q1 = _l2norm(q[..., HALF:])
        k0 = _l2norm(sub_key0)
        k1 = _l2norm(sub_key1)
        s0 = jnp.einsum('bshq,kq->bshk', q0, k0)
        s1 = jnp.einsum('bshq,kq->bshk', q1, k1)
        ts0, ti0 = jax.lax.top_k(s0, DTK)
        ts1, ti1 = jax.lax.top_k(s1, DTK)
        comb_s = (ts0[..., :, None] + ts1[..., None, :]).reshape(B, S, H, DTK * DTK)
        comb_i = (ti0[..., :, None] * DIMS[1] + ti1[..., None, :]).reshape(B, S, H, DTK * DTK)
        top_s, pos = jax.lax.top_k(comb_s, TOPK)
        idx = jnp.take_along_axis(comb_i, pos, axis=-1)
        w = jax.nn.softmax(top_s, axis=-1)
        down = expert_down[idx]
        up = expert_up[idx]
        eh = jnp.einsum('bshkd,bsd->bshk', down, hidden_states)
        eh = jax.nn.gelu(eh, approximate=False)
        out = jnp.einsum('bshko,bshk->bso', up, eh * w)
        return out

    def _L1_xattn_ref(x, context, Wq, Wk, Wv, Wo, bo):
        import jax, jax.numpy as jnp
        import numpy as np
        HEADS = 8
        DIM_HEAD = 64
        QUERY_DIM = 256
        CONTEXT_DIM = 192
        INNER = HEADS * DIM_HEAD
        B, Sq, _ = x.shape
        h, d = (HEADS, DIM_HEAD)
        scale = d ** (-0.5)
        q = (x @ Wq).reshape(B, Sq, h, d).transpose(0, 2, 1, 3)
        k = (context @ Wk).reshape(B, -1, h, d).transpose(0, 2, 1, 3)
        v = (context @ Wv).reshape(B, -1, h, d).transpose(0, 2, 1, 3)
        scores = jnp.einsum('bhid,bhjd->bhij', q, k) * scale
        attn = jax.nn.softmax(scores, axis=-1)
        out = jnp.einsum('bhij,bhjd->bhid', attn, v)
        out = out.transpose(0, 2, 1, 3).reshape(B, Sq, h * d)
        return out @ Wo + bo

    def _L1_ffn_ref(x, w1, w2):
        import jax, jax.numpy as jnp
        import numpy as np
        A, M, H = (4, 256, 256)
        E, N = (8, 1024)
        mid = jnp.einsum('amh,ehn->aemn', x, w1)
        out = jnp.einsum('aemn,enh->amh', mid, w2)
        return out
    x = x + jnp.tanh(g_xattn[0]) * _L0_xattn_ref(_layernorm(x, axis=-1), ctx_768, L0_xattn_Wq, L0_xattn_bq, L0_xattn_Wk, L0_xattn_bk, L0_xattn_Wv, L0_xattn_bv, L0_xattn_W1, L0_xattn_b1, L0_xattn_W2, L0_xattn_b2)
    x = x + jnp.tanh(g_ffn[0]) * _L0_ffn_ref(_layernorm(x, axis=-1), L0_ffn_Wq, L0_ffn_bq, L0_ffn_bn_gamma, L0_ffn_bn_beta, L0_ffn_sub_key0, L0_ffn_sub_key1, L0_ffn_expert_down, L0_ffn_expert_up)
    x = x + jnp.tanh(g_xattn[1]) * _L1_xattn_ref(_layernorm(x, axis=-1), ctx_768, L1_xattn_Wq, L1_xattn_Wk, L1_xattn_Wv, L1_xattn_Wo, L1_xattn_bo)
    x = x + jnp.tanh(g_ffn[1]) * _L1_ffn_ref(_layernorm(x, axis=-1), L1_ffn_w1, L1_ffn_w2)
    return x

_drawn_inputs = setup_inputs


def setup_inputs(seed=0):
    import zlib

    import numpy as np

    out = dict(_drawn_inputs(seed))
    spreads = {'g_ffn': (-1.0, 0.548),
     'L0_ffn_bq': (0.0, 2.0),
     'L0_ffn_bn_gamma': (1.0, 0.6),
     'L0_ffn_bn_beta': (0.0, 2.0)}
    factors = {'L0_xattn_bq': 8.0,
     'L0_xattn_bk': 200.0,
     'L0_ffn_Wq': 21.963,
     'L0_ffn_sub_key0': 8.0,
     'L0_ffn_sub_key1': 154.931,
     'L0_ffn_expert_down': 3.659,
     'L0_ffn_expert_up': 3.607,
     'L1_xattn_bo': 7.118}
    for name, (base, spread) in spreads.items():
        noise = np.random.default_rng([zlib.crc32(name.encode()), seed]).standard_normal(out[name].shape)
        drawn = base * np.exp(spread * noise) if base else spread * noise
        out[name] = jnp.asarray(drawn.astype(out[name].dtype))
    for name, factor in factors.items():
        out[name] = (out[name] * factor).astype(out[name].dtype)
    return out
```

```python
from contextlib import ExitStack

import concourse.bass as bass
from concourse import mybir

F32 = mybir.dt.float32
BF16 = mybir.dt.bfloat16
ALU = mybir.AluOpType
ACT = mybir.ActivationFunctionType
AX = mybir.AxisListType

B, S, D = 16, 100, 256
M, DC = 361, 192
KC = 96
H0, D0 = 16, 16
H1, D1 = 8, 64
HID = 512
MSTART = [0, 128, M - 128]
OVERLAP = 2 * 128 - MSTART[2]
TOP, NKEY, NEXP = 4, 32, 256
WK = B * 4
EPS = 1e-5
TINY = 1e-24


def program(nc, x, ctxT, g_xattn, g_ffn, Wq0, bq0, Wk0, bk0, Wv0, bv0, W1, b1, W2, b2, Wqf, bqf, gamma, beta,
            key0, key1, downT, up, Wq1, Wk1, Wv1, Wo1, bo1, w1T, w2, out):
    with ExitStack() as stack:
        def sb(name, shape, dt=F32):
            return stack.enter_context(nc.sbuf_tensor(name, shape, dt))

        def sem(name):
            return stack.enter_context(nc.semaphore(name))

        psum = stack.enter_context(nc.psum_tensor("psum", [128, 8, 512], F32))

        def bank(n, *dims, parts=128, dt=F32):
            size = 1
            for d in dims:
                size *= d
            ap = psum[0:parts, n, 0:size] if dt == F32 else psum[0:parts, n, :].bitcast(dt)[:, 0:size]
            if len(dims) == 1:
                return ap
            names = " ".join("abc"[:len(dims)])
            return ap.rearrange(f"p ({names}) -> p {names}", **{n: d for n, d in zip("abc", dims)})

        ups = sb("ups", [128, 2, D])
        wq1 = sb("wq1", [128, 2, HID]); wk1 = sb("wk1", [KC, 2, HID]); wv1 = sb("wv1", [KC, 2, HID])
        wo1 = sb("wo1", [128, 4, D])
        bq0s = sb("bq0s", [128, 2]); bk0s = sb("bk0s", [128, 2]); bqfs = sb("bqfs", [128, 4])
        bv0b = sb("bv0b", [128, D]); bv0m = sb("bv0m", [128, D])
        b1b = sb("b1b", [S, HID]); b2b = sb("b2b", [S, D]); bo1b = sb("bo1b", [S, D])
        gb2 = sb("gb2", [S, D]); gbo = sb("gbo", [S, D])
        gate = sb("gate", [128, 4]); tgate = sb("tgate", [128, 4])
        gam = sb("gam", [128, 1]); bet = sb("bet", [128, 1])
        ident = sb("ident", [128, 128]); identb = sb("identb", [128, 128], BF16)
        negones = sb("negones", [96, 128], BF16)
        partmask = sb("partmask", [96, 8])
        headmask0 = sb("headmask0", [128, 8])
        headmask1 = sb("headmask1", [128, 2])
        ones4 = sb("ones4", [128, 4])
        lastmask = sb("lastmask", [128, 1])
        samedim = sb("samedim", [128, 128])
        half = sb("half", [128, 1])
        eps = sb("eps", [S, 1]); scratch = sb("scratch", [1, 1])
        xs = sb("xs", [S, B, D])
        hidden = sb("hidden", [S, B, NEXP])
        qall = sb("qall", [128, 4, B * S])
        qstat = sb("qstat", [128, 4, B, 6])
        prod = sb("prod", [128, 2, D])
        ctx = sb("ctx", [KC, 2, M])
        stat = sb("stat", [S, 2, 6]); mv = sb("mv", [S, 2, 2]); rstd = sb("rstd", [S, 2, 1]); vare = sb("vare", [S, 2, 1])
        xl = sb("xl", [S, 2, D]); xT = sb("xT", [128, 2, S]); xT2 = sb("xT2", [128, 2, S])
        qT = sb("qT", [128, 2, S]); qz = sb("qz", [128, 2, 8, S])
        mx = sb("mx", [S, H0]); parts = sb("parts", [S, 2, 96], BF16); mxb = sb("mxb", [96, 2, 8, S], BF16)
        prob = sb("prob", [128, 4, 3, 4, S])
        oTp = sb("oTp", [128, 4, S]); rden = sb("rden", [S, H0]); o = sb("o", [S, HID]); oT = sb("oT", [128, 4, S])
        early = stack.enter_context(ExitStack())

        def sb1(name, shape, dt=F32):
            return early.enter_context(nc.sbuf_tensor(name, shape, dt))

        wq0 = sb1("wq0", [128, 2, D]); wk0 = sb1("wk0", [KC, 2, D]); wv0 = sb1("wv0", [KC, 2, D])
        w1s = sb1("w1s", [128, 2, HID]); w2s = sb1("w2s", [128, 4, D]); wqf = sb1("wqf", [128, 2, HID])
        downs = sb1("downs", [128, 2, NEXP])
        e1 = sb1("e1", [128, 4, D]); e2 = sb1("e2", [128, 4, D])
        kT0 = sb1("kT0", [128, 2, M]); v0 = sb1("v0", [128, 3, H0, 32])
        h = sb1("h", [S, HID]); hT = sb1("hT", [128, 4, S])
        loaded = sem("loaded"); x_loaded = sem("x_loaded"); ctx_loaded = sem("ctx_loaded"); e_loaded = sem("e_loaded")
        late_loaded = sem("late_loaded")
        zeroed = sem("zeroed"); selected = sem("selected"); gates_ready = sem("gates_ready"); consts_ready = sem("consts_ready")
        ring_full = [sem(f"ring_full{i}") for i in range(4)]
        ring_free = [sem(f"ring_free{i}") for i in range(4)]
        st_full = [sem(f"st_full{i}") for i in range(2)]
        st_free = [sem(f"st_free{i}") for i in range(2)]
        o_full = sem("o_full"); o_free = sem("o_free")
        tail_full = sem("tail_full"); tail_free = sem("tail_free")
        ln1_stat = sem("ln1_stat"); ln1_var = sem("ln1_var"); ln1_eps = sem("ln1_eps"); ln1_rstd = sem("ln1_rstd"); xl1_ready = sem("xl1_ready")
        ln2_stat = sem("ln2_stat"); ln2_var = sem("ln2_var"); ln2_eps = sem("ln2_eps"); ln2_rstd = sem("ln2_rstd"); xl2_ready = sem("xl2_ready")
        qz_ready = sem("qz_ready"); biased = sem("biased"); parts_hi = sem("parts_hi"); parts_ready = sem("parts_ready")
        rden_ready = sem("rden_ready"); qstat_done = sem("qstat_done"); mul_done = sem("mul_done")

        def need(eng, s, value):
            if not isinstance(value, int) or value > 0:
                eng.wait_ge(s, value)

        RING = {n: i for i, n in enumerate(["xT", "q", "k0", "k1", "v0", "v1", "v2", "prod"] + [f"s{i}" for i in range(H0)])}
        ST = {n: i for i, n in enumerate([n for c in range(2) for n in [f"m{c}"] + [f"t{6 * c + i}" for i in range(6)]])}
        TAIL = {n: i for i, n in enumerate(["nat", "oT", "h", "hT", "y", "x2T", "qf", "down"])}

        def ring(name, b):
            i = RING[name]
            return i % 4, b * (len(RING) // 4) + i // 4

        def stb(name, b):
            i = ST[name]
            return i % 2, b * (len(ST) // 2) + i // 2

        def tail(name, b):
            return b * len(TAIL) + TAIL[name]

        chunk = [slice(m, m + 128) for m in MSTART]

        with nc.Block() as block:
            @block.sync
            def _(sp):
                sp.dma_start(xs[:], x.rearrange("b s d -> s b d")).then_inc(x_loaded, 16)

                def load_ctx(b):
                    sp.dma_start(ctx[:], ctxT[b].rearrange("(k p) m -> p k m", p=KC)).then_inc(ctx_loaded, 16)

                def load_experts(b):
                    sp.dma_start(e1[:], w1T[b]).then_inc(e_loaded, 16)
                    sp.dma_start(e2[:], w2[b]).then_inc(e_loaded, 16)

                sp.dma_start(wq0[:], Wq0.rearrange("(k p) n -> p k n", p=128)).then_inc(loaded, 16)
                sp.dma_start(wk0[:], Wk0.rearrange("(k p) n -> p k n", p=KC)).then_inc(loaded, 16)
                load_ctx(0)
                sp.dma_start(wv0[:], Wv0.rearrange("(k p) n -> p k n", p=KC)).then_inc(loaded, 16)
                sp.dma_start(bq0s[:], bq0).then_inc(loaded, 16)
                sp.dma_start(bk0s[:], bk0).then_inc(loaded, 16)
                sp.dma_start(bqfs[:], bqf).then_inc(loaded, 16)
                sp.dma_start(bv0b[:], bv0.partition_broadcast(128)).then_inc(loaded, 16)
                sp.dma_start(b1b[:], b1.partition_broadcast(S)).then_inc(loaded, 16)
                sp.dma_start(b2b[:], b2.partition_broadcast(S)).then_inc(loaded, 16)
                sp.dma_start(gate[:, 0:2], g_xattn.partition_broadcast(128)).then_inc(loaded, 16)
                sp.dma_start(gate[:, 2:4], g_ffn.partition_broadcast(128)).then_inc(loaded, 16)
                load_experts(0)
                sp.dma_start(w1s[:], W1.rearrange("(k p) n -> p k n", p=128)).then_inc(loaded, 16)
                sp.dma_start(w2s[:], W2.rearrange("(k p) n -> p k n", p=128)).then_inc(loaded, 16)
                sp.dma_start(wqf[:], Wqf.rearrange("(k p) n -> p k n", p=128)).then_inc(loaded, 16)
                sp.dma_start(downs[:], downT.rearrange("(k p) n -> p k n", p=128)).then_inc(loaded, 16)
                sp.dma_start(bo1b[:], bo1.partition_broadcast(S)).then_inc(loaded, 16)
                for w, src in ((ups, up), (wq1, Wq1), (wo1, Wo1)):
                    sp.dma_start(w[:], src.rearrange("(k p) n -> p k n", p=128)).then_inc(late_loaded, 16)
                for w, src in ((wk1, Wk1), (wv1, Wv1)):
                    sp.dma_start(w[:], src.rearrange("(k p) n -> p k n", p=KC)).then_inc(late_loaded, 16)
                for i in range(2):
                    sp.dma_start(gam[64 * i:64 * i + 64, :], gamma.rearrange("(p a) -> p a", a=1)).then_inc(late_loaded, 16)
                    sp.dma_start(bet[64 * i:64 * i + 64, :], beta.rearrange("(p a) -> p a", a=1)).then_inc(late_loaded, 16)
                with sp.Fori(1, B) as b:
                    bk, n = ring("v2", b - 1)
                    sp.wait_ge(ring_full[bk], n + 1)
                    load_ctx(b)
                    bk, n = ring("prod", b - 1)
                    sp.wait_ge(ring_full[bk], n + 1)
                    load_experts(b)
                sp.wait_ge(late_loaded, 9 * 16)
            NLOADED = 16 * 16

            @block.gpsimd
            def _(pool):
                for t in (ident, identb, samedim, parts, partmask):
                    nc.gpsimd.memset(t[:], 0.0).then_inc(zeroed, 1)
                for t in (headmask0, headmask1, ones4, lastmask, v0):
                    nc.gpsimd.memset(t[:], 1.0).then_inc(zeroed, 1)
                nc.gpsimd.memset(negones[:], -1.0).then_inc(consts_ready, 1)
                nc.gpsimd.memset(half[:], -0.5).then_inc(consts_ready, 1)
                nc.gpsimd.memset(eps[:], EPS).then_inc(consts_ready, 1)
                pool.wait_ge(zeroed, 10)

                done = [0]

                def select(ap, pattern, base, op, fill, cm=1):
                    done[0] += 1
                    nc.gpsimd.affine_select(out=ap, in_=ap, compare_op=op, fill=fill, base=base, pattern=pattern,
                                            channel_multiplier=cm).then_inc(selected, 1)
                    pool.wait_ge(selected, done[0])

                for t in (ident, identb):
                    select(t[:], [[-1, 128]], 0, ALU.not_equal, 1.0)
                for off in (0, 64, -64):
                    select(samedim[:], [[-1, 128]], off, ALU.not_equal, 1.0 / 8)
                for off in (0, -32):
                    select(partmask[:], [[-1, 8]], off, ALU.not_equal, 1.0)
                for t, n in ((headmask0, 8), (headmask1, 2), (ones4, 4)):
                    select(t[:], [[-128 // n, n]], 0, ALU.is_ge, 0.0)
                    select(t[:], [[128 // n, n]], 128 // n - 1, ALU.is_ge, 0.0, cm=-1)
                select(lastmask[:], [[0, 1]], -OVERLAP, ALU.is_ge, 0.0)
                select(v0[:, 2, :, :].rearrange("p h d -> p (h d)"), [[0, H0 * 32]], -OVERLAP, ALU.is_ge, 0.0)
                pool.wait_ge(loaded, NLOADED)
                pool.wait_ge(gates_ready, 1)
                nc.gpsimd.tensor_scalar(gb2[:], b2b[:], tgate[0:S, 0:1], None, ALU.mult).then_inc(consts_ready, 1)
                nc.gpsimd.tensor_scalar(gbo[:], bo1b[:], tgate[0:S, 1:2], None, ALU.mult).then_inc(consts_ready, 1)
                nc.gpsimd.tensor_scalar(bv0m[:], bv0b[:], lastmask[:], None, ALU.mult).then_inc(consts_ready, 1)
                pool.wait_ge(consts_ready, 6)

                def step(b, attn, after):
                    if attn:
                        pool.wait_ge(ln1_var, b + 1)
                        nc.gpsimd.tensor_tensor(vare[:, 0, :], mv[:, 0, 1:2], eps[:], ALU.add).then_inc(ln1_eps, 1)
                        pool.wait_ge(ln1_eps, b + 1)
                        nc.gpsimd.tensor_tensor(rstd[:, 0, :], vare[:, 0, :], half[0:S, :], ALU.pow).then_inc(ln1_rstd, 1)
                        pool.wait_ge(xl1_ready, b + 1)
                        nc.gpsimd.tensor_tensor(xs[:, b, :], xs[:, b, :], gb2[:], ALU.add).then_inc(biased, 1)
                        bk, n = ring("q", b)
                        pool.wait_ge(ring_free[bk], n + 1)
                        nc.gpsimd.tensor_tensor(
                            qz[:], qT[:].unsqueeze(2).broadcast_to([128, 2, 8, S]),
                            headmask0[:].unsqueeze(1).unsqueeze(3).broadcast_to([128, 2, 8, S]), ALU.mult).then_inc(qz_ready, 1)
                    if after:
                        t = b - 1
                        pool.wait_ge(ln2_var, t + 1)
                        nc.gpsimd.tensor_tensor(vare[:, 1, :], mv[:, 1, 1:2], eps[:], ALU.add).then_inc(ln2_eps, 1)
                        pool.wait_ge(ln2_eps, t + 1)
                        nc.gpsimd.tensor_tensor(rstd[:, 1, :], vare[:, 1, :], half[0:S, :], ALU.pow).then_inc(ln2_rstd, 1)

                step(0, True, False)
                with pool.Fori(1, B) as b:
                    step(b, True, True)
                step(B, False, True)

            @block.scalar
            def _(act):
                act.wait_ge(loaded, NLOADED)
                nc.scalar.activation(tgate[:], gate[:], ACT.Tanh).then_inc(gates_ready, 1)

                def drain(name, b, dst, src, func=ACT.Copy, **kw):
                    bk, n = ring(name, b)
                    act.wait_ge(ring_full[bk], n + 1)
                    nc.scalar.activation(dst, src(bk), func, **kw).then_inc(ring_free[bk], 1)

                def drain_tail(name, b, dst, src, func=ACT.Copy):
                    act.wait_ge(tail_full, tail(name, b) + 1)
                    nc.scalar.activation(dst, src, func).then_inc(tail_free, 1)

                def step(b, attn, after):
                    t = b - 1
                    if attn:
                        drain("xT", b, xT[:], lambda k: bank(k, 2, S))
                        drain("k0", b, kT0[:, 0, :], lambda k: bank(k, M), ACT.Identity, bias=bk0s[:, 0:1])
                    if after:
                        drain_tail("oT", t, oT[:, 0:2, :], bank(7, 2, S))
                    if attn:
                        drain("k1", b, kT0[:, 1, :], lambda k: bank(k, M), ACT.Identity, bias=bk0s[:, 1:2])
                    if after:
                        drain_tail("hT", t, hT[:], bank(7, 4, S), ACT.Relu)
                        drain_tail("x2T", t, xT2[:], bank(7, 2, S))
                        drain_tail("down", t, hidden[:, t, :], bank(7, NEXP, parts=S))
                    if attn:
                        for g in range(4):
                            for mc in range(3):
                                sb_, n = stb(f"t{3 * g + mc}", b)
                                act.wait_ge(st_full[sb_], n + 1)
                                nc.scalar.activation(prob[:, g, mc, :, :], bank(4 + sb_, 4, S), ACT.Exp,
                                                     scale=D0 ** -0.5).then_inc(st_free[sb_], 1)
                        act.wait_ge(o_full, b + 1)
                        nc.scalar.activation(oTp[:], bank(6, 4, S), ACT.Copy).then_inc(o_free, 1)

                step(0, True, False)
                with act.Fori(1, B) as b:
                    step(b, True, True)
                step(B, False, True)

            @block.vector
            def _(dve):
                def carry():
                    nc.vector.memset(scratch[:], 0.0)

                dve.wait_ge(x_loaded, 16)
                dve.wait_ge(loaded, NLOADED)
                dve.wait_ge(consts_ready, 6)
                dve.wait_ge(selected, 15)

                def norm(b, k, stat_sem, var_sem, rstd_sem, ready):
                    carry()
                    nc.vector.bn_stats(stat[:, k, :], xs[:, b, :]).then_inc(stat_sem, 1)
                    dve.wait_ge(stat_sem, b + 1)
                    carry()
                    nc.vector.bn_aggr(mv[:, k, :], stat[:, k, :]).then_inc(var_sem, 1)

                def norm_apply(b, k, rstd_sem, ready):
                    dve.wait_ge(rstd_sem, b + 1)
                    nc.vector.tensor_scalar(xl[:, k, :], xs[:, b, :], mv[:, k, 0:1], rstd[:, k, :], ALU.subtract,
                                            ALU.mult).then_inc(ready, 1)

                def step(b, attn, after):
                    t = b - 1
                    if attn:
                        norm(b, 0, ln1_stat, ln1_var, ln1_rstd, xl1_ready)
                        norm_apply(b, 0, ln1_rstd, xl1_ready)
                        bk, n = ring("q", b)
                        dve.wait_ge(ring_full[bk], n + 1)
                        nc.vector.tensor_tensor(qT[:], bank(bk, 2, S), bq0s[:].unsqueeze(2).broadcast_to([128, 2, S]),
                                                ALU.add).then_inc(ring_free[bk], 1)
                    if after:
                        dve.wait_ge(tail_full, tail("nat", t) + 1)
                        nat = bank(7, H0, 32, parts=S)
                        nc.vector.reciprocal(rden[:], nat[:, :, D0]).then_inc(rden_ready, 1)
                        dve.wait_ge(rden_ready, t + 1)
                        nc.vector.tensor_tensor(o[:, 0:D].rearrange("p (h d) -> p h d", h=H0), nat[:, :, 0:D0],
                                                rden[:].unsqueeze(2).broadcast_to([S, H0, D0]), ALU.mult).then_inc(tail_free, 1)
                        dve.wait_ge(tail_full, tail("h", t) + 1)
                        nc.vector.tensor_tensor(h[:], bank(7, HID, parts=S), b1b[:], ALU.add).then_inc(tail_free, 1)
                    if attn:
                        for mc in range(3):
                            bk, n = ring(f"v{mc}", b)
                            dve.wait_ge(ring_full[bk], n + 1)
                            src = bank(bk, H0, D0)
                            if mc < 2:
                                nc.vector.tensor_tensor(v0[:, mc, :, 0:D0], src, bv0b[:].rearrange("p (h d) -> p h d", h=H0),
                                                        ALU.add).then_inc(ring_free[bk], 1)
                            else:
                                nc.vector.scalar_tensor_tensor(v0[:, mc, :, 0:D0], src, lastmask[:],
                                                               bv0m[:].rearrange("p (h d) -> p h d", h=H0), ALU.mult,
                                                               ALU.add).then_inc(ring_free[bk], 1)
                            if mc == 1 and after:
                                dve.wait_ge(tail_full, tail("y", t) + 1)
                                dve.wait_ge(biased, t + 1)
                                nc.vector.scalar_tensor_tensor(xs[:, t, :], bank(7, D, parts=S), tgate[0:S, 0:1], xs[:, t, :],
                                                               ALU.mult, ALU.add).then_inc(tail_free, 1)
                                dve.wait_ge(tail_free, tail("y", t) + 1)
                                norm(t, 1, ln2_stat, ln2_var, ln2_rstd, xl2_ready)
                        bk, n = ring("prod", b)
                        dve.wait_ge(ring_full[bk], n + 1)
                        if isinstance(b, int) and b == 0:
                            nc.vector.tensor_copy(prod[:], bank(bk, 2, D)).then_inc(ring_free[bk], 1)
                        else:
                            nc.vector.tensor_tensor(prod[:], bank(bk, 2, D), prod[:], ALU.add).then_inc(ring_free[bk], 1)
                    elif after:
                        dve.wait_ge(tail_full, tail("y", t) + 1)
                        dve.wait_ge(biased, t + 1)
                        nc.vector.scalar_tensor_tensor(xs[:, t, :], bank(7, D, parts=S), tgate[0:S, 0:1], xs[:, t, :],
                                                       ALU.mult, ALU.add).then_inc(tail_free, 1)
                        dve.wait_ge(tail_free, tail("y", t) + 1)
                        norm(t, 1, ln2_stat, ln2_var, ln2_rstd, xl2_ready)
                    if after:
                        norm_apply(t, 1, ln2_rstd, xl2_ready)

                    def maxima(i):
                        bk, n = ring(f"s{i}", b)
                        dve.wait_ge(ring_full[bk], n + 1)
                        nc.vector.reduce_max(mx[:, i:i + 1], bank(bk, M, parts=S), AX.X).then_inc(ring_free[bk], 1)

                    def split(c):
                        for i in range(4):
                            bk, n = ring(f"s{8 * c + 4 + i}", b)
                            dve.wait_ge(ring_free[bk], n + 1)
                        nc.vector.tensor_copy(parts[:, c, 0:8], mx[:, 8 * c:8 * c + 8]).then_inc(parts_hi, 1)
                        dve.wait_ge(parts_hi, 2 * b + c + 1)
                        nc.vector.tensor_tensor(parts[:, c, 32:40], mx[:, 8 * c:8 * c + 8], parts[:, c, 0:8],
                                                ALU.subtract).then_inc(parts_ready, 1)

                    def spread(c):
                        k, n = stb(f"m{c}", b)
                        dve.wait_ge(st_full[k], n + 1)
                        nc.vector.tensor_tensor(mxb[:, c, :, :],
                                                bank(4 + k, S, parts=96, dt=BF16).unsqueeze(1).broadcast_to([96, 8, S]),
                                                partmask[:].unsqueeze(2).broadcast_to([96, 8, S]), ALU.mult).then_inc(st_free[k], 1)

                    if attn:
                        for i in range(6):
                            maxima(i)
                    if after:
                        dve.wait_ge(tail_full, tail("qf", t) + 1)
                        nc.vector.tensor_tensor(qall[:, :, bass.ts(t, S)], bank(7, 4, S), bqfs[:].unsqueeze(2).broadcast_to([128, 4, S]),
                                                ALU.add).then_inc(tail_free, 1)
                    if attn:
                        maxima(6)
                        maxima(7)
                        split(0)
                    if after:
                        dve.wait_ge(tail_free, tail("qf", t) + 1)
                        carry()
                        for c in range(4):
                            nc.vector.bn_stats(qstat[:, c, t, :], qall[:, c, bass.ts(t, S)]).then_inc(qstat_done, 1)
                    if attn:
                        for i in range(8, 12):
                            maxima(i)
                        spread(0)
                        for i in range(12, 16):
                            maxima(i)
                        split(1)
                        spread(1)

                step(0, True, False)
                with dve.Fori(1, B) as b:
                    step(b, True, True)
                step(B, False, True)

            @block.tensor
            def _(pe):
                pe.wait_ge(loaded, NLOADED)
                pe.wait_ge(consts_ready, 6)
                pe.wait_ge(selected, 15)

                def step(b, attn, after):
                    t = b - 1

                    def open_ring(name):
                        bk, n = ring(name, b)
                        need(pe, ring_free[bk], n)
                        return bk

                    def open_tail(name):
                        need(pe, tail_free, tail(name, t))
                        return 7

                    def scores(i):
                        bk = open_ring(f"s{i}")
                        c, hd = divmod(i, 8)
                        nc.tensor.matmul(bank(bk, M, parts=S), qz[:, c, hd, :], kT0[:, c, :], start=True,
                                         stop=True).then_inc(ring_full[bk], 1)

                    def put_parts(c):
                        k, n = stb(f"m{c}", b)
                        need(pe, st_free[k], n)
                        pe.wait_ge(parts_ready, 2 * b + c + 1)
                        nc.tensor.transpose(bank(4 + k, S, parts=96, dt=BF16), parts[:, c, :], identb[0:S, 0:S]).then_inc(st_full[k], 1)

                    def tscores(g):
                        c = g // 2
                        hs = slice(4 * (g % 2), 4 * (g % 2) + 4)
                        k, n = stb(f"m{c}", b)
                        pe.wait_ge(st_free[k], n + 1)
                        for mc in range(3):
                            k, n = stb(f"t{3 * g + mc}", b)
                            need(pe, st_free[k], n)
                            dst = bank(4 + k, 4 * S)
                            nc.tensor.matmul(dst, kT0[:, c, chunk[mc]], qz[:, c, hs, :].rearrange("p h s -> p (h s)"),
                                             start=True, stop=False)
                            nc.tensor.matmul(dst, negones[:], mxb[:, c, hs, :].rearrange("p h s -> p (h s)"), start=False,
                                             stop=True).then_inc(st_full[k], 1)

                    def values(g):
                        if g == 0:
                            need(pe, o_free, b)
                        for mc in range(3):
                            k, n = stb(f"t{3 * g + mc}", b)
                            pe.wait_ge(st_free[k], n + 1)
                            for j in range(4):
                                last = nc.tensor.matmul(psum[32 * j:32 * j + 32, 6, g * S:(g + 1) * S], v0[:, mc, 4 * g + j, :],
                                                        prob[:, g, mc, j, :], start=mc == 0, stop=mc == 2)
                        if g == 3:
                            last.then_inc(o_full, 1)

                    def project(name, dst, pairs):
                        bk = open_ring(name)
                        for j in range(len(pairs)):
                            lhs, rhs = pairs[j]
                            last = nc.tensor.matmul(dst(bk), lhs, rhs, start=j == 0, stop=j == len(pairs) - 1)
                        last.then_inc(ring_full[bk], 1)

                    if attn:
                        pe.wait_ge(xl1_ready, b + 1)
                        bk = open_ring("xT")
                        for k in range(2):
                            last = nc.tensor.transpose(bank(bk, 2, S)[:, k, :], xl[:, 0, 128 * k:128 * k + 128], ident[0:S, 0:S])
                        last.then_inc(ring_full[bk], 1)
                        xbk, n = ring("xT", b)
                        bk = open_ring("q")
                        pe.wait_ge(ring_free[xbk], n + 1)
                        for mo in range(2):
                            for k in range(2):
                                last = nc.tensor.matmul(bank(bk, 2, S)[:, mo, :], wq0[:, k, 128 * mo:128 * mo + 128], xT[:, k, :],
                                                        start=k == 0, stop=k == 1)
                        last.then_inc(ring_full[bk], 1)
                    if after:
                        pe.wait_ge(o_free, t + 1)
                        open_tail("nat")
                        for g in range(4):
                            last = nc.tensor.transpose(bank(7, 4, 128, parts=S)[:, g, :], oTp[:, g, :], ident[:])
                        last.then_inc(tail_full, 1)
                    if attn:
                        pe.wait_ge(ctx_loaded, 16 * b + 16)
                        project("k0", lambda k: bank(k, M), [(wk0[:, k, 0:128], ctx[:, k, :]) for k in range(2)])
                    if after:
                        open_tail("oT")
                        for k in range(2):
                            last = nc.tensor.transpose(bank(7, 2, S)[:, k, :], o[:, 128 * k:128 * k + 128], ident[0:S, 0:S])
                        last.then_inc(tail_full, 1)
                    if attn:
                        project("k1", lambda k: bank(k, M), [(wk0[:, k, 128:256], ctx[:, k, :]) for k in range(2)])
                    if after:
                        open_tail("h")
                        for k in range(2):
                            last = nc.tensor.matmul(bank(7, HID, parts=S), oT[:, k, :], w1s[:, k, :], start=k == 0, stop=k == 1)
                        last.then_inc(tail_full, 1)
                    if attn:
                        project("v0", lambda k: bank(k, D), [(ctx[:, k, chunk[0]], wv0[:, k, :]) for k in range(2)])
                    if after:
                        open_tail("hT")
                        for k in range(4):
                            last = nc.tensor.transpose(bank(7, 4, S)[:, k, :], h[:, 128 * k:128 * k + 128], ident[0:S, 0:S])
                        last.then_inc(tail_full, 1)
                    if attn:
                        project("v1", lambda k: bank(k, D), [(ctx[:, k, chunk[1]], wv0[:, k, :]) for k in range(2)])
                    if after:
                        open_tail("y")
                        for k in range(4):
                            last = nc.tensor.matmul(bank(7, D, parts=S), hT[:, k, :], w2s[:, k, :], start=k == 0, stop=k == 3)
                        last.then_inc(tail_full, 1)
                    if attn:
                        project("v2", lambda k: bank(k, D), [(ctx[:, k, chunk[2]], wv0[:, k, :]) for k in range(2)])
                        pe.wait_ge(e_loaded, 32 * b + 32)
                        bk = open_ring("prod")
                        for mo in range(2):
                            for k in range(4):
                                last = nc.tensor.matmul(bank(bk, 2, D)[:, mo, :], e1[:, k, 128 * mo:128 * mo + 128], e2[:, k, :],
                                                        start=k == 0, stop=k == 3)
                        last.then_inc(ring_full[bk], 1)
                        pe.wait_ge(qz_ready, b + 1)
                        for c in range(2):
                            bk, n = ring(f"k{c}", b)
                            pe.wait_ge(ring_free[bk], n + 1)
                        for i in range(4):
                            scores(i)
                    if after:
                        pe.wait_ge(xl2_ready, t + 1)
                        open_tail("x2T")
                        for k in range(2):
                            last = nc.tensor.transpose(bank(7, 2, S)[:, k, :], xl[:, 1, 128 * k:128 * k + 128], ident[0:S, 0:S])
                        last.then_inc(tail_full, 1)
                    if attn:
                        scores(4)
                        scores(5)
                    if after:
                        open_tail("qf")
                        for mo in range(4):
                            for k in range(2):
                                last = nc.tensor.matmul(bank(7, 4, S)[:, mo, :], wqf[:, k, 128 * mo:128 * mo + 128], xT2[:, k, :],
                                                        start=k == 0, stop=k == 1)
                        last.then_inc(tail_full, 1)
                    if attn:
                        for i in range(6, 9):
                            scores(i)
                    if after:
                        open_tail("down")
                        for k in range(2):
                            last = nc.tensor.matmul(bank(7, NEXP, parts=S), xT2[:, k, :], downs[:, k, :], start=k == 0, stop=k == 1)
                        last.then_inc(tail_full, 1)
                    if attn:
                        for i in range(9, 12):
                            scores(i)
                        put_parts(0)
                        for i in range(12, 16):
                            scores(i)
                        for mc in range(3):
                            bk, n = ring(f"v{mc}", b)
                            pe.wait_ge(ring_free[bk], n + 1)
                        tscores(0)
                        tscores(1)
                        put_parts(1)
                        values(0)
                        tscores(2)
                        values(1)
                        tscores(3)
                        values(2)
                        values(3)

                step(0, True, False)
                with pe.Fori(1, B) as b:
                    step(b, True, True)
                step(B, False, True)

        early.close()
        agg = sb("agg", [128, 4, 2]); mean = sb("mean", [128, 1]); dev = sb("dev", [128, 4]); spreads = sb("spreads", [128, 4])
        varq = sb("varq", [128, 1]); rstdq = sb("rstdq", [128, 1]); qscale = sb("qscale", [128, 1]); qshift = sb("qshift", [128, 1])
        keys = sb("keys", [128, NKEY]); keysq = sb("keysq", [128, NKEY]); keyn = sb("keyn", [128, 1]); keyr = sb("keyr", [128, 1])
        keyd = sb("keyd", [128, 128]); keyT = sb("keyT", [128, 128])
        keys_loaded = sem("keys_loaded"); agg_ready = sem("agg_ready"); mean_summed = sem("mean_summed"); bn_step = sem("bn_step")
        spread_summed = sem("spread_summed"); varq_ready = sem("varq_ready"); rstdq_ready = sem("rstdq_ready")
        rstdq_eps = sem("rstdq_eps"); keyn_ready = sem("keyn_ready"); keyr_ready = sem("keyr_ready"); keyd_ready = sem("keyd_ready")
        keyT_full = sem("keyT_full"); gelu_done = sem("gelu_done")

        with nc.Block() as block:
            @block.sync
            def _(sp):
                for i in range(4):
                    sp.dma_start(keys[32 * i:32 * i + 32, :], (key0, key1)[i % 2]).then_inc(keys_loaded, 16)

            @block.scalar
            def _(act):
                nc.scalar.activation(hidden[:], hidden[:], ACT.Gelu).then_inc(gelu_done, 1)
                act.wait_ge(gelu_done, 1)

            @block.tensor
            def _(pe):
                pe.wait_ge(agg_ready, 4)
                nc.tensor.matmul(bank(0, 4), samedim[:], agg[:, :, 0], start=True, stop=True).then_inc(mean_summed, 1)
                pe.wait_ge(bn_step, 4)
                nc.tensor.matmul(bank(1, 4), samedim[:], spreads[:], start=True, stop=True).then_inc(spread_summed, 1)
                pe.wait_ge(keyd_ready, 4)
                nc.tensor.transpose(bank(2, 128), keyd[:], ident[:]).then_inc(keyT_full, 1)

            @block.gpsimd
            def _(pool):
                pool.wait_ge(keyn_ready, 1)
                nc.gpsimd.tensor_tensor(keyr[:], keyn[:], half[:], ALU.pow).then_inc(keyr_ready, 1)
                pool.wait_ge(varq_ready, 1)
                nc.gpsimd.tensor_scalar(varq[:], varq[:], EPS, None, ALU.add).then_inc(rstdq_eps, 1)
                pool.wait_ge(rstdq_eps, 1)
                nc.gpsimd.tensor_tensor(rstdq[:], varq[:], half[:], ALU.pow).then_inc(rstdq_ready, 1)

            @block.vector
            def _(dve):
                done = [0]

                def then(instruction):
                    done[0] += 1
                    instruction.then_inc(bn_step, 1)
                    dve.wait_ge(bn_step, done[0])

                for c in range(4):
                    nc.vector.bn_aggr(agg[:, c, :], qstat[:, c, :, :].rearrange("p b s -> p (b s)")).then_inc(agg_ready, 1)
                dve.wait_ge(agg_ready, 4)
                dve.wait_ge(mean_summed, 1)
                then(nc.vector.reduce_sum(mean[:], bank(0, 4), AX.X))
                then(nc.vector.tensor_scalar(dev[:], agg[:, :, 0], mean[:], None, ALU.subtract))
                then(nc.vector.tensor_tensor(dev[:], dev[:], dev[:], ALU.mult))
                then(nc.vector.tensor_tensor(spreads[:], dev[:], agg[:, :, 1], ALU.add))
                dve.wait_ge(keys_loaded, 64)
                then(nc.vector.tensor_tensor(keysq[:], keys[:], keys[:], ALU.mult))
                then(nc.vector.reduce_sum(keyn[:], keysq[:], AX.X))
                nc.vector.tensor_scalar(keyn[:], keyn[:], TINY, None, ALU.max).then_inc(keyn_ready, 1)
                then(nc.vector.memset(keyd[:], 0.0))
                dve.wait_ge(spread_summed, 1)
                nc.vector.reduce_sum(varq[:], bank(1, 4), AX.X).then_inc(varq_ready, 1)
                dve.wait_ge(keyr_ready, 1)
                for i in range(4):
                    q = slice(32 * i, 32 * i + 32)
                    nc.vector.tensor_scalar(keyd[q, q], keys[q, :], keyr[q, :], None, ALU.mult).then_inc(keyd_ready, 1)
                dve.wait_ge(rstdq_ready, 1)
                then(nc.vector.tensor_tensor(qscale[:], rstdq[:], gam[:], ALU.mult))
                then(nc.vector.tensor_tensor(mean[:], mean[:], qscale[:], ALU.mult))
                then(nc.vector.tensor_tensor(qshift[:], bet[:], mean[:], ALU.subtract))
                dve.wait_ge(keyT_full, 1)
                then(nc.vector.tensor_copy(keyT[:], bank(2, 128)))

        kT1 = sb("kT1", [128, 4, M]); v1 = sb("v1", [128, 3, H1, D1 + 1]); qz1 = sb("qz1", [128, 4, 2, S])
        rden1 = sb("rden1", [S, H1])
        qn = sb("qn", [128, 4, S]); qsq = sb("qsq", [128, 4, S]); n2s = sb("n2s", [S, 16]); rn = sb("rn", [S, 16])
        FILL, TAKEN = -10.0, 10.0
        score = sb("score", [S, 16, NKEY + TOP]); top8 = sb("top8", [S, 16, 8]); marked = sb("marked", [S, 16, NKEY + TOP])
        expo = sb("expo", [S, 16, NKEY]); kept = sb("kept", [S, 16, NKEY]); den = sb("den", [S, 16]); rdn = sb("rdn", [S, 16])
        prb = sb("prb", [S, 8, 2, NKEY]); outer = sb("outer", [S, 8, NEXP]); wt = sb("wt", [S, NEXP]); beyond = sb("beyond", [S, 1])
        gw = sb("gw", [S, NEXP]); gT = sb("gT", [128, 2, S])
        ctx3_loaded = sem("ctx3_loaded"); masks_ready = sem("masks_ready"); v1_ones = sem("v1_ones"); stored = sem("stored")
        a_full = [sem(f"a_full{i}") for i in range(2)]
        a_free = [sem(f"a_free{i}") for i in range(2)]
        t_full = [sem(f"t_full{i}") for i in range(2)]
        t_free = [sem(f"t_free{i}") for i in range(2)]
        pv_full = [sem(f"pv_full{i}") for i in range(2)]
        pv_free = [sem(f"pv_free{i}") for i in range(2)]
        f_full = sem("f_full"); f_free = sem("f_free"); r_full = sem("r_full"); r_free = sem("r_free")
        ln3_stat = sem("ln3_stat"); ln3_var = sem("ln3_var"); ln3_eps = sem("ln3_eps"); ln3_rstd = sem("ln3_rstd"); xl3_ready = sem("xl3_ready")
        ln4_stat = sem("ln4_stat"); ln4_var = sem("ln4_var"); ln4_eps = sem("ln4_eps"); ln4_rstd = sem("ln4_rstd"); xl4_ready = sem("xl4_ready")
        hi3 = sem("parts_hi3"); parts3 = sem("parts_ready3"); biased3 = sem("biased3"); rden1_ready = sem("rden1_ready")
        qn_ready = sem("qn_ready"); qsq_ready = sem("qsq_ready"); rn_ready = sem("rn_ready"); expo_ready = sem("expo_ready")
        top_ready = sem("top_ready"); floor_set = sem("floor_set"); marked_ready = sem("marked_ready"); kept_ready = sem("kept_ready")
        den_ready = sem("den_ready"); rdn_ready = sem("rdn_ready"); prb_ready = sem("prb_ready"); outer_ready = sem("outer_ready")
        halved = sem("halved"); wt_ready = sem("wt_ready"); beyond_ready = sem("beyond_ready"); wt_whole = sem("wt_whole"); gw_ready = sem("gw_ready")

        A3 = {n: i for i, n in enumerate(["k0", "k1", "q", "k2", "k3", "v0", "v1", "v2"] + [f"s{i}" for i in range(H1)])}
        R3 = {n: i for i, n in enumerate(["m", "oT", "y", "x4T", "out"])}

        def a3(name, b):
            return A3[name] % 2, b * (len(A3) // 2) + A3[name] // 2

        def f3(name, b):
            if not isinstance(b, int):
                return 6 + 5 * b + ["x3T", "n2", "gT", "sc", "y2"].index(name)
            uses = [(s, n) for s in range(-2, B) for n, on in
                    (("x3T", s >= 0), ("n2", s < B - 2), ("gT", -1 <= s < B - 1), ("sc", s < B - 2), ("y2", -1 <= s < B - 1)) if on]
            return uses.index((b, name))

        def r3(name, b):
            return b * len(R3) + R3[name]

        def steps(eng, step):
            step(-2, False, False, False, True)
            step(-1, False, False, True, True)
            step(0, True, False, True, True)
            with eng.Fori(1, B - 2) as b:
                step(b, True, True, True, True)
            step(B - 2, True, True, True, False)
            step(B - 1, True, True, False, False)
            step(B, False, True, False, False)

        with nc.Block() as block:
            @block.sync
            def _(sp):
                def load(b):
                    sp.dma_start(ctx[:], ctxT[b].rearrange("(k p) m -> p k m", p=KC)).then_inc(ctx3_loaded, 16)

                def store(t):
                    sp.wait_ge(r_free, r3("out", t) + 1)
                    sp.dma_start(out[t], xs[:, t, :]).then_inc(stored, 16)

                load(0)
                with sp.Fori(1, B) as b:
                    k, n = a3("v2", b - 1)
                    sp.wait_ge(a_full[k], n + 1)
                    load(b)
                    store(b - 1)
                store(B - 1)
                sp.wait_ge(stored, 16 * B)

            @block.gpsimd
            def _(pool):
                nc.gpsimd.memset(score[:], FILL).then_inc(masks_ready, 1)
                nc.gpsimd.memset(v1[:], 1.0).then_inc(v1_ones, 1)
                pool.wait_ge(v1_ones, 1)
                nc.gpsimd.affine_select(out=v1[:, 2, :, :].rearrange("p h d -> p (h d)"), in_=v1[:, 2, :, :].rearrange("p h d -> p (h d)"),
                                        compare_op=ALU.is_ge, fill=0.0, base=-OVERLAP, pattern=[[0, H1 * (D1 + 1)]],
                                        channel_multiplier=1).then_inc(masks_ready, 1)

                def root(b, k, var, eps_added, ready):
                    pool.wait_ge(var, b + 1)
                    nc.gpsimd.tensor_tensor(vare[:, k, :], mv[:, k, 1:2], eps[:], ALU.add).then_inc(eps_added, 1)
                    pool.wait_ge(eps_added, b + 1)
                    nc.gpsimd.tensor_tensor(rstd[:, k, :], vare[:, k, :], half[0:S, :], ALU.pow).then_inc(ready, 1)

                def step(b, attn, after, mix, choose):
                    t, m, f = b - 1, b + 1, b + 2
                    if attn:
                        pool.wait_ge(xl3_ready, b + 1)
                        nc.gpsimd.tensor_tensor(xs[:, b, :], xs[:, b, :], gbo[:], ALU.add).then_inc(biased3, 1)
                    if after:
                        root(t, 1, ln4_var, ln4_eps, ln4_rstd)
                    if choose:
                        pool.wait_ge(qn_ready, f + 1)
                        nc.gpsimd.tensor_tensor(qsq[:], qn[:], qn[:], ALU.mult).then_inc(qsq_ready, 1)
                        pool.wait_ge(f_free, f3("n2", b) + 1)
                        nc.gpsimd.tensor_tensor(rn[:], n2s[:], half[0:S, :].broadcast_to([S, 16]), ALU.pow).then_inc(rn_ready, 1)
                    if mix:
                        root(m, 0, ln3_var, ln3_eps, ln3_rstd)
                    if choose:
                        pool.wait_ge(outer_ready, f + 1)
                        nc.gpsimd.tensor_tensor(outer[:, 0:4, :], outer[:, 0:4, :], outer[:, 4:8, :], ALU.add).then_inc(halved, 1)
                        pool.wait_ge(halved, 2 * f + 1)
                        nc.gpsimd.tensor_tensor(outer[:, 0:2, :], outer[:, 0:2, :], outer[:, 2:4, :], ALU.add).then_inc(halved, 1)
                        pool.wait_ge(halved, 2 * f + 2)
                        nc.gpsimd.tensor_tensor(wt[:], outer[:, 0, :], outer[:, 1, :], ALU.add).then_inc(wt_ready, 1)

                steps(pool, step)

            @block.scalar
            def _(act):
                def drain(name, b, dst, src, func=ACT.Copy, **kw):
                    k, n = a3(name, b)
                    act.wait_ge(a_full[k], n + 1)
                    nc.scalar.activation(dst, src(k), func, **kw).then_inc(a_free[k], 1)

                def step(b, attn, after, mix, choose):
                    t, m, f = b - 1, b + 1, b + 2
                    if choose:
                        nc.scalar.activation(qn[:], qall[:, :, bass.ts(f, S)], ACT.Identity, scale=qscale[:],
                                             bias=qshift[:]).then_inc(qn_ready, 1)
                    if attn:
                        drain("k0", b, kT1[:, 0, :], lambda k: bank(k, M))
                    if after:
                        act.wait_ge(r_full, r3("oT", t) + 1)
                        nc.scalar.activation(oT[:], bank(7, 4, S), ACT.Copy).then_inc(r_free, 1)
                    if attn:
                        act.wait_ge(f_full, f3("x3T", b) + 1)
                        nc.scalar.activation(xT[:], bank(6, 2, S), ACT.Copy).then_inc(f_free, 1)
                        for c in range(1, 4):
                            drain(f"k{c}", b, kT1[:, c, :], lambda k: bank(k, M))
                    if after:
                        act.wait_ge(r_full, r3("x4T", t) + 1)
                        nc.scalar.activation(xT2[:], bank(7, 2, S), ACT.Copy).then_inc(r_free, 1)
                    if attn:
                        act.wait_ge(masks_ready, 2)
                        for mc in range(3):
                            drain(f"v{mc}", b, v1[:, mc, :, 0:D1], lambda k: bank(k, H1, D1), ACT.Identity,
                                  **({"scale": lastmask[:]} if mc == 2 else {}))
                    if mix:
                        act.wait_ge(f_full, f3("gT", b) + 1)
                        nc.scalar.activation(gT[:], bank(6, 2, S), ACT.Copy).then_inc(f_free, 1)

                    def probabilities(g):
                        for mc in range(3):
                            i = 3 * g + mc
                            act.wait_ge(t_full[i % 2], 3 * b + i // 2 + 1)
                            nc.scalar.activation(prob[:, g, mc, :, :], bank(2 + i % 2, 4, S), ACT.Exp,
                                                 scale=D1 ** -0.5).then_inc(t_free[i % 2], 1)

                    if attn:
                        probabilities(0)
                    if choose:
                        act.wait_ge(f_free, f3("sc", b) + 1)
                        nc.scalar.activation(expo[:], score[:, :, 0:NKEY], ACT.Exp).then_inc(expo_ready, 1)
                    if attn:
                        probabilities(1)

                steps(act, step)

            @block.vector
            def _(dve):
                def carry():
                    nc.vector.memset(scratch[:], 0.0)

                dve.wait_ge(masks_ready, 2)

                def norm(b, k, stat_sem, var_sem):
                    carry()
                    nc.vector.bn_stats(stat[:, k, :], xs[:, b, :]).then_inc(stat_sem, 1)
                    dve.wait_ge(stat_sem, b + 1)
                    carry()
                    nc.vector.bn_aggr(mv[:, k, :], stat[:, k, :]).then_inc(var_sem, 1)

                def norm_apply(b, k, rstd_sem, ready):
                    dve.wait_ge(rstd_sem, b + 1)
                    nc.vector.tensor_scalar(xl[:, k, :], xs[:, b, :], mv[:, k, 0:1], rstd[:, k, :], ALU.subtract,
                                            ALU.mult).then_inc(ready, 1)

                def step(b, attn, after, mix, choose):
                    t, m, f = b - 1, b + 1, b + 2
                    if after:
                        for i in range(2):
                            dve.wait_ge(pv_full[i], t + 1)
                            src = bank(4 + i, 4, D1 + 1, parts=S)
                            nc.vector.reciprocal(rden1[:, 4 * i:4 * i + 4], src[:, :, D1]).then_inc(rden1_ready, 1)
                            dve.wait_ge(rden1_ready, 2 * t + i + 1)
                            nc.vector.tensor_tensor(o[:, D * i:D * i + D].rearrange("p (h d) -> p h d", h=4), src[:, :, 0:D1],
                                                    rden1[:, 4 * i:4 * i + 4].unsqueeze(2).broadcast_to([S, 4, D1]),
                                                    ALU.mult).then_inc(pv_free[i], 1)
                    if attn:
                        k, n = a3("q", b)
                        dve.wait_ge(a_full[k], n + 1)
                        nc.vector.tensor_tensor(qz1[:], bank(k, 4, S).unsqueeze(2).broadcast_to([128, 4, 2, S]),
                                                headmask1[:].unsqueeze(1).unsqueeze(3).broadcast_to([128, 4, 2, S]),
                                                ALU.mult).then_inc(a_free[k], 1)
                    if after:
                        dve.wait_ge(r_full, r3("y", t) + 1)
                        dve.wait_ge(biased3, t + 1)
                        nc.vector.scalar_tensor_tensor(xs[:, t, :], bank(7, D, parts=S), tgate[0:S, 1:2], xs[:, t, :], ALU.mult,
                                                       ALU.add).then_inc(r_free, 1)
                        dve.wait_ge(r_free, r3("y", t) + 1)
                        norm(t, 1, ln4_stat, ln4_var)
                        norm_apply(t, 1, ln4_rstd, xl4_ready)
                        dve.wait_ge(r_full, r3("out", t) + 1)
                        nc.vector.scalar_tensor_tensor(xs[:, t, :], bank(7, D, parts=S), tgate[0:S, 3:4], xs[:, t, :], ALU.mult,
                                                       ALU.add).then_inc(r_free, 1)
                    if mix:
                        dve.wait_ge(beyond_ready, m + 1)
                        dve.wait_ge(wt_ready, m + 1)
                        nc.vector.tensor_tensor(wt[:, NEXP - 1:NEXP], wt[:, NEXP - 1:NEXP], beyond[:], ALU.add).then_inc(wt_whole, 1)
                        dve.wait_ge(wt_whole, m + 1)
                        nc.vector.tensor_tensor(gw[:], wt[:], hidden[:, m, :], ALU.mult).then_inc(gw_ready, 1)
                    if choose:
                        dve.wait_ge(f_full, f3("n2", b) + 1)
                        nc.vector.tensor_scalar(n2s[:], bank(6, 16, parts=S), TINY, None, ALU.max).then_inc(f_free, 1)
                    if attn:
                        for i in range(H1):
                            k, n = a3(f"s{i}", b)
                            dve.wait_ge(a_full[k], n + 1)
                            nc.vector.reduce_max(mx[:, i:i + 1], bank(k, M, parts=S), AX.X).then_inc(a_free[k], 1)
                        for i in (H1 - 2, H1 - 1):
                            k, n = a3(f"s{i}", b)
                            dve.wait_ge(a_free[k], n + 1)
                        nc.vector.tensor_copy(parts[:, 0, 0:8], mx[:, 0:8]).then_inc(hi3, 1)
                        dve.wait_ge(hi3, b + 1)
                        nc.vector.tensor_tensor(parts[:, 0, 32:40], mx[:, 0:8], parts[:, 0, 0:8], ALU.subtract).then_inc(parts3, 1)
                    if attn:
                        dve.wait_ge(r_full, r3("m", b) + 1)
                        nc.vector.tensor_tensor(mxb[:, 0, :, :], bank(7, S, parts=96, dt=BF16).unsqueeze(1).broadcast_to([96, 8, S]),
                                                partmask[:].unsqueeze(2).broadcast_to([96, 8, S]), ALU.mult).then_inc(r_free, 1)
                    if choose:
                        dve.wait_ge(f_full, f3("sc", b) + 1)
                        dve.wait_ge(rn_ready, f + 1)
                        nc.vector.tensor_tensor(score[:, :, 0:NKEY], bank(6, 16, NKEY, parts=S), rn[:].unsqueeze(2).broadcast_to([S, 16, NKEY]),
                                                ALU.mult).then_inc(f_free, 1)
                        dve.wait_ge(f_free, f3("sc", b) + 1)
                        carry()
                        for g in range(16):
                            nc.vector.max(top8[:, g, :], score[:, g, :]).then_inc(top_ready, 1)
                        dve.wait_ge(top_ready, 16 * f + 16)
                        nc.vector.memset(top8[:, :, TOP:8], FILL).then_inc(floor_set, 1)
                        dve.wait_ge(floor_set, f + 1)
                        carry()
                        for g in range(16):
                            nc.vector.match_replace(marked[:, g, :], top8[:, g, :], score[:, g, :], TAKEN).then_inc(marked_ready, 1)
                        dve.wait_ge(marked_ready, 16 * f + 16)
                        dve.wait_ge(expo_ready, f + 1)
                        nc.vector.scalar_tensor_tensor(kept[:], marked[:, :, 0:NKEY], TAKEN / 2, expo[:], ALU.is_ge,
                                                       ALU.mult).then_inc(kept_ready, 1)
                        dve.wait_ge(kept_ready, f + 1)
                        nc.vector.reduce_sum(den[:], kept[:], AX.X).then_inc(den_ready, 1)
                        dve.wait_ge(den_ready, f + 1)
                        nc.vector.reciprocal(rdn[:], den[:]).then_inc(rdn_ready, 1)
                        dve.wait_ge(rdn_ready, f + 1)
                        nc.vector.tensor_tensor(prb[:].rearrange("p h s k -> p (h s) k"), kept[:], rdn[:].unsqueeze(2).broadcast_to([S, 16, NKEY]),
                                                ALU.mult).then_inc(prb_ready, 1)
                        dve.wait_ge(prb_ready, f + 1)
                        nc.vector.tensor_tensor(outer[:].rearrange("p h (i j) -> p h i j", i=8),
                                                prb[:, :, 0, 0:8].unsqueeze(3).broadcast_to([S, 8, 8, NKEY]),
                                                prb[:, :, 1, :].unsqueeze(2).broadcast_to([S, 8, 8, NKEY]), ALU.mult).then_inc(outer_ready, 1)
                        nc.vector.reduce_sum(beyond[:], prb[:, :, 0, 8:NKEY], AX.XY).then_inc(beyond_ready, 1)
                    if mix:
                        dve.wait_ge(f_full, f3("y2", b) + 1)
                        nc.vector.scalar_tensor_tensor(xs[:, m, :], bank(6, D, parts=S), tgate[0:S, 2:3], xs[:, m, :], ALU.mult,
                                                       ALU.add).then_inc(f_free, 1)
                        dve.wait_ge(f_free, f3("y2", b) + 1)
                        norm(m, 0, ln3_stat, ln3_var)
                        norm_apply(m, 0, ln3_rstd, xl3_ready)

                steps(dve, step)

            @block.tensor
            def _(pe):
                def step(b, attn, after, mix, choose):
                    t, m, f = b - 1, b + 1, b + 2

                    def project(name, dst, pairs):
                        k, n = a3(name, b)
                        need(pe, a_free[k], n)
                        for j in range(len(pairs)):
                            last = nc.tensor.matmul(dst(k), pairs[j][0], pairs[j][1], start=j == 0, stop=j == len(pairs) - 1)
                        last.then_inc(a_full[k], 1)

                    def keys_of(c):
                        project(f"k{c}", lambda k: bank(k, M), [(wk1[:, k, 128 * c:128 * c + 128], ctx[:, k, :]) for k in range(2)])

                    def values_of(mc):
                        project(f"v{mc}", lambda k: bank(k, HID), [(ctx[:, k, chunk[mc]], wv1[:, k, :]) for k in range(2)])

                    def probabilities(g):
                        for mc in range(3):
                            i = 3 * g + mc
                            need(pe, t_free[i % 2], 3 * b + i // 2)
                            dst = bank(2 + i % 2, 4 * S)
                            nc.tensor.matmul(dst, negones[:], mxb[:, 0, 4 * g:4 * g + 4, :].rearrange("p h s -> p (h s)"), start=True,
                                             stop=False)
                            for c in range(2):
                                last = nc.tensor.matmul(dst[:, 2 * S * c:2 * S * c + 2 * S], kT1[:, 2 * g + c, chunk[mc]],
                                                        qz1[:, 2 * g + c, :, :].rearrange("p h s -> p (h s)"), start=False, stop=c == 1)
                            last.then_inc(t_full[i % 2], 1)

                    def attend(g):
                        need(pe, pv_free[g], b)
                        for i in (3 * g + 1, 3 * g + 2):
                            pe.wait_ge(t_free[i % 2], 3 * b + i // 2 + 1)
                        for j in range(4):
                            for mc in range(3):
                                last = nc.tensor.matmul(bank(4 + g, 4, D1 + 1, parts=S)[:, j, :], prob[:, g, mc, j, :],
                                                        v1[:, mc, 4 * g + j, :], start=mc == 0, stop=mc == 2)
                        last.then_inc(pv_full[g], 1)

                    if attn:
                        pe.wait_ge(ctx3_loaded, 16 * b + 16)
                        keys_of(0)
                    if after:
                        need(pe, r_free, r3("oT", t))
                        for i in range(2):
                            pe.wait_ge(pv_free[i], t + 1)
                        for k in range(4):
                            last = nc.tensor.transpose(bank(7, 4, S)[:, k, :], o[:, 128 * k:128 * k + 128], ident[0:S, 0:S])
                        last.then_inc(r_full, 1)
                    if attn:
                        pe.wait_ge(xl3_ready, b + 1)
                        need(pe, f_free, f3("x3T", b))
                        for k in range(2):
                            last = nc.tensor.transpose(bank(6, 2, S)[:, k, :], xl[:, 0, 128 * k:128 * k + 128], ident[0:S, 0:S])
                        last.then_inc(f_full, 1)
                        keys_of(1)
                        k, n = a3("q", b)
                        need(pe, a_free[k], n)
                        pe.wait_ge(f_free, f3("x3T", b) + 1)
                        for mo in range(4):
                            for j in range(2):
                                last = nc.tensor.matmul(bank(k, 4, S)[:, mo, :], wq1[:, j, 128 * mo:128 * mo + 128], xT[:, j, :],
                                                        start=j == 0, stop=j == 1)
                        last.then_inc(a_full[k], 1)
                    if after:
                        need(pe, r_free, r3("y", t))
                        for k in range(4):
                            last = nc.tensor.matmul(bank(7, D, parts=S), oT[:, k, :], wo1[:, k, :], start=k == 0, stop=k == 3)
                        last.then_inc(r_full, 1)
                    if attn:
                        keys_of(2)
                        keys_of(3)
                    if after:
                        need(pe, r_free, r3("x4T", t))
                        pe.wait_ge(xl4_ready, t + 1)
                        for k in range(2):
                            last = nc.tensor.transpose(bank(7, 2, S)[:, k, :], xl[:, 1, 128 * k:128 * k + 128], ident[0:S, 0:S])
                        last.then_inc(r_full, 1)
                    if attn:
                        values_of(0)
                        values_of(1)
                    if after:
                        need(pe, r_free, r3("out", t))
                        for k in range(2):
                            last = nc.tensor.matmul(bank(7, D, parts=S), xT2[:, k, :], prod[:, k, :], start=k == 0, stop=k == 1)
                        last.then_inc(r_full, 1)
                    if choose:
                        need(pe, f_free, f3("n2", b))
                        pe.wait_ge(qsq_ready, f + 1)
                        for c in range(4):
                            last = nc.tensor.matmul(bank(6, 4, 4, parts=S)[:, c, :], qsq[:, c, :], ones4[:], start=True, stop=True)
                        last.then_inc(f_full, 1)
                    if attn:
                        values_of(2)
                    if mix:
                        need(pe, f_free, f3("gT", b))
                        pe.wait_ge(gw_ready, m + 1)
                        for k in range(2):
                            last = nc.tensor.transpose(bank(6, 2, S)[:, k, :], gw[:, 128 * k:128 * k + 128], ident[0:S, 0:S])
                        last.then_inc(f_full, 1)
                    if attn:
                        for name in ("k2", "k3"):
                            k, n = a3(name, b)
                            pe.wait_ge(a_free[k], n + 1)
                        for i in range(H1):
                            k, n = a3(f"s{i}", b)
                            need(pe, a_free[k], n)
                            nc.tensor.matmul(bank(k, M, parts=S), qz1[:, i // 2, i % 2, :], kT1[:, i // 2, :], start=True,
                                             stop=True).then_inc(a_full[k], 1)
                    if attn:
                        need(pe, r_free, r3("m", b))
                        pe.wait_ge(parts3, b + 1)
                        nc.tensor.transpose(bank(7, S, parts=96, dt=BF16), parts[:, 0, :], identb[0:S, 0:S]).then_inc(r_full, 1)
                    if choose:
                        need(pe, f_free, f3("sc", b))
                        for c in range(4):
                            last = nc.tensor.matmul(bank(6, 4, 128, parts=S)[:, c, :], qn[:, c, :], keyT[:], start=True, stop=True)
                        last.then_inc(f_full, 1)
                    if attn:
                        pe.wait_ge(r_free, r3("m", b) + 1)
                        probabilities(0)
                    if mix:
                        need(pe, f_free, f3("y2", b))
                        for k in range(2):
                            last = nc.tensor.matmul(bank(6, D, parts=S), gT[:, k, :], ups[:, k, :], start=k == 0, stop=k == 1)
                        last.then_inc(f_full, 1)
                    if attn:
                        probabilities(1)
                        attend(0)
                        attend(1)

                steps(pe, step)



_INS = ["x", "ctxT", "g_xattn", "g_ffn", "L0_xattn_Wq", "L0_xattn_bq", "L0_xattn_Wk", "L0_xattn_bk", "L0_xattn_Wv", "L0_xattn_bv",
        "L0_xattn_W1", "L0_xattn_b1", "L0_xattn_W2", "L0_xattn_b2", "L0_ffn_Wq", "L0_ffn_bq", "L0_ffn_bn_gamma", "L0_ffn_bn_beta",
        "L0_ffn_sub_key0", "L0_ffn_sub_key1", "downT", "L0_ffn_expert_up", "L1_xattn_Wq", "L1_xattn_Wk", "L1_xattn_Wv",
        "L1_xattn_Wo", "L1_xattn_bo", "w1T", "w2"]


def kernel(**inputs):
    import numpy as _np
    import concourse.bacc as _bacc
    from concourse import mybir as _mybir
    from concourse.bass_utils import run_bass_kernel_spmd as _run

    laid = {n: _np.asarray(a) for n, a in inputs.items()}
    laid["ctxT"] = laid["ctx_768"].transpose(0, 2, 1)
    for n, k in (("L0_xattn_bq", 2), ("L0_xattn_bk", 2), ("L0_ffn_bq", 4)):
        laid[n] = laid[n].reshape(k, 128).T
    laid["downT"] = laid["L0_ffn_expert_down"].T
    laid["w1T"] = laid["L1_ffn_w1"].transpose(0, 2, 1).reshape(B, 128, 4, D)
    laid["w2"] = laid["L1_ffn_w2"].reshape(B, 128, 4, D)

    nc = _bacc.Bacc("TRN2", target_bir_lowering=False, num_devices=1)
    arrays, args = {}, []
    for name in _INS:
        a = _np.ascontiguousarray(laid[name])
        arrays[f"in_{name}"] = a
        args.append(nc.dram_tensor(f"in_{name}", a.shape, _mybir.dt.from_np(a.dtype), kind="ExternalInput").ap())
    args.append(nc.dram_tensor("out_0", (B, S, D), _mybir.dt.float32, kind="ExternalOutput").ap())
    program(nc, *args)
    r = _run(nc, [arrays], core_ids=[0])
    return r.results[0]["out_0"]
```

```python
from contextlib import ExitStack

import concourse.bass as bass
from concourse import mybir

F32 = mybir.dt.float32
BF16 = mybir.dt.bfloat16
F32R = mybir.dt.float32r
ALU = mybir.AluOpType
ACT = mybir.ActivationFunctionType
AX = mybir.AxisListType

B, S, D = 16, 100, 256
M, DC = 361, 192
DT = DC - 128
MP = M + 1
KEY0, VAL0, KEY1, VAL1 = (slice(0, 256), slice(256, 512), slice(512, 1024), slice(1024, 1536))
H0, D0 = 16, 16
H1, D1 = 8, 64
HID = 512
MSTART = [0, 128, M - 128]
OVERLAP = 2 * 128 - MSTART[2]
TOP, NKEY, NEXP = 4, 32, 256
WK = B * 4
EPS = 1e-5
TINY = 1e-24


def program(nc, x, ctxT, g_xattn, g_ffn, Wq0, bq0, Wk0, bk0, Wv0, bv0, W1, b1, W2, b2, Wqf, bqf, gamma, beta,
            key0, key1, downT, up, Wq1, Wk1, Wv1, Wo1, bo1, w1T, w2, out):
    with ExitStack() as stack:
        def sb(name, shape, dt=F32):
            return stack.enter_context(nc.sbuf_tensor(name, shape, dt))

        def sem(name):
            return stack.enter_context(nc.semaphore(name))

        psum = stack.enter_context(nc.psum_tensor("psum", [128, 8, 512], F32))

        def bank(n, *dims, parts=128, dt=F32):
            size = 1
            for d in dims:
                size *= d
            ap = psum[0:parts, n, 0:size] if dt == F32 else psum[0:parts, n, :].bitcast(dt)[:, 0:size]
            if len(dims) == 1:
                return ap
            names = " ".join("abc"[:len(dims)])
            return ap.rearrange(f"p ({names}) -> p {names}", **{n: d for n, d in zip("abc", dims)})

        wctx = sb("wctx", [128, 4, 1536], F32R)
        bq0s = sb("bq0s", [128, 2]); bk0s = sb("bk0s", [128, 2]); bqfs = sb("bqfs", [128, 4])
        bv0b = sb("bv0b", [128, D]); bv0m = sb("bv0m", [128, D])
        b1b = sb("b1b", [S, HID]); b2b = sb("b2b", [S, D]); bo1b = sb("bo1b", [S, D])
        gb2 = sb("gb2", [S, D]); gbo = sb("gbo", [S, D])
        gate = sb("gate", [128, 4]); tgate = sb("tgate", [128, 4])
        gam = sb("gam", [128, 1]); bet = sb("bet", [128, 1])
        keys = sb("keys", [128, NKEY])
        ident = sb("ident", [128, 128]); identb = sb("identb", [128, 128], BF16)
        negones = sb("negones", [96, 128], BF16)
        partmask = sb("partmask", [96, 8])
        quads = sb("quads", [128, 4, 2]); pairmask = sb("pairmask", [128, 2])
        negupper = sb("negupper", [128, 1])
        headmask1 = sb("headmask1", [128, 2])
        ones4 = sb("ones4", [128, 4])
        lastmask = sb("lastmask", [128, 1])
        samedim = sb("samedim", [128, 128])
        half = sb("half", [128, 1])
        eps = sb("eps", [S, 1]); scratch = sb("scratch", [1, 1])
        xs = sb("xs", [S, B, D])
        hidden = sb("hidden", [S, B, NEXP])
        qall = sb("qall", [128, 4, B * S])
        qstat = sb("qstat", [128, 4, B, 6])
        prod = sb("prod", [128, 2, D])
        ctx = sb("ctx", [128, 2, MP])
        cparts = sb("cparts", [128, 4, MP], F32R)
        stat = sb("stat", [S, 2, 6]); mv = sb("mv", [S, 2, 2]); rstd = sb("rstd", [S, 2, 1]); vare = sb("vare", [S, 2, 1])
        xl = sb("xl", [S, 2, D]); xT = sb("xT", [128, 2, S]); xT2 = sb("xT2", [128, 2, S])
        mx = sb("mx", [S, H0]); parts = sb("parts", [S, 2, 96], BF16); mxb = sb("mxb", [96, 2, 8, S], BF16)
        prob = sb("prob", [128, 2, 3, 4, S])
        oTp = sb("oTp", [128, 4, S]); rden = sb("rden", [S, H0]); o = sb("o", [S, HID]); oT = sb("oT", [128, 4, S])
        early = stack.enter_context(ExitStack())

        def sb1(name, shape, dt=F32):
            return early.enter_context(nc.sbuf_tensor(name, shape, dt))

        wq0 = sb1("wq0", [128, 2, D])
        w1s = sb1("w1s", [128, 2, HID]); w2s = sb1("w2s", [128, 4, D]); wqf = sb1("wqf", [128, 2, HID])
        downs = sb1("downs", [128, 2, NEXP])
        e1 = sb1("e1", [128, 4, D]); e2 = sb1("e2", [128, 4, D])
        qT = sb1("qT", [128, 2, S]); qm = sb1("qm", [128, 2, 2, S])
        qhi = sb1("qhi", [128, 2, 2, S], F32R); qlo = sb1("qlo", [128, 2, 2, S], F32R)
        khi = sb1("khi", [128, 2, MP], F32R); klo = sb1("klo", [128, 2, MP], F32R)
        qstack = sb1("qstack", [96, 2, 2, 4, 2, S], F32R); kstack = sb1("kstack", [96, 2, 2, 4, MP], F32R)
        v0 = sb1("v0", [128, 3, H0, 32])
        h = sb1("h", [S, HID]); hT = sb1("hT", [128, 4, S])
        loaded = sem("loaded"); x_loaded = sem("x_loaded"); ctx_loaded = sem("ctx_loaded"); e_loaded = sem("e_loaded")
        late_loaded = sem("late_loaded")
        zeroed = sem("zeroed"); selected = sem("selected"); gates_ready = sem("gates_ready"); consts_ready = sem("consts_ready")
        ring_full = [sem(f"ring_full{i}") for i in range(4)]
        ring_free = [sem(f"ring_free{i}") for i in range(4)]
        st_full = [sem(f"st_full{i}") for i in range(2)]
        st_free = [sem(f"st_free{i}") for i in range(2)]
        o_full = sem("o_full"); o_free = sem("o_free")
        tail_full = sem("tail_full"); tail_free = sem("tail_free")
        ln1_stat = sem("ln1_stat"); ln1_var = sem("ln1_var"); ln1_eps = sem("ln1_eps"); ln1_rstd = sem("ln1_rstd"); xl1_ready = sem("xl1_ready")
        ln2_stat = sem("ln2_stat"); ln2_var = sem("ln2_var"); ln2_eps = sem("ln2_eps"); ln2_rstd = sem("ln2_rstd"); xl2_ready = sem("xl2_ready")
        q_masked = sem("q_masked"); q_hi = sem("q_hi"); q_lo = sem("q_lo"); k_hi = sem("k_hi")
        qstack_loaded = sem("qstack_loaded"); kstack_loaded = sem("kstack_loaded"); padded = sem("padded")
        wparts_ready = sem("wparts_ready"); wstage_loaded = sem("wstage_loaded"); halves = sem("halves")
        ctx_hi = sem("ctx_hi"); ctx_lo = sem("ctx_lo"); ctx_mix = sem("ctx_mix")
        biased = sem("biased"); parts_hi = sem("parts_hi"); parts_ready = sem("parts_ready")
        rden_ready = sem("rden_ready"); qstat_done = sem("qstat_done"); mul_done = sem("mul_done")

        def need(eng, s, value):
            if not isinstance(value, int) or value > 0:
                eng.wait_ge(s, value)

        NEXT = ["k0", "k1", "xT", "q"]
        RING = ["v0", "v1", "v2", "prod", "s0", "s1", "s2", "s3", "s4", "s5", "s6", "s7", "k0", "k1", "s8", "s9", "s10", "s11",
                "xT", "s12", "q", "s13", "s14", "s15"]
        ST = [f"t{i}" for i in range(12)]
        TAIL = ["nat", "oT", "h", "hT", "y", "x2T", "qf", "down", "m0", "m1"]

        def ring(name, b):
            if isinstance(b, int) and b < 0:
                return NEXT.index(name), 0
            order = RING if not isinstance(b, int) or b < B - 1 else [n for n in RING if n not in NEXT]
            i = order.index(name)
            return i % 4, b * (len(RING) // 4) + i // 4 + 1

        def stb(name, b):
            i = ST.index(name)
            return i % 2, b * (len(ST) // 2) + i // 2

        def tail(name, t):
            return t * len(TAIL) + TAIL.index(name) + 2

        def steps(eng, step):
            step(0, 0, True, False, True)
            with eng.Fori(0, (B - 2) // 2) as i:
                step(i * 2 + 1, 1, True, True, True)
                step(i * 2 + 2, 0, True, True, True)
            step(B - 1, 1, True, True, False)
            step(B, 0, False, True, False)

        chunk = [slice(m, m + 128) for m in MSTART]

        PASSES = [(0, 0), (0, 1), (1, 0), (2, 2), (3, 3)]

        def split_hi(act, n, loaded_sem, hi):
            act.wait_ge(loaded_sem, 48 * n + 48)
            nc.scalar.activation(cparts[:, 0, :], ctx[:, 0, :], ACT.Identity).then_inc(hi, 1)
            nc.scalar.activation(cparts[:, 3, :], ctx[:, 1, :], ACT.Identity).then_inc(hi, 1)

        def split_lo(pool, n, hi, lo):
            pool.wait_ge(hi, 2 * n + 2)
            nc.gpsimd.tensor_tensor(cparts[:, 1, :], ctx[:, 0, :], cparts[:, 0, :].bitcast(F32), ALU.subtract).then_inc(lo, 1)

        def split_mix(dve, n, hi, mix):
            dve.wait_ge(hi, 2 * n + 2)
            nc.vector.scalar_tensor_tensor(cparts[:, 2, :], cparts[:, 3, :].bitcast(F32), negupper[:], ctx[:, 1, :], ALU.mult,
                                           ALU.add).then_inc(mix, 1)

        def load_context(eng, b, done):
            eng.dma_start(ctx[:, 0, 0:M], ctxT[b, 0:128, :]).then_inc(done, 16)
            for i in range(2):
                eng.dma_start(ctx[64 * i:64 * i + 64, 1, 0:M], ctxT[b, 128:DC, :]).then_inc(done, 16)

        wstage = qall[:].rearrange("p c n -> p (c n)")[:, 0:2 * 1536].rearrange("p (k n) -> p k n", k=2)

        with nc.Block() as block:
            @block.sync
            def _(sp):
                sp.dma_start(xs[:], x.rearrange("b s d -> s b d")).then_inc(x_loaded, 16)

                def load_experts(b):
                    sp.dma_start(e1[:], w1T[b]).then_inc(e_loaded, 16)
                    sp.dma_start(e2[:], w2[b]).then_inc(e_loaded, 16)

                sp.dma_start(wq0[:], Wq0.rearrange("(k p) n -> p k n", p=128)).then_inc(loaded, 16)
                load_context(sp, 0, ctx_loaded)
                for cols, w in ((KEY0, Wk0), (VAL0, Wv0), (KEY1, Wk1), (VAL1, Wv1)):
                    sp.dma_start(wstage[:, 0, cols], w[0:128, :]).then_inc(wstage_loaded, 16)
                    for i in range(2):
                        sp.dma_start(wstage[64 * i:64 * i + 64, 1, cols], w[128:DC, :]).then_inc(wstage_loaded, 16)
                sp.dma_start(bq0s[:], bq0).then_inc(loaded, 16)
                sp.dma_start(bk0s[:], bk0).then_inc(loaded, 16)
                sp.dma_start(bqfs[:], bqf).then_inc(loaded, 16)
                sp.dma_start(bv0b[:], bv0.partition_broadcast(128)).then_inc(loaded, 16)
                sp.dma_start(b1b[:], b1.partition_broadcast(S)).then_inc(loaded, 16)
                sp.dma_start(b2b[:], b2.partition_broadcast(S)).then_inc(loaded, 16)
                sp.dma_start(gate[:, 0:2], g_xattn.partition_broadcast(128)).then_inc(loaded, 16)
                sp.dma_start(gate[:, 2:4], g_ffn.partition_broadcast(128)).then_inc(loaded, 16)
                load_experts(0)
                sp.dma_start(w1s[:], W1.rearrange("(k p) n -> p k n", p=128)).then_inc(loaded, 16)
                sp.dma_start(w2s[:], W2.rearrange("(k p) n -> p k n", p=128)).then_inc(loaded, 16)
                sp.dma_start(wqf[:], Wqf.rearrange("(k p) n -> p k n", p=128)).then_inc(loaded, 16)
                sp.dma_start(downs[:], downT.rearrange("(k p) n -> p k n", p=128)).then_inc(loaded, 16)
                sp.dma_start(bo1b[:], bo1.partition_broadcast(S)).then_inc(loaded, 16)
                for i in range(4):
                    sp.dma_start(keys[32 * i:32 * i + 32, :], (key0, key1)[i % 2]).then_inc(late_loaded, 16)
                for i in range(2):
                    sp.dma_start(gam[64 * i:64 * i + 64, :], gamma.rearrange("(p a) -> p a", a=1)).then_inc(late_loaded, 16)
                    sp.dma_start(bet[64 * i:64 * i + 64, :], beta.rearrange("(p a) -> p a", a=1)).then_inc(late_loaded, 16)

                def load_stacks(b, p):
                    bk, n = ring("k1", b - 1)
                    sp.wait_ge(ring_free[bk], n + 1)
                    for a, part in enumerate((khi, khi, klo)):
                        for q in range(4):
                            sp.dma_start(kstack[32 * a:32 * a + 32, p, :, q, :].bitcast(F32),
                                         part[32 * q:32 * q + 32, :, :].bitcast(F32)).then_inc(kstack_loaded, 16)
                    sp.wait_ge(q_lo, b + 1)
                    for a, part in enumerate((qhi, qlo, qhi)):
                        for q in range(4):
                            sp.dma_start(qstack[32 * a:32 * a + 32, p, :, q, :, :].bitcast(F32),
                                         part[32 * q:32 * q + 32, :, :, :].bitcast(F32)).then_inc(qstack_loaded, 16)

                def next_context(b):
                    sp.wait_ge(ctx_lo, b)
                    sp.wait_ge(ctx_mix, b)
                    load_context(sp, b, ctx_loaded)

                def step(b, p, two_more):
                    bk, n = ring("prod", b)
                    sp.wait_ge(ring_full[bk], n + 1)
                    load_experts(b + 1)
                    if two_more:
                        next_context(b + 2)
                    load_stacks(b + 1, 1 - p)

                next_context(1)
                load_stacks(0, 0)
                with sp.Fori(0, (B - 2) // 2) as i:
                    step(i * 2, 0, True)
                    step(i * 2 + 1, 1, True)
                step(B - 2, 0, False)
                sp.wait_ge(late_loaded, 8 * 16)
            NLOADED = 14 * 16

            @block.gpsimd
            def _(pool):
                for t in (ident, identb, samedim, parts, partmask):
                    nc.gpsimd.memset(t[:], 0.0).then_inc(zeroed, 1)
                for t in (quads, headmask1, ones4, lastmask, v0):
                    nc.gpsimd.memset(t[:], 1.0).then_inc(zeroed, 1)
                nc.gpsimd.memset(ctx[:, :, M:MP], 0.0).then_inc(padded, 1)
                nc.gpsimd.memset(negupper[:], -1.0).then_inc(zeroed, 1)
                nc.gpsimd.memset(negones[:], -1.0).then_inc(consts_ready, 1)
                nc.gpsimd.memset(half[:], -0.5).then_inc(consts_ready, 1)
                nc.gpsimd.memset(eps[:], EPS).then_inc(consts_ready, 1)
                pool.wait_ge(zeroed, 11)

                done = [0]

                def select(ap, pattern, base, op, fill, cm=1):
                    done[0] += 1
                    nc.gpsimd.affine_select(out=ap, in_=ap, compare_op=op, fill=fill, base=base, pattern=pattern,
                                            channel_multiplier=cm).then_inc(selected, 1)
                    pool.wait_ge(selected, done[0])

                for t in (ident, identb):
                    select(t[:], [[-1, 128]], 0, ALU.not_equal, 1.0)
                for off in (0, 64, -64):
                    select(samedim[:], [[-1, 128]], off, ALU.not_equal, 1.0 / 8)
                for off in (0, -32):
                    select(partmask[:], [[-1, 8]], off, ALU.not_equal, 1.0)
                for t, n in ((headmask1, 2), (ones4, 4)):
                    select(t[:], [[-128 // n, n]], 0, ALU.is_ge, 0.0)
                    select(t[:], [[128 // n, n]], 128 // n - 1, ALU.is_ge, 0.0, cm=-1)
                select(quads[:], [[-32, 4], [-16, 2]], 0, ALU.is_ge, 0.0)
                select(quads[:], [[32, 4], [16, 2]], 15, ALU.is_ge, 0.0, cm=-1)
                for i in range(2):
                    nc.gpsimd.tensor_tensor(quads[:, i, :], quads[:, i, :], quads[:, i + 2, :], ALU.add).then_inc(halves, 1)
                pool.wait_ge(halves, 2)
                nc.gpsimd.tensor_tensor(pairmask[:], quads[:, 0, :], quads[:, 1, :], ALU.add).then_inc(halves, 1)
                pool.wait_ge(halves, 3)
                select(negupper[:], [[0, 1]], -64, ALU.is_ge, 0.0)
                select(lastmask[:], [[0, 1]], -OVERLAP, ALU.is_ge, 0.0)
                select(v0[:, 2, :, :].rearrange("p h d -> p (h d)"), [[0, H0 * 32]], -OVERLAP, ALU.is_ge, 0.0)
                pool.wait_ge(loaded, NLOADED)
                pool.wait_ge(gates_ready, 1)
                nc.gpsimd.tensor_scalar(gb2[:], b2b[:], tgate[0:S, 0:1], None, ALU.mult).then_inc(consts_ready, 1)
                nc.gpsimd.tensor_scalar(gbo[:], bo1b[:], tgate[0:S, 1:2], None, ALU.mult).then_inc(consts_ready, 1)
                nc.gpsimd.tensor_scalar(bv0m[:], bv0b[:], lastmask[:], None, ALU.mult).then_inc(consts_ready, 1)
                pool.wait_ge(consts_ready, 6)

                def root1(b):
                    pool.wait_ge(ln1_var, b + 1)
                    nc.gpsimd.tensor_tensor(vare[:, 0, :], mv[:, 0, 1:2], eps[:], ALU.add).then_inc(ln1_eps, 1)
                    pool.wait_ge(ln1_eps, b + 1)
                    nc.gpsimd.tensor_tensor(rstd[:, 0, :], vare[:, 0, :], half[0:S, :], ALU.pow).then_inc(ln1_rstd, 1)

                def bias_residual(b):
                    pool.wait_ge(xl1_ready, b + 1)
                    nc.gpsimd.tensor_tensor(xs[:, b, :], xs[:, b, :], gb2[:], ALU.add).then_inc(biased, 1)

                def mask_queries(b):
                    bk, n = ring("q", b - 1)
                    pool.wait_ge(ring_free[bk], n + 1)
                    nc.gpsimd.tensor_tensor(
                        qm[:], qT[:].unsqueeze(2).broadcast_to([128, 2, 2, S]),
                        pairmask[:].unsqueeze(1).unsqueeze(3).broadcast_to([128, 2, 2, S]), ALU.mult).then_inc(q_masked, 1)
                    pool.wait_ge(q_hi, b + 1)
                    nc.gpsimd.tensor_tensor(qlo[:], qm[:], qhi[:].bitcast(F32), ALU.subtract).then_inc(q_lo, 1)

                def step(b, p, attn, after, more):
                    if more:
                        root1(b + 1)
                        split_lo(pool, b + 1, ctx_hi, ctx_lo)
                    if after:
                        t = b - 1
                        pool.wait_ge(ln2_var, t + 1)
                        nc.gpsimd.tensor_tensor(vare[:, 1, :], mv[:, 1, 1:2], eps[:], ALU.add).then_inc(ln2_eps, 1)
                        pool.wait_ge(ln2_eps, t + 1)
                        nc.gpsimd.tensor_tensor(rstd[:, 1, :], vare[:, 1, :], half[0:S, :], ALU.pow).then_inc(ln2_rstd, 1)
                    if more:
                        bias_residual(b + 1)
                        mask_queries(b + 1)

                split_lo(pool, 0, ctx_hi, ctx_lo)
                root1(0)
                bias_residual(0)
                mask_queries(0)
                steps(pool, step)

            @block.scalar
            def _(act):
                act.wait_ge(loaded, NLOADED)
                nc.scalar.activation(tgate[:], gate[:], ACT.Tanh).then_inc(gates_ready, 1)

                act.wait_ge(wstage_loaded, 12 * 16)
                nc.scalar.activation(wctx[:, 0, :], wstage[:, 0, :], ACT.Identity).then_inc(wparts_ready, 1)
                nc.scalar.activation(wctx[:, 2, :], wstage[:, 1, :], ACT.Identity).then_inc(wparts_ready, 1)
                act.wait_ge(padded, 1)

                def drain_tail(name, b, dst, src, func=ACT.Copy):
                    act.wait_ge(tail_full, tail(name, b) + 1)
                    nc.scalar.activation(dst, src, func).then_inc(tail_free, 1)

                def round_keys(b, c):
                    bk, n = ring(f"k{c}", b - 1)
                    act.wait_ge(ring_full[bk], n + 1)
                    nc.scalar.activation(khi[:, c, :], bank(bk, MP), ACT.Identity, bias=bk0s[:, c:c + 1]).then_inc(k_hi, 1)

                def drain_xT(b):
                    bk, n = ring("xT", b - 1)
                    act.wait_ge(ring_full[bk], n + 1)
                    nc.scalar.activation(xT[:], bank(bk, 2, S), ACT.Copy).then_inc(ring_free[bk], 1)

                def round_queries(b):
                    act.wait_ge(q_masked, b + 1)
                    nc.scalar.activation(qhi[:], qm[:], ACT.Identity).then_inc(q_hi, 1)

                def step(b, p, attn, after, more):
                    t = b - 1
                    if after:
                        drain_tail("oT", t, oT[:, 0:2, :], bank(7, 2, S))
                    if more:
                        bk, n = ring("v2", b)
                        act.wait_ge(ring_full[bk], n + 1)
                        split_hi(act, b + 1, ctx_loaded, ctx_hi)
                    if after:
                        drain_tail("hT", t, hT[:], bank(7, 4, S), ACT.Relu)
                    if more:
                        round_keys(b + 1, 0)
                    if after:
                        drain_tail("x2T", t, xT2[:], bank(7, 2, S))
                    if more:
                        round_keys(b + 1, 1)
                        drain_xT(b + 1)
                    if after:
                        drain_tail("down", t, hidden[:, t, :], bank(7, NEXP, parts=S))
                    if attn:
                        for i in range(12):
                            sb_, n = stb(f"t{i}", b)
                            act.wait_ge(st_full[sb_], n + 1)
                            nc.scalar.activation(prob[:, i // 3 % 2, i % 3, :, :], bank(4 + sb_, 4, S), ACT.Exp,
                                                 scale=D0 ** -0.5).then_inc(st_free[sb_], 1)
                            if more and i == 2:
                                round_queries(b + 1)
                        act.wait_ge(o_full, b + 1)
                        nc.scalar.activation(oTp[:], bank(6, 4, S), ACT.Copy).then_inc(o_free, 1)

                split_hi(act, 0, ctx_loaded, ctx_hi)
                for c in range(2):
                    round_keys(0, c)
                drain_xT(0)
                round_queries(0)
                steps(act, step)

            @block.vector
            def _(dve):
                def carry():
                    nc.vector.memset(scratch[:], 0.0)

                dve.wait_ge(x_loaded, 16)
                dve.wait_ge(loaded, NLOADED)
                dve.wait_ge(consts_ready, 6)
                dve.wait_ge(selected, 16)

                dve.wait_ge(wparts_ready, 2)
                nc.vector.tensor_tensor(wctx[:, 1, :], wstage[:, 0, :], wctx[:, 0, :].bitcast(F32), ALU.subtract).then_inc(wparts_ready, 1)
                nc.vector.tensor_tensor(wctx[0:64, 3, :], wstage[0:64, 1, :], wctx[0:64, 2, :].bitcast(F32),
                                        ALU.subtract).then_inc(wparts_ready, 1)
                nc.vector.memset(wctx[64:128, 3, :].bitcast(F32), 0.0).then_inc(wparts_ready, 1)

                def norm(b, k, stat_sem, var_sem, rstd_sem, ready):
                    carry()
                    nc.vector.bn_stats(stat[:, k, :], xs[:, b, :]).then_inc(stat_sem, 1)
                    dve.wait_ge(stat_sem, b + 1)
                    carry()
                    nc.vector.bn_aggr(mv[:, k, :], stat[:, k, :]).then_inc(var_sem, 1)

                def norm_apply(b, k, rstd_sem, ready):
                    dve.wait_ge(rstd_sem, b + 1)
                    nc.vector.tensor_scalar(xl[:, k, :], xs[:, b, :], mv[:, k, 0:1], rstd[:, k, :], ALU.subtract,
                                            ALU.mult).then_inc(ready, 1)

                def key_remainder(b, c):
                    bk, n = ring(f"k{c}", b - 1)
                    dve.wait_ge(k_hi, 2 * b + c + 1)
                    nc.vector.scalar_tensor_tensor(klo[:, c, :], bank(bk, MP), bk0s[:, c:c + 1], khi[:, c, :].bitcast(F32),
                                                   ALU.add, ALU.subtract).then_inc(ring_free[bk], 1)

                def bias_queries(b):
                    bk, n = ring("q", b - 1)
                    dve.wait_ge(ring_full[bk], n + 1)
                    nc.vector.tensor_tensor(qT[:], bank(bk, 2, S), bq0s[:].unsqueeze(2).broadcast_to([128, 2, S]),
                                            ALU.add).then_inc(ring_free[bk], 1)

                def step(b, p, attn, after, more):
                    t = b - 1

                    def drain_values(mc):
                        bk, n = ring(f"v{mc}", b)
                        dve.wait_ge(ring_full[bk], n + 1)
                        src = bank(bk, H0, D0)
                        if mc < 2:
                            nc.vector.tensor_tensor(v0[:, mc, :, 0:D0], src, bv0b[:].rearrange("p (h d) -> p h d", h=H0),
                                                    ALU.add).then_inc(ring_free[bk], 1)
                        else:
                            nc.vector.scalar_tensor_tensor(v0[:, mc, :, 0:D0], src, lastmask[:],
                                                           bv0m[:].rearrange("p (h d) -> p h d", h=H0), ALU.mult,
                                                           ALU.add).then_inc(ring_free[bk], 1)

                    def maxima(i):
                        bk, n = ring(f"s{i}", b)
                        dve.wait_ge(ring_full[bk], n + 1)
                        nc.vector.reduce_max(mx[:, i:i + 1], bank(bk, M, parts=S), AX.X).then_inc(ring_free[bk], 1)

                    def split(c):
                        for i in range(4):
                            bk, n = ring(f"s{8 * c + 4 + i}", b)
                            dve.wait_ge(ring_free[bk], n + 1)
                        nc.vector.tensor_copy(parts[:, c, 0:8], mx[:, 8 * c:8 * c + 8]).then_inc(parts_hi, 1)
                        dve.wait_ge(parts_hi, 2 * b + c + 1)
                        nc.vector.tensor_tensor(parts[:, c, 32:40], mx[:, 8 * c:8 * c + 8], parts[:, c, 0:8],
                                                ALU.subtract).then_inc(parts_ready, 1)

                    def spread(c):
                        dve.wait_ge(tail_full, tail(f"m{c}", t) + 1)
                        nc.vector.tensor_tensor(mxb[:, c, :, :],
                                                bank(7, S, parts=96, dt=BF16).unsqueeze(1).broadcast_to([96, 8, S]),
                                                partmask[:].unsqueeze(2).broadcast_to([96, 8, S]), ALU.mult).then_inc(tail_free, 1)

                    if attn:
                        drain_values(0)
                    if after:
                        dve.wait_ge(tail_full, tail("nat", t) + 1)
                        nat = bank(7, H0, 32, parts=S)
                        nc.vector.reciprocal(rden[:], nat[:, :, D0]).then_inc(rden_ready, 1)
                        dve.wait_ge(rden_ready, t + 1)
                        nc.vector.tensor_tensor(o[:, 0:D].rearrange("p (h d) -> p h d", h=H0), nat[:, :, 0:D0],
                                                rden[:].unsqueeze(2).broadcast_to([S, H0, D0]), ALU.mult).then_inc(tail_free, 1)
                    if attn:
                        drain_values(1)
                        drain_values(2)
                    if more:
                        norm(b + 1, 0, ln1_stat, ln1_var, ln1_rstd, xl1_ready)
                    if after:
                        dve.wait_ge(tail_full, tail("h", t) + 1)
                        nc.vector.tensor_tensor(h[:], bank(7, HID, parts=S), b1b[:], ALU.add).then_inc(tail_free, 1)
                    if more:
                        split_mix(dve, b + 1, ctx_hi, ctx_mix)
                        norm_apply(b + 1, 0, ln1_rstd, xl1_ready)
                    if attn:
                        bk, n = ring("prod", b)
                        dve.wait_ge(ring_full[bk], n + 1)
                        if isinstance(b, int) and b == 0:
                            nc.vector.tensor_copy(prod[:], bank(bk, 2, D)).then_inc(ring_free[bk], 1)
                        else:
                            nc.vector.tensor_tensor(prod[:], bank(bk, 2, D), prod[:], ALU.add).then_inc(ring_free[bk], 1)
                    if attn:
                        for i in range(4):
                            maxima(i)
                    if after:
                        dve.wait_ge(tail_full, tail("y", t) + 1)
                        dve.wait_ge(biased, t + 1)
                        nc.vector.scalar_tensor_tensor(xs[:, t, :], bank(7, D, parts=S), tgate[0:S, 0:1], xs[:, t, :],
                                                       ALU.mult, ALU.add).then_inc(tail_free, 1)
                        dve.wait_ge(tail_free, tail("y", t) + 1)
                        norm(t, 1, ln2_stat, ln2_var, ln2_rstd, xl2_ready)
                    if attn:
                        maxima(4)
                        maxima(5)
                    if after:
                        norm_apply(t, 1, ln2_rstd, xl2_ready)
                    if attn:
                        maxima(6)
                        maxima(7)
                    if more:
                        key_remainder(b + 1, 0)
                    if attn:
                        split(0)
                    if more:
                        key_remainder(b + 1, 1)
                    if attn:
                        maxima(8)
                        maxima(9)
                    if after:
                        dve.wait_ge(tail_full, tail("qf", t) + 1)
                        nc.vector.tensor_tensor(qall[:, :, bass.ts(t, S)], bank(7, 4, S), bqfs[:].unsqueeze(2).broadcast_to([128, 4, S]),
                                                ALU.add).then_inc(tail_free, 1)
                    if attn:
                        for i in range(10, 13):
                            maxima(i)
                        if more:
                            bias_queries(b + 1)
                        spread(0)
                        for i in range(13, 16):
                            maxima(i)
                        split(1)
                        spread(1)
                    if after:
                        dve.wait_ge(tail_free, tail("qf", t) + 1)
                        carry()
                        for c in range(4):
                            nc.vector.bn_stats(qstat[:, c, t, :], qall[:, c, bass.ts(t, S)]).then_inc(qstat_done, 1)

                split_mix(dve, 0, ctx_hi, ctx_mix)
                norm(0, 0, ln1_stat, ln1_var, ln1_rstd, xl1_ready)
                norm_apply(0, 0, ln1_rstd, xl1_ready)
                for c in range(2):
                    key_remainder(0, c)
                bias_queries(0)
                steps(dve, step)

            @block.tensor
            def _(pe):
                pe.wait_ge(loaded, NLOADED)
                pe.wait_ge(consts_ready, 6)
                pe.wait_ge(selected, 16)
                pe.wait_ge(wparts_ready, 5)

                def project(name, b, dst, pairs):
                    bk, n = ring(name, b)
                    need(pe, ring_free[bk], n)
                    for j in range(len(pairs)):
                        lhs, rhs = pairs[j]
                        last = nc.tensor.matmul(dst(bk), lhs, rhs, start=j == 0, stop=j == len(pairs) - 1)
                    last.then_inc(ring_full[bk], 1)

                def keys(b, c):
                    pe.wait_ge(ctx_lo, b + 1)
                    pe.wait_ge(ctx_mix, b + 1)
                    cols = slice(KEY0.start + 128 * c, KEY0.start + 128 * c + 128)
                    project(f"k{c}", b - 1, lambda k: bank(k, MP), [(wctx[:, w, cols], cparts[:, x, :]) for w, x in PASSES])

                def transpose_x(b):
                    bk, n = ring("xT", b - 1)
                    need(pe, ring_free[bk], n)
                    pe.wait_ge(xl1_ready, b + 1)
                    for k in range(2):
                        last = nc.tensor.transpose(bank(bk, 2, S)[:, k, :], xl[:, 0, 128 * k:128 * k + 128], ident[0:S, 0:S])
                    last.then_inc(ring_full[bk], 1)

                def queries(b):
                    xbk, xn = ring("xT", b - 1)
                    bk, n = ring("q", b - 1)
                    need(pe, ring_free[bk], n)
                    pe.wait_ge(ring_free[xbk], xn + 1)
                    for mo in range(2):
                        for k in range(2):
                            last = nc.tensor.matmul(bank(bk, 2, S)[:, mo, :], wq0[:, k, 128 * mo:128 * mo + 128], xT[:, k, :],
                                                    start=k == 0, stop=k == 1)
                    last.then_inc(ring_full[bk], 1)

                def step(b, p, attn, after, more):
                    t = b - 1

                    def open_tail(name):
                        need(pe, tail_free, tail(name, t))

                    def scores(*heads):
                        for i in heads:
                            bk, n = ring(f"s{i}", b)
                            need(pe, ring_free[bk], n)
                            c, hd = divmod(i, 8)
                            nc.tensor.matmul(bank(bk, MP, parts=S), qstack[:, p, c, hd // 2, hd % 2, :], kstack[:, p, c, hd // 2, :],
                                             start=True, stop=True).then_inc(ring_full[bk], 1)

                    def put_parts(c):
                        open_tail(f"m{c}")
                        pe.wait_ge(parts_ready, 2 * b + c + 1)
                        nc.tensor.transpose(bank(7, S, parts=96, dt=BF16), parts[:, c, :], identb[0:S, 0:S]).then_inc(tail_full, 1)

                    def tscores(i):
                        g, mc = divmod(i, 3)
                        c = g // 2
                        hs = slice(4 * (g % 2), 4 * (g % 2) + 4)
                        if mc == 0 and g % 2 == 0:
                            pe.wait_ge(tail_free, tail(f"m{c}", t) + 1)
                        k, n = stb(f"t{i}", b)
                        need(pe, st_free[k], n)
                        dst = bank(4 + k, 4 * S)
                        nc.tensor.matmul(dst, negones[:], mxb[:, c, hs, :].rearrange("p h s -> p (h s)"), start=True, stop=False)
                        for a in range(2):
                            q = 2 * (g % 2) + a
                            last = nc.tensor.matmul(dst[:, 2 * S * a:2 * S * a + 2 * S], kstack[:, p, c, q, chunk[mc]],
                                                    qstack[:, p, c, q, :, :].rearrange("p a s -> p (a s)"), start=False, stop=a == 1)
                        last.then_inc(st_full[k], 1)

                    def values(i):
                        g, mc = divmod(i, 3)
                        if i == 0:
                            need(pe, o_free, b)
                        k, n = stb(f"t{i}", b)
                        pe.wait_ge(st_free[k], n + 1)
                        for j in range(4):
                            last = nc.tensor.matmul(psum[32 * j:32 * j + 32, 6, g * S:(g + 1) * S], v0[:, mc, 4 * g + j, :],
                                                    prob[:, g % 2, mc, j, :], start=mc == 0, stop=mc == 2)
                        if i == 11:
                            last.then_inc(o_full, 1)

                    def values_of(mc):
                        project(f"v{mc}", b, lambda k: bank(k, D), [(cparts[:, x, chunk[mc]], wctx[:, w, VAL0]) for w, x in PASSES])

                    if attn:
                        values_of(0)
                    if after:
                        pe.wait_ge(o_free, t + 1)
                        open_tail("nat")
                        for g in range(4):
                            last = nc.tensor.transpose(bank(7, 4, 128, parts=S)[:, g, :], oTp[:, g, :], ident[:])
                        last.then_inc(tail_full, 1)
                    if attn:
                        values_of(1)
                        values_of(2)
                    if after:
                        open_tail("oT")
                        for k in range(2):
                            last = nc.tensor.transpose(bank(7, 2, S)[:, k, :], o[:, 128 * k:128 * k + 128], ident[0:S, 0:S])
                        last.then_inc(tail_full, 1)

                    def expert_product(mo):
                        bk, n = ring("prod", b)
                        if mo == 0:
                            pe.wait_ge(e_loaded, 32 * b + 32)
                            need(pe, ring_free[bk], n)
                        for k in range(4):
                            last = nc.tensor.matmul(bank(bk, 2, D)[:, mo, :], e1[:, k, 128 * mo:128 * mo + 128], e2[:, k, :],
                                                    start=k == 0, stop=k == 3)
                        if mo == 1:
                            last.then_inc(ring_full[bk], 1)

                    if attn:
                        expert_product(0)
                    if after:
                        open_tail("h")
                        for k in range(2):
                            last = nc.tensor.matmul(bank(7, HID, parts=S), oT[:, k, :], w1s[:, k, :], start=k == 0, stop=k == 1)
                        last.then_inc(tail_full, 1)
                    if attn:
                        expert_product(1)
                    if after:
                        open_tail("hT")
                        for k in range(4):
                            last = nc.tensor.transpose(bank(7, 4, S)[:, k, :], h[:, 128 * k:128 * k + 128], ident[0:S, 0:S])
                        last.then_inc(tail_full, 1)
                    if attn:
                        pe.wait_ge(kstack_loaded, 12 * 16 * (b + 1))
                        pe.wait_ge(qstack_loaded, 12 * 16 * (b + 1))
                        scores(0, 1, 2, 3)
                    if after:
                        open_tail("y")
                        for k in range(4):
                            last = nc.tensor.matmul(bank(7, D, parts=S), hT[:, k, :], w2s[:, k, :], start=k == 0, stop=k == 3)
                        last.then_inc(tail_full, 1)
                    if attn:
                        scores(4, 5, 6, 7)
                    if more:
                        keys(b + 1, 0)
                    if after:
                        pe.wait_ge(xl2_ready, t + 1)
                        open_tail("x2T")
                        for k in range(2):
                            last = nc.tensor.transpose(bank(7, 2, S)[:, k, :], xl[:, 1, 128 * k:128 * k + 128], ident[0:S, 0:S])
                        last.then_inc(tail_full, 1)
                    if more:
                        keys(b + 1, 1)
                    if attn:
                        scores(8, 9)
                    if after:
                        open_tail("qf")
                        for mo in range(4):
                            for k in range(2):
                                last = nc.tensor.matmul(bank(7, 4, S)[:, mo, :], wqf[:, k, 128 * mo:128 * mo + 128], xT2[:, k, :],
                                                        start=k == 0, stop=k == 1)
                        last.then_inc(tail_full, 1)
                    if attn:
                        scores(10, 11)
                    if more:
                        transpose_x(b + 1)
                    if after:
                        open_tail("down")
                        for k in range(2):
                            last = nc.tensor.matmul(bank(7, NEXP, parts=S), xT2[:, k, :], downs[:, k, :], start=k == 0, stop=k == 1)
                        last.then_inc(tail_full, 1)
                    if attn:
                        scores(12)
                    if more:
                        queries(b + 1)
                    if attn:
                        put_parts(0)
                        scores(13, 14, 15)
                        for mc in range(3):
                            bk, n = ring(f"v{mc}", b)
                            pe.wait_ge(ring_free[bk], n + 1)
                        for i in range(12):
                            if i == 4:
                                put_parts(1)
                            tscores(i)
                            if i >= 2:
                                values(i - 2)
                        values(10)
                        values(11)

                for c in range(2):
                    keys(0, c)
                transpose_x(0)
                queries(0)
                steps(pe, step)

        early.close()
        agg = sb("agg", [128, 4, 2]); mean = sb("mean", [128, 1]); dev = sb("dev", [128, 4]); spreads = sb("spreads", [128, 4])
        varq = sb("varq", [128, 1]); rstdq = sb("rstdq", [128, 1]); qscale = sb("qscale", [128, 1]); qshift = sb("qshift", [128, 1])
        keysq = sb("keysq", [128, NKEY]); keyn = sb("keyn", [128, 1]); keyr = sb("keyr", [128, 1])
        keyd = sb("keyd", [128, 128]); keyT = sb("keyT", [128, 128])
        ups = sb("ups", [128, 2, D]); wq1 = sb("wq1", [128, 2, HID]); wo1 = sb("wo1", [128, 4, D])
        weights_loaded = sem("weights_loaded"); agg_ready = sem("agg_ready"); mean_summed = sem("mean_summed"); bn_step = sem("bn_step")
        spread_summed = sem("spread_summed"); varq_ready = sem("varq_ready"); rstdq_ready = sem("rstdq_ready")
        rstdq_eps = sem("rstdq_eps"); keyn_ready = sem("keyn_ready"); keyr_ready = sem("keyr_ready"); keyd_ready = sem("keyd_ready")
        keyT_full = sem("keyT_full"); gelu_done = sem("gelu_done")

        with nc.Block() as block:
            @block.sync
            def _(sp):
                for w, src in ((ups, up), (wq1, Wq1), (wo1, Wo1)):
                    sp.dma_start(w[:], src.rearrange("(k p) n -> p k n", p=128)).then_inc(weights_loaded, 16)
                sp.wait_ge(weights_loaded, 3 * 16)

            @block.scalar
            def _(act):
                nc.scalar.activation(hidden[:], hidden[:], ACT.Gelu).then_inc(gelu_done, 1)
                act.wait_ge(gelu_done, 1)

            @block.tensor
            def _(pe):
                pe.wait_ge(agg_ready, 4)
                nc.tensor.matmul(bank(0, 4), samedim[:], agg[:, :, 0], start=True, stop=True).then_inc(mean_summed, 1)
                pe.wait_ge(bn_step, 4)
                nc.tensor.matmul(bank(1, 4), samedim[:], spreads[:], start=True, stop=True).then_inc(spread_summed, 1)
                pe.wait_ge(keyd_ready, 4)
                nc.tensor.transpose(bank(2, 128), keyd[:], ident[:]).then_inc(keyT_full, 1)

            @block.gpsimd
            def _(pool):
                pool.wait_ge(keyn_ready, 1)
                nc.gpsimd.tensor_tensor(keyr[:], keyn[:], half[:], ALU.pow).then_inc(keyr_ready, 1)
                pool.wait_ge(varq_ready, 1)
                nc.gpsimd.tensor_scalar(varq[:], varq[:], EPS, None, ALU.add).then_inc(rstdq_eps, 1)
                pool.wait_ge(rstdq_eps, 1)
                nc.gpsimd.tensor_tensor(rstdq[:], varq[:], half[:], ALU.pow).then_inc(rstdq_ready, 1)

            @block.vector
            def _(dve):
                done = [0]

                def then(instruction):
                    done[0] += 1
                    instruction.then_inc(bn_step, 1)
                    dve.wait_ge(bn_step, done[0])

                for c in range(4):
                    nc.vector.bn_aggr(agg[:, c, :], qstat[:, c, :, :].rearrange("p b s -> p (b s)")).then_inc(agg_ready, 1)
                dve.wait_ge(agg_ready, 4)
                dve.wait_ge(mean_summed, 1)
                then(nc.vector.reduce_sum(mean[:], bank(0, 4), AX.X))
                then(nc.vector.tensor_scalar(dev[:], agg[:, :, 0], mean[:], None, ALU.subtract))
                then(nc.vector.tensor_tensor(dev[:], dev[:], dev[:], ALU.mult))
                then(nc.vector.tensor_tensor(spreads[:], dev[:], agg[:, :, 1], ALU.add))
                then(nc.vector.tensor_tensor(keysq[:], keys[:], keys[:], ALU.mult))
                then(nc.vector.reduce_sum(keyn[:], keysq[:], AX.X))
                nc.vector.tensor_scalar(keyn[:], keyn[:], TINY, None, ALU.max).then_inc(keyn_ready, 1)
                then(nc.vector.memset(keyd[:], 0.0))
                dve.wait_ge(spread_summed, 1)
                nc.vector.reduce_sum(varq[:], bank(1, 4), AX.X).then_inc(varq_ready, 1)
                dve.wait_ge(keyr_ready, 1)
                for i in range(4):
                    q = slice(32 * i, 32 * i + 32)
                    nc.vector.tensor_scalar(keyd[q, q], keys[q, :], keyr[q, :], None, ALU.mult).then_inc(keyd_ready, 1)
                dve.wait_ge(rstdq_ready, 1)
                then(nc.vector.tensor_tensor(qscale[:], rstdq[:], gam[:], ALU.mult))
                then(nc.vector.tensor_tensor(mean[:], mean[:], qscale[:], ALU.mult))
                then(nc.vector.tensor_tensor(qshift[:], bet[:], mean[:], ALU.subtract))
                dve.wait_ge(keyT_full, 1)
                then(nc.vector.tensor_copy(keyT[:], bank(2, 128)))

        kT1 = sb("kT1", [128, 4, M]); v1 = sb("v1", [128, 3, H1, D1 + 1]); qz1 = sb("qz1", [128, 4, 2, S])
        rden1 = sb("rden1", [S, H1])
        qn = sb("qn", [128, 4, S]); qsq = sb("qsq", [128, 4, S]); n2s = sb("n2s", [S, 16]); rn = sb("rn", [S, 16])
        FILL, TAKEN = -10.0, 10.0
        score = sb("score", [S, 16, NKEY + TOP]); top8 = sb("top8", [S, 16, 8]); marked = sb("marked", [S, 16, NKEY + TOP])
        expo = sb("expo", [S, 16, NKEY]); kept = sb("kept", [S, 16, NKEY]); den = sb("den", [S, 16]); rdn = sb("rdn", [S, 16])
        prb = sb("prb", [S, 8, 2, NKEY]); outer = sb("outer", [S, 8, NEXP]); wt = sb("wt", [S, NEXP]); beyond = sb("beyond", [S, 1])
        gw = sb("gw", [S, NEXP]); gT = sb("gT", [128, 2, S])
        ctx3_loaded = sem("ctx3_loaded"); ctx3_hi = sem("ctx3_hi"); ctx3_lo = sem("ctx3_lo"); ctx3_mix = sem("ctx3_mix")
        masks_ready = sem("masks_ready"); v1_ones = sem("v1_ones"); stored = sem("stored")
        a_full = [sem(f"a_full{i}") for i in range(2)]
        a_free = [sem(f"a_free{i}") for i in range(2)]
        t_full = [sem(f"t_full{i}") for i in range(2)]
        t_free = [sem(f"t_free{i}") for i in range(2)]
        pv_full = [sem(f"pv_full{i}") for i in range(2)]
        pv_free = [sem(f"pv_free{i}") for i in range(2)]
        f_full = sem("f_full"); f_free = sem("f_free"); r_full = sem("r_full"); r_free = sem("r_free")
        ln3_stat = sem("ln3_stat"); ln3_var = sem("ln3_var"); ln3_eps = sem("ln3_eps"); ln3_rstd = sem("ln3_rstd"); xl3_ready = sem("xl3_ready")
        ln4_stat = sem("ln4_stat"); ln4_var = sem("ln4_var"); ln4_eps = sem("ln4_eps"); ln4_rstd = sem("ln4_rstd"); xl4_ready = sem("xl4_ready")
        hi3 = sem("parts_hi3"); parts3 = sem("parts_ready3"); biased3 = sem("biased3"); rden1_ready = sem("rden1_ready")
        qn_ready = sem("qn_ready"); qsq_ready = sem("qsq_ready"); rn_ready = sem("rn_ready"); expo_ready = sem("expo_ready")
        top_ready = sem("top_ready"); floor_set = sem("floor_set"); marked_ready = sem("marked_ready"); kept_ready = sem("kept_ready")
        den_ready = sem("den_ready"); rdn_ready = sem("rdn_ready"); prb_ready = sem("prb_ready"); outer_ready = sem("outer_ready")
        halved = sem("halved"); wt_ready = sem("wt_ready"); beyond_ready = sem("beyond_ready"); wt_whole = sem("wt_whole"); gw_ready = sem("gw_ready")

        A3 = {n: i for i, n in enumerate(["k0", "k1", "q", "k2", "k3", "v0", "v1", "v2"] + [f"s{i}" for i in range(H1)])}
        R3 = ["oT", "y", "x4T", "out", "m"]
        F3 = ["n2", "gT", "y2", "sc", "x3T"]

        def a3(name, b):
            return A3[name] % 2, b * (len(A3) // 2) + A3[name] // 2

        def f3(name, b):
            if not isinstance(b, int):
                return 7 + 5 * b + F3.index(name)
            uses = [(s, n) for s in range(-2, B) for n in F3 if (s < B - 2 if n in ("n2", "sc") else -1 <= s < B - 1)]
            return uses.index((b, name))

        def r3(name, t):
            return 1 + t * len(R3) + R3.index(name)

        def steps(eng, step):
            step(-2, False, False, False, True)
            step(-1, False, False, True, True)
            step(0, True, False, True, True)
            with eng.Fori(1, B - 2) as b:
                step(b, True, True, True, True)
            step(B - 2, True, True, True, False)
            step(B - 1, True, True, False, False)
            step(B, False, True, False, False)

        with nc.Block() as block:
            @block.sync
            def _(sp):
                def store(t):
                    sp.wait_ge(r_free, r3("out", t) + 1)
                    sp.dma_start(out[t], xs[:, t, :]).then_inc(stored, 16)

                load_context(sp, 0, ctx3_loaded)

                def next_context(b):
                    sp.wait_ge(ctx3_lo, b)
                    sp.wait_ge(ctx3_mix, b)
                    load_context(sp, b, ctx3_loaded)

                next_context(1)
                with sp.Fori(1, B - 1) as b:
                    next_context(b + 1)
                    store(b - 1)
                store(B - 2)
                store(B - 1)
                sp.wait_ge(stored, 16 * B)

            @block.gpsimd
            def _(pool):
                nc.gpsimd.memset(score[:], FILL).then_inc(masks_ready, 1)
                nc.gpsimd.memset(v1[:], 1.0).then_inc(v1_ones, 1)
                pool.wait_ge(v1_ones, 1)
                nc.gpsimd.affine_select(out=v1[:, 2, :, :].rearrange("p h d -> p (h d)"), in_=v1[:, 2, :, :].rearrange("p h d -> p (h d)"),
                                        compare_op=ALU.is_ge, fill=0.0, base=-OVERLAP, pattern=[[0, H1 * (D1 + 1)]],
                                        channel_multiplier=1).then_inc(masks_ready, 1)

                def root(b, k, var, eps_added, ready):
                    pool.wait_ge(var, b + 1)
                    nc.gpsimd.tensor_tensor(vare[:, k, :], mv[:, k, 1:2], eps[:], ALU.add).then_inc(eps_added, 1)
                    pool.wait_ge(eps_added, b + 1)
                    nc.gpsimd.tensor_tensor(rstd[:, k, :], vare[:, k, :], half[0:S, :], ALU.pow).then_inc(ready, 1)

                def step(b, attn, after, mix, choose):
                    t, m, f = b - 1, b + 1, b + 2
                    if choose:
                        pool.wait_ge(qn_ready, f + 1)
                        nc.gpsimd.tensor_tensor(qsq[:], qn[:], qn[:], ALU.mult).then_inc(qsq_ready, 1)
                    if attn:
                        pool.wait_ge(xl3_ready, b + 1)
                        nc.gpsimd.tensor_tensor(xs[:, b, :], xs[:, b, :], gbo[:], ALU.add).then_inc(biased3, 1)
                    if after:
                        root(t, 1, ln4_var, ln4_eps, ln4_rstd)
                    if choose:
                        pool.wait_ge(f_free, f3("n2", b) + 1)
                        nc.gpsimd.tensor_tensor(rn[:], n2s[:], half[0:S, :].broadcast_to([S, 16]), ALU.pow).then_inc(rn_ready, 1)
                    if mix:
                        root(m, 0, ln3_var, ln3_eps, ln3_rstd)
                    if mix:
                        split_lo(pool, b + 1, ctx3_hi, ctx3_lo)
                    if choose:
                        pool.wait_ge(outer_ready, f + 1)
                        nc.gpsimd.tensor_tensor(outer[:, 0:4, :], outer[:, 0:4, :], outer[:, 4:8, :], ALU.add).then_inc(halved, 1)
                        pool.wait_ge(halved, 2 * f + 1)
                        nc.gpsimd.tensor_tensor(outer[:, 0:2, :], outer[:, 0:2, :], outer[:, 2:4, :], ALU.add).then_inc(halved, 1)
                        pool.wait_ge(halved, 2 * f + 2)
                        nc.gpsimd.tensor_tensor(wt[:], outer[:, 0, :], outer[:, 1, :], ALU.add).then_inc(wt_ready, 1)

                steps(pool, step)

            @block.scalar
            def _(act):
                def drain(name, b, dst, src, func=ACT.Copy, **kw):
                    k, n = a3(name, b)
                    act.wait_ge(a_full[k], n + 1)
                    nc.scalar.activation(dst, src(k), func, **kw).then_inc(a_free[k], 1)

                def step(b, attn, after, mix, choose):
                    t, m, f = b - 1, b + 1, b + 2
                    if choose:
                        nc.scalar.activation(qn[:], qall[:, :, bass.ts(f, S)], ACT.Identity, scale=qscale[:],
                                             bias=qshift[:]).then_inc(qn_ready, 1)
                    if attn:
                        for c in range(2):
                            drain(f"k{c}", b, kT1[:, c, :], lambda k: bank(k, M))
                    if after:
                        act.wait_ge(r_full, r3("oT", t) + 1)
                        nc.scalar.activation(oT[:], bank(7, 4, S), ACT.Copy).then_inc(r_free, 1)
                    if attn:
                        for c in range(2, 4):
                            drain(f"k{c}", b, kT1[:, c, :], lambda k: bank(k, M))
                        act.wait_ge(masks_ready, 2)
                        for mc in range(2):
                            drain(f"v{mc}", b, v1[:, mc, :, 0:D1], lambda k: bank(k, H1, D1), ACT.Identity)
                    if mix:
                        act.wait_ge(f_full, f3("gT", b) + 1)
                        nc.scalar.activation(gT[:], bank(6, 2, S), ACT.Copy).then_inc(f_free, 1)
                    if attn:
                        drain("v2", b, v1[:, 2, :, 0:D1], lambda k: bank(k, H1, D1), ACT.Identity, scale=lastmask[:])
                    if mix:
                        split_hi(act, b + 1, ctx3_loaded, ctx3_hi)
                    if after:
                        act.wait_ge(r_full, r3("x4T", t) + 1)
                        nc.scalar.activation(xT2[:], bank(7, 2, S), ACT.Copy).then_inc(r_free, 1)

                    def probabilities(*chunks):
                        for i in chunks:
                            act.wait_ge(t_full[i % 2], 3 * b + i // 2 + 1)
                            nc.scalar.activation(prob[:, i // 3, i % 3, :, :], bank(2 + i % 2, 4, S), ACT.Exp,
                                                 scale=D1 ** -0.5).then_inc(t_free[i % 2], 1)

                    if attn:
                        probabilities(0, 1)
                    if mix:
                        act.wait_ge(f_full, f3("x3T", b) + 1)
                        nc.scalar.activation(xT[:], bank(6, 2, S), ACT.Copy).then_inc(f_free, 1)
                    if attn:
                        probabilities(2)
                    if choose:
                        act.wait_ge(f_free, f3("sc", b) + 1)
                        nc.scalar.activation(expo[:], score[:, :, 0:NKEY], ACT.Exp).then_inc(expo_ready, 1)
                    if attn:
                        probabilities(3, 4, 5)

                steps(act, step)

            @block.vector
            def _(dve):
                def carry():
                    nc.vector.memset(scratch[:], 0.0)

                dve.wait_ge(masks_ready, 2)

                def norm(b, k, stat_sem, var_sem):
                    carry()
                    nc.vector.bn_stats(stat[:, k, :], xs[:, b, :]).then_inc(stat_sem, 1)
                    dve.wait_ge(stat_sem, b + 1)
                    carry()
                    nc.vector.bn_aggr(mv[:, k, :], stat[:, k, :]).then_inc(var_sem, 1)

                def norm_apply(b, k, rstd_sem, ready):
                    dve.wait_ge(rstd_sem, b + 1)
                    nc.vector.tensor_scalar(xl[:, k, :], xs[:, b, :], mv[:, k, 0:1], rstd[:, k, :], ALU.subtract,
                                            ALU.mult).then_inc(ready, 1)

                def step(b, attn, after, mix, choose):
                    t, m, f = b - 1, b + 1, b + 2
                    if after:
                        for i in range(2):
                            dve.wait_ge(pv_full[i], t + 1)
                            src = bank(4 + i, 4, D1 + 1, parts=S)
                            nc.vector.reciprocal(rden1[:, 4 * i:4 * i + 4], src[:, :, D1]).then_inc(rden1_ready, 1)
                            dve.wait_ge(rden1_ready, 2 * t + i + 1)
                            nc.vector.tensor_tensor(o[:, D * i:D * i + D].rearrange("p (h d) -> p h d", h=4), src[:, :, 0:D1],
                                                    rden1[:, 4 * i:4 * i + 4].unsqueeze(2).broadcast_to([S, 4, D1]),
                                                    ALU.mult).then_inc(pv_free[i], 1)
                    if attn:
                        k, n = a3("q", b)
                        dve.wait_ge(a_full[k], n + 1)
                        nc.vector.tensor_tensor(qz1[:], bank(k, 4, S).unsqueeze(2).broadcast_to([128, 4, 2, S]),
                                                headmask1[:].unsqueeze(1).unsqueeze(3).broadcast_to([128, 4, 2, S]),
                                                ALU.mult).then_inc(a_free[k], 1)
                    if mix:
                        dve.wait_ge(beyond_ready, m + 1)
                        dve.wait_ge(wt_ready, m + 1)
                        nc.vector.tensor_tensor(wt[:, NEXP - 1:NEXP], wt[:, NEXP - 1:NEXP], beyond[:], ALU.add).then_inc(wt_whole, 1)
                        dve.wait_ge(wt_whole, m + 1)
                        nc.vector.tensor_tensor(gw[:], wt[:], hidden[:, m, :], ALU.mult).then_inc(gw_ready, 1)
                    if after:
                        dve.wait_ge(r_full, r3("y", t) + 1)
                        dve.wait_ge(biased3, t + 1)
                        nc.vector.scalar_tensor_tensor(xs[:, t, :], bank(7, D, parts=S), tgate[0:S, 1:2], xs[:, t, :], ALU.mult,
                                                       ALU.add).then_inc(r_free, 1)
                        dve.wait_ge(r_free, r3("y", t) + 1)
                        norm(t, 1, ln4_stat, ln4_var)
                    if choose:
                        dve.wait_ge(f_full, f3("n2", b) + 1)
                        nc.vector.tensor_scalar(n2s[:], bank(6, 16, parts=S), TINY, None, ALU.max).then_inc(f_free, 1)
                    if after:
                        norm_apply(t, 1, ln4_rstd, xl4_ready)

                    def maxima(*heads):
                        for i in heads:
                            k, n = a3(f"s{i}", b)
                            dve.wait_ge(a_full[k], n + 1)
                            nc.vector.reduce_max(mx[:, i:i + 1], bank(k, M, parts=S), AX.X).then_inc(a_free[k], 1)

                    if attn:
                        maxima(0, 1)
                    if mix:
                        dve.wait_ge(f_full, f3("y2", b) + 1)
                        nc.vector.scalar_tensor_tensor(xs[:, m, :], bank(6, D, parts=S), tgate[0:S, 2:3], xs[:, m, :], ALU.mult,
                                                       ALU.add).then_inc(f_free, 1)
                        dve.wait_ge(f_free, f3("y2", b) + 1)
                        norm(m, 0, ln3_stat, ln3_var)
                    if attn:
                        maxima(2, 3)
                    if mix:
                        norm_apply(m, 0, ln3_rstd, xl3_ready)
                    if after:
                        dve.wait_ge(r_full, r3("out", t) + 1)
                        nc.vector.scalar_tensor_tensor(xs[:, t, :], bank(7, D, parts=S), tgate[0:S, 3:4], xs[:, t, :], ALU.mult,
                                                       ALU.add).then_inc(r_free, 1)
                    if attn:
                        maxima(4, 5, 6, 7)
                        for i in (H1 - 2, H1 - 1):
                            k, n = a3(f"s{i}", b)
                            dve.wait_ge(a_free[k], n + 1)
                        nc.vector.tensor_copy(parts[:, 0, 0:8], mx[:, 0:8]).then_inc(hi3, 1)
                        dve.wait_ge(hi3, b + 1)
                        nc.vector.tensor_tensor(parts[:, 0, 32:40], mx[:, 0:8], parts[:, 0, 0:8], ALU.subtract).then_inc(parts3, 1)
                        dve.wait_ge(r_full, r3("m", t) + 1)
                        nc.vector.tensor_tensor(mxb[:, 0, :, :], bank(7, S, parts=96, dt=BF16).unsqueeze(1).broadcast_to([96, 8, S]),
                                                partmask[:].unsqueeze(2).broadcast_to([96, 8, S]), ALU.mult).then_inc(r_free, 1)
                    if mix:
                        split_mix(dve, b + 1, ctx3_hi, ctx3_mix)
                    if choose:
                        dve.wait_ge(f_full, f3("sc", b) + 1)
                        dve.wait_ge(rn_ready, f + 1)
                        nc.vector.tensor_tensor(score[:, :, 0:NKEY], bank(6, 16, NKEY, parts=S), rn[:].unsqueeze(2).broadcast_to([S, 16, NKEY]),
                                                ALU.mult).then_inc(f_free, 1)
                        dve.wait_ge(f_free, f3("sc", b) + 1)
                        carry()
                        for g in range(16):
                            nc.vector.max(top8[:, g, :], score[:, g, :]).then_inc(top_ready, 1)
                        dve.wait_ge(top_ready, 16 * f + 16)
                        nc.vector.memset(top8[:, :, TOP:8], FILL).then_inc(floor_set, 1)
                        dve.wait_ge(floor_set, f + 1)
                        carry()
                        for g in range(16):
                            nc.vector.match_replace(marked[:, g, :], top8[:, g, :], score[:, g, :], TAKEN).then_inc(marked_ready, 1)
                        dve.wait_ge(marked_ready, 16 * f + 16)
                        dve.wait_ge(expo_ready, f + 1)
                        nc.vector.scalar_tensor_tensor(kept[:], marked[:, :, 0:NKEY], TAKEN / 2, expo[:], ALU.is_ge,
                                                       ALU.mult).then_inc(kept_ready, 1)
                        dve.wait_ge(kept_ready, f + 1)
                        nc.vector.reduce_sum(den[:], kept[:], AX.X).then_inc(den_ready, 1)
                        dve.wait_ge(den_ready, f + 1)
                        nc.vector.reciprocal(rdn[:], den[:]).then_inc(rdn_ready, 1)
                        dve.wait_ge(rdn_ready, f + 1)
                        nc.vector.tensor_tensor(prb[:].rearrange("p h s k -> p (h s) k"), kept[:], rdn[:].unsqueeze(2).broadcast_to([S, 16, NKEY]),
                                                ALU.mult).then_inc(prb_ready, 1)
                        dve.wait_ge(prb_ready, f + 1)
                        nc.vector.tensor_tensor(outer[:].rearrange("p h (i j) -> p h i j", i=8),
                                                prb[:, :, 0, 0:8].unsqueeze(3).broadcast_to([S, 8, 8, NKEY]),
                                                prb[:, :, 1, :].unsqueeze(2).broadcast_to([S, 8, 8, NKEY]), ALU.mult).then_inc(outer_ready, 1)
                        nc.vector.reduce_sum(beyond[:], prb[:, :, 0, 8:NKEY], AX.XY).then_inc(beyond_ready, 1)

                steps(dve, step)

            @block.tensor
            def _(pe):
                def step(b, attn, after, mix, choose):
                    t, m, f = b - 1, b + 1, b + 2

                    def project(name, dst, pairs):
                        k, n = a3(name, b)
                        need(pe, a_free[k], n)
                        for j in range(len(pairs)):
                            last = nc.tensor.matmul(dst(k), pairs[j][0], pairs[j][1], start=j == 0, stop=j == len(pairs) - 1)
                        last.then_inc(a_full[k], 1)

                    def keys_of(c):
                        project(f"k{c}", lambda k: bank(k, MP), [(wctx[:, w, KEY1.start + 128 * c:KEY1.start + 128 * c + 128], cparts[:, x, :]) for w, x in PASSES])

                    def values_of(mc):
                        project(f"v{mc}", lambda k: bank(k, HID), [(cparts[:, x, chunk[mc]], wctx[:, w, VAL1]) for w, x in PASSES])

                    def tscores(*chunks):
                        for i in chunks:
                            g, mc = divmod(i, 3)
                            need(pe, t_free[i % 2], 3 * b + i // 2)
                            dst = bank(2 + i % 2, 4 * S)
                            nc.tensor.matmul(dst, negones[:], mxb[:, 0, 4 * g:4 * g + 4, :].rearrange("p h s -> p (h s)"), start=True,
                                             stop=False)
                            for c in range(2):
                                last = nc.tensor.matmul(dst[:, 2 * S * c:2 * S * c + 2 * S], kT1[:, 2 * g + c, chunk[mc]],
                                                        qz1[:, 2 * g + c, :, :].rearrange("p h s -> p (h s)"), start=False, stop=c == 1)
                            last.then_inc(t_full[i % 2], 1)

                    def attend(g):
                        need(pe, pv_free[g], b)
                        for i in (3 * g + 1, 3 * g + 2):
                            pe.wait_ge(t_free[i % 2], 3 * b + i // 2 + 1)
                        for j in range(4):
                            for mc in range(3):
                                last = nc.tensor.matmul(bank(4 + g, 4, D1 + 1, parts=S)[:, j, :], prob[:, g, mc, j, :],
                                                        v1[:, mc, 4 * g + j, :], start=mc == 0, stop=mc == 2)
                        last.then_inc(pv_full[g], 1)

                    def scores(*heads):
                        for i in heads:
                            k, n = a3(f"s{i}", b)
                            need(pe, a_free[k], n)
                            nc.tensor.matmul(bank(k, M, parts=S), qz1[:, i // 2, i % 2, :], kT1[:, i // 2, :], start=True,
                                             stop=True).then_inc(a_full[k], 1)

                    if attn:
                        pe.wait_ge(ctx3_lo, b + 1)
                        pe.wait_ge(ctx3_mix, b + 1)
                        keys_of(0)
                        keys_of(1)
                    if after:
                        need(pe, r_free, r3("oT", t))
                        for i in range(2):
                            pe.wait_ge(pv_free[i], t + 1)
                        for k in range(4):
                            last = nc.tensor.transpose(bank(7, 4, S)[:, k, :], o[:, 128 * k:128 * k + 128], ident[0:S, 0:S])
                        last.then_inc(r_full, 1)
                    if attn:
                        k, n = a3("q", b)
                        need(pe, a_free[k], n)
                        pe.wait_ge(f_free, f3("x3T", b - 1) + 1)
                        for mo in range(4):
                            for j in range(2):
                                last = nc.tensor.matmul(bank(k, 4, S)[:, mo, :], wq1[:, j, 128 * mo:128 * mo + 128], xT[:, j, :],
                                                        start=j == 0, stop=j == 1)
                        last.then_inc(a_full[k], 1)
                        keys_of(2)
                        keys_of(3)
                    if after:
                        need(pe, r_free, r3("y", t))
                        for k in range(4):
                            last = nc.tensor.matmul(bank(7, D, parts=S), oT[:, k, :], wo1[:, k, :], start=k == 0, stop=k == 3)
                        last.then_inc(r_full, 1)
                    if attn:
                        values_of(0)
                        values_of(1)
                    if choose:
                        need(pe, f_free, f3("n2", b))
                        pe.wait_ge(qsq_ready, f + 1)
                        for c in range(4):
                            last = nc.tensor.matmul(bank(6, 4, 4, parts=S)[:, c, :], qsq[:, c, :], ones4[:], start=True, stop=True)
                        last.then_inc(f_full, 1)
                    if mix:
                        need(pe, f_free, f3("gT", b))
                        pe.wait_ge(gw_ready, m + 1)
                        for k in range(2):
                            last = nc.tensor.transpose(bank(6, 2, S)[:, k, :], gw[:, 128 * k:128 * k + 128], ident[0:S, 0:S])
                        last.then_inc(f_full, 1)
                    if attn:
                        values_of(2)
                    if after:
                        need(pe, r_free, r3("x4T", t))
                        pe.wait_ge(xl4_ready, t + 1)
                        for k in range(2):
                            last = nc.tensor.transpose(bank(7, 2, S)[:, k, :], xl[:, 1, 128 * k:128 * k + 128], ident[0:S, 0:S])
                        last.then_inc(r_full, 1)
                    if attn:
                        for name in ("v0", "v1"):
                            k, n = a3(name, b)
                            pe.wait_ge(a_free[k], n + 1)
                        scores(0, 1)
                    if mix:
                        need(pe, f_free, f3("y2", b))
                        for k in range(2):
                            last = nc.tensor.matmul(bank(6, D, parts=S), gT[:, k, :], ups[:, k, :], start=k == 0, stop=k == 1)
                        last.then_inc(f_full, 1)
                    if attn:
                        scores(2, 3)
                    if after:
                        need(pe, r_free, r3("out", t))
                        for k in range(2):
                            last = nc.tensor.matmul(bank(7, D, parts=S), xT2[:, k, :], prod[:, k, :], start=k == 0, stop=k == 1)
                        last.then_inc(r_full, 1)
                    if attn:
                        scores(4, 5, 6, 7)
                    if choose:
                        need(pe, f_free, f3("sc", b))
                        for c in range(4):
                            last = nc.tensor.matmul(bank(6, 4, 128, parts=S)[:, c, :], qn[:, c, :], keyT[:], start=True, stop=True)
                        last.then_inc(f_full, 1)
                    if attn:
                        need(pe, r_free, r3("m", t))
                        pe.wait_ge(parts3, b + 1)
                        nc.tensor.transpose(bank(7, S, parts=96, dt=BF16), parts[:, 0, :], identb[0:S, 0:S]).then_inc(r_full, 1)
                        pe.wait_ge(r_free, r3("m", t) + 1)
                        tscores(0, 1)
                    if mix:
                        pe.wait_ge(xl3_ready, m + 1)
                        need(pe, f_free, f3("x3T", b))
                        for k in range(2):
                            last = nc.tensor.transpose(bank(6, 2, S)[:, k, :], xl[:, 0, 128 * k:128 * k + 128], ident[0:S, 0:S])
                        last.then_inc(f_full, 1)
                    if attn:
                        tscores(2, 3, 4, 5)
                        attend(0)
                        attend(1)

                steps(pe, step)



_INS = ["x", "ctxT", "g_xattn", "g_ffn", "L0_xattn_Wq", "L0_xattn_bq", "L0_xattn_Wk", "L0_xattn_bk", "L0_xattn_Wv", "L0_xattn_bv",
        "L0_xattn_W1", "L0_xattn_b1", "L0_xattn_W2", "L0_xattn_b2", "L0_ffn_Wq", "L0_ffn_bq", "L0_ffn_bn_gamma", "L0_ffn_bn_beta",
        "L0_ffn_sub_key0", "L0_ffn_sub_key1", "downT", "L0_ffn_expert_up", "L1_xattn_Wq", "L1_xattn_Wk", "L1_xattn_Wv",
        "L1_xattn_Wo", "L1_xattn_bo", "w1T", "w2"]


def kernel(**inputs):
    import numpy as _np
    import concourse.bacc as _bacc
    from concourse import mybir as _mybir
    from concourse.bass_utils import run_bass_kernel_spmd as _run

    laid = {n: _np.asarray(a) for n, a in inputs.items()}
    laid["ctxT"] = laid["ctx_768"].transpose(0, 2, 1)
    for n, k in (("L0_xattn_bq", 2), ("L0_xattn_bk", 2), ("L0_ffn_bq", 4)):
        laid[n] = laid[n].reshape(k, 128).T
    laid["downT"] = laid["L0_ffn_expert_down"].T
    laid["w1T"] = laid["L1_ffn_w1"].transpose(0, 2, 1).reshape(B, 128, 4, D)
    laid["w2"] = laid["L1_ffn_w2"].reshape(B, 128, 4, D)

    nc = _bacc.Bacc("TRN2", target_bir_lowering=False, num_devices=1)
    arrays, args = {}, []
    for name in _INS:
        a = _np.ascontiguousarray(laid[name])
        arrays[f"in_{name}"] = a
        args.append(nc.dram_tensor(f"in_{name}", a.shape, _mybir.dt.from_np(a.dtype), kind="ExternalInput").ap())
    args.append(nc.dram_tensor("out_0", (B, S, D), _mybir.dt.float32, kind="ExternalOutput").ap())
    program(nc, *args)
    r = _run(nc, [arrays], core_ids=[0])
    return r.results[0]["out_0"]
```

```python
from contextlib import ExitStack

import concourse.bass as bass
from concourse import mybir

F32 = mybir.dt.float32
BF16 = mybir.dt.bfloat16
F32R = mybir.dt.float32r
ALU = mybir.AluOpType
ACT = mybir.ActivationFunctionType
AX = mybir.AxisListType

B, S, D = 16, 100, 256
M, DC = 361, 192
DT = DC - 128
MP = M + 1
KEY0, VAL0, KEY1, VAL1 = (slice(0, 256), slice(256, 512), slice(512, 1024), slice(1024, 1536))
H0, D0 = 16, 16
H1, D1 = 8, 64
HID = 512
MSTART = [0, 128, M - 128]
OVERLAP = 2 * 128 - MSTART[2]
TOP, NKEY, NEXP = 4, 32, 256
WK = B * 4
EPS = 1e-5
TINY = 1e-24


def program(nc, x, ctxT, g_xattn, g_ffn, Wq0, bq0, Wk0, bk0, Wv0, bv0, W1, b1, W2, b2, Wqf, bqf, gamma, beta,
            key0, key1, downT, up, Wq1, Wk1, Wv1, Wo1, bo1, w1T, w2, out):
    with ExitStack() as stack:
        def sb(name, shape, dt=F32):
            return stack.enter_context(nc.sbuf_tensor(name, shape, dt))

        def sem(name):
            return stack.enter_context(nc.semaphore(name))

        psum = stack.enter_context(nc.psum_tensor("psum", [128, 8, 512], F32))

        def bank(n, *dims, parts=128, dt=F32):
            size = 1
            for d in dims:
                size *= d
            ap = psum[0:parts, n, 0:size] if dt == F32 else psum[0:parts, n, :].bitcast(dt)[:, 0:size]
            if len(dims) == 1:
                return ap
            names = " ".join("abc"[:len(dims)])
            return ap.rearrange(f"p ({names}) -> p {names}", **{n: d for n, d in zip("abc", dims)})

        wctx = sb("wctx", [128, 4, 1536], F32R)
        bq0s = sb("bq0s", [128, 2]); bk0s = sb("bk0s", [128, 2]); bqfs = sb("bqfs", [128, 4])
        bv0b = sb("bv0b", [128, D]); bv0m = sb("bv0m", [128, D])
        b1b = sb("b1b", [S, HID]); b2b = sb("b2b", [S, D]); bo1b = sb("bo1b", [S, D])
        gb2 = sb("gb2", [S, D]); gbo = sb("gbo", [S, D])
        gate = sb("gate", [128, 4]); tgate = sb("tgate", [128, 4])
        gam = sb("gam", [128, 1]); bet = sb("bet", [128, 1])
        keys = sb("keys", [128, NKEY])
        ident = sb("ident", [128, 128]); identb = sb("identb", [128, 128], BF16)
        negones = sb("negones", [96, 128], BF16)
        partmask = sb("partmask", [96, 8])
        quads = sb("quads", [128, 4, 2]); pairmask = sb("pairmask", [128, 2])
        negupper = sb("negupper", [128, 1])
        headmask1 = sb("headmask1", [128, 2])
        ones4 = sb("ones4", [128, 4])
        lastmask = sb("lastmask", [128, 1])
        samedim = sb("samedim", [128, 128])
        half = sb("half", [128, 1])
        eps = sb("eps", [S, 1]); scratch = sb("scratch", [1, 1])
        xs = sb("xs", [S, B, D])
        hidden = sb("hidden", [S, B, NEXP])
        qall = sb("qall", [128, 4, B * S])
        qstat = sb("qstat", [128, 4, B, 6])
        prod = sb("prod", [128, 2, D])
        ctx = sb("ctx", [128, 2, MP])
        cparts = sb("cparts", [128, 4, MP], F32R)
        stat = sb("stat", [S, 2, 6]); mv = sb("mv", [S, 2, 2]); rstd = sb("rstd", [S, 2, 1]); vare = sb("vare", [S, 2, 1])
        xl = sb("xl", [S, 2, D]); xT = sb("xT", [128, 2, S]); xT2 = sb("xT2", [128, 2, S])
        mx = sb("mx", [S, H0]); parts = sb("parts", [S, 2, 96], BF16); mxb = sb("mxb", [96, 2, 8, S], BF16)
        oTp = sb("oTp", [128, 4, S]); rden = sb("rden", [S, H0]); o = sb("o", [S, HID]); oT = sb("oT", [128, 4, S])
        early = stack.enter_context(ExitStack())

        def sb1(name, shape, dt=F32):
            return early.enter_context(nc.sbuf_tensor(name, shape, dt))

        wq0 = sb1("wq0", [128, 2, D])
        w1s = sb1("w1s", [128, 2, HID]); w2s = sb1("w2s", [128, 4, D]); wqf = sb1("wqf", [128, 2, HID])
        downs = sb1("downs", [128, 2, NEXP])
        e1 = sb1("e1", [128, 4, D]); e2 = sb1("e2", [128, 4, D])
        qT = sb1("qT", [128, 2, S]); qm = sb1("qm", [128, 2, 2, S])
        qhi = sb1("qhi", [128, 2, 2, S], F32R); qlo = sb1("qlo", [128, 2, 2, S], F32R)
        khi = sb1("khi", [128, 2, MP], F32R); klo = sb1("klo", [128, 2, MP], F32R)
        qstack = sb1("qstack", [96, 2, 2, 4, 2, S], F32R); kstack = sb1("kstack", [96, 2, 2, 4, MP], F32R)
        v0 = sb1("v0", [128, 3, H0, 32])
        prob = sb1("prob", [128, 2, 3, 4, S])
        h = sb1("h", [S, HID]); hT = sb1("hT", [128, 4, S])
        first_loaded = sem("first_loaded"); loaded = sem("loaded"); x_loaded = sem("x_loaded"); ctx_loaded = sem("ctx_loaded"); e_loaded = sem("e_loaded")
        late_loaded = sem("late_loaded"); mlp_loaded = sem("mlp_loaded"); rest_loaded = sem("rest_loaded")
        zeroed = sem("zeroed"); selected = sem("selected"); gates_ready = sem("gates_ready"); consts_ready = sem("consts_ready")
        ring_full = [sem(f"ring_full{i}") for i in range(4)]
        ring_free = [sem(f"ring_free{i}") for i in range(4)]
        st_full = [sem(f"st_full{i}") for i in range(2)]
        st_free = [sem(f"st_free{i}") for i in range(2)]
        o_full = sem("o_full"); o_free = sem("o_free")
        tail_full = sem("tail_full"); tail_free = sem("tail_free")
        ln1_stat = sem("ln1_stat"); ln1_var = sem("ln1_var"); ln1_eps = sem("ln1_eps"); ln1_rstd = sem("ln1_rstd"); xl1_ready = sem("xl1_ready")
        ln2_stat = sem("ln2_stat"); ln2_var = sem("ln2_var"); ln2_eps = sem("ln2_eps"); ln2_rstd = sem("ln2_rstd"); xl2_ready = sem("xl2_ready")
        q_masked = sem("q_masked"); q_hi = sem("q_hi"); q_lo = sem("q_lo"); k_hi = sem("k_hi")
        stack_loaded = [sem(f"stack_loaded{q}") for q in range(4)]; padded = sem("padded")
        wparts_ready = sem("wparts_ready"); wstage_loaded = [sem(f"wstage_loaded{i}") for i in range(2)]; halves = sem("halves")
        ctx_hi = sem("ctx_hi"); ctx_lo = sem("ctx_lo"); ctx_mix = sem("ctx_mix")
        biased = sem("biased"); parts_hi = sem("parts_hi"); parts_ready = sem("parts_ready")
        rden_ready = sem("rden_ready"); qstat_done = sem("qstat_done"); mul_done = sem("mul_done")

        def need(eng, s, value):
            if not isinstance(value, int) or value > 0:
                eng.wait_ge(s, value)

        NEXT = ["k0", "k1", "xT", "q"]
        RING = ["v0", "v1", "v2", "prod", "s0", "s1", "s2", "k0", "s3", "s4", "s5", "xT", "s6", "s7", "k1", "q", "s8", "s9", "s10",
                "s11", "s12", "s13", "s14", "s15"]
        ST = ["m0"] + [f"t{i}" for i in range(6)] + ["m1"] + [f"t{i}" for i in range(6, 12)]
        TAIL = ["nat", "oT", "h", "hT", "y", "x2T", "down", "qf"]

        def ring(name, b):
            if isinstance(b, int) and b < 0:
                return NEXT.index(name), 0
            order = RING if not isinstance(b, int) or b < B - 1 else [n for n in RING if n not in NEXT]
            i = order.index(name)
            return i % 4, b * (len(RING) // 4) + i // 4 + 1

        def stb(name, b):
            i = ST.index(name)
            return i % 2, b * (len(ST) // 2) + i // 2

        def tail(name, t):
            return t * len(TAIL) + TAIL.index(name)

        def steps(eng, step):
            step(0, 0, True, False, True)
            with eng.Fori(0, (B - 2) // 2) as i:
                step(i * 2 + 1, 1, True, True, True)
                step(i * 2 + 2, 0, True, True, True)
            step(B - 1, 1, True, True, False)
            step(B, 0, False, True, False)

        chunk = [slice(m, m + 128) for m in MSTART]

        PASSES = [(0, 0), (0, 1), (1, 0), (2, 2), (3, 3)]

        def split_hi(act, n, loaded_sem, hi):
            act.wait_ge(loaded_sem, 48 * n + 48)
            nc.scalar.activation(cparts[:, 0, :], ctx[:, 0, :], ACT.Identity).then_inc(hi, 1)
            nc.scalar.activation(cparts[:, 3, :], ctx[:, 1, :], ACT.Identity).then_inc(hi, 1)

        def split_lo(pool, n, hi, lo):
            pool.wait_ge(hi, 2 * n + 2)
            nc.gpsimd.tensor_tensor(cparts[:, 1, :], ctx[:, 0, :], cparts[:, 0, :].bitcast(F32), ALU.subtract).then_inc(lo, 1)

        def split_mix(dve, n, hi, mix):
            dve.wait_ge(hi, 2 * n + 2)
            nc.vector.scalar_tensor_tensor(cparts[:, 2, :], cparts[:, 3, :].bitcast(F32), negupper[:], ctx[:, 1, :], ALU.mult,
                                           ALU.add).then_inc(mix, 1)

        def load_context(eng, b, done):
            eng.dma_start(ctx[:, 0, 0:M], ctxT[b, 0:128, :]).then_inc(done, 16)
            for i in range(2):
                eng.dma_start(ctx[64 * i:64 * i + 64, 1, 0:M], ctxT[b, 128:DC, :]).then_inc(done, 16)

        wstage = qall[:].rearrange("p c n -> p (c n)")[:, 0:2 * 1536].rearrange("p (k n) -> p k n", k=2)

        with nc.Block() as block:
            @block.sync
            def _(sp):
                sp.dma_start(xs[:, 0:2, :], x[0:2].rearrange("b s d -> s b d")).then_inc(x_loaded, 16)

                def load_experts(b):
                    sp.dma_start(e1[:], w1T[b]).then_inc(e_loaded, 16)
                    sp.dma_start(e2[:], w2[b]).then_inc(e_loaded, 16)

                def load_context_weights(stage, *weights):
                    for cols, w in weights:
                        sp.dma_start(wstage[:, 0, cols], w[0:128, :]).then_inc(wstage_loaded[stage], 16)
                        for i in range(2):
                            sp.dma_start(wstage[64 * i:64 * i + 64, 1, cols], w[128:DC, :]).then_inc(wstage_loaded[stage], 16)

                sp.dma_start(wq0[:], Wq0.rearrange("(k p) n -> p k n", p=128)).then_inc(first_loaded, 16)
                sp.dma_start(bq0s[:], bq0).then_inc(first_loaded, 16)
                sp.dma_start(bk0s[:], bk0).then_inc(first_loaded, 16)
                load_context_weights(0, (KEY0, Wk0), (VAL0, Wv0))
                load_context(sp, 0, ctx_loaded)
                sp.dma_start(gate[:, 0:2], g_xattn.partition_broadcast(128)).then_inc(loaded, 16)
                sp.dma_start(gate[:, 2:4], g_ffn.partition_broadcast(128)).then_inc(loaded, 16)
                sp.dma_start(bv0b[:], bv0.partition_broadcast(128)).then_inc(loaded, 16)
                sp.dma_start(b2b[:], b2.partition_broadcast(S)).then_inc(loaded, 16)
                sp.dma_start(bo1b[:], bo1.partition_broadcast(S)).then_inc(loaded, 16)
                load_experts(0)

                def load_stacks(b, p):
                    bk, n = ring("k1", b - 1)
                    sp.wait_ge(ring_free[bk], n + 1)
                    for q in range(4):
                        for a, part in enumerate((khi, khi, klo)):
                            sp.dma_start(kstack[32 * a:32 * a + 32, p, :, q, :].bitcast(F32),
                                         part[32 * q:32 * q + 32, :, :].bitcast(F32)).then_inc(stack_loaded[q], 16)
                    sp.wait_ge(q_lo, b + 1)
                    for q in range(4):
                        for a, part in enumerate((qhi, qlo, qhi)):
                            sp.dma_start(qstack[32 * a:32 * a + 32, p, :, q, :, :].bitcast(F32),
                                         part[32 * q:32 * q + 32, :, :, :].bitcast(F32)).then_inc(stack_loaded[q], 16)

                def next_context(b):
                    sp.wait_ge(ctx_lo, b)
                    sp.wait_ge(ctx_mix, b)
                    load_context(sp, b, ctx_loaded)

                def step(b, p, two_more):
                    bk, n = ring("prod", b)
                    sp.wait_ge(ring_full[bk], n + 1)
                    load_experts(b + 1)
                    if two_more:
                        next_context(b + 2)
                    load_stacks(b + 1, 1 - p)

                next_context(1)
                load_stacks(0, 0)
                load_context_weights(1, (KEY1, Wk1), (VAL1, Wv1))
                sp.dma_start(b1b[:], b1.partition_broadcast(S)).then_inc(mlp_loaded, 16)
                sp.dma_start(bqfs[:], bqf).then_inc(mlp_loaded, 16)
                sp.dma_start(w1s[:], W1.rearrange("(k p) n -> p k n", p=128)).then_inc(mlp_loaded, 16)
                sp.dma_start(w2s[:], W2.rearrange("(k p) n -> p k n", p=128)).then_inc(mlp_loaded, 16)
                sp.dma_start(downs[:], downT.rearrange("(k p) n -> p k n", p=128)).then_inc(mlp_loaded, 16)
                sp.dma_start(wqf[:], Wqf.rearrange("(k p) n -> p k n", p=128)).then_inc(mlp_loaded, 16)
                sp.dma_start(xs[:, 2:B, :], x[2:B].rearrange("b s d -> s b d")).then_inc(rest_loaded, 16)
                for i in range(4):
                    sp.dma_start(keys[32 * i:32 * i + 32, :], (key0, key1)[i % 2]).then_inc(late_loaded, 16)
                for i in range(2):
                    sp.dma_start(gam[64 * i:64 * i + 64, :], gamma.rearrange("(p a) -> p a", a=1)).then_inc(late_loaded, 16)
                    sp.dma_start(bet[64 * i:64 * i + 64, :], beta.rearrange("(p a) -> p a", a=1)).then_inc(late_loaded, 16)
                with sp.Fori(0, (B - 2) // 2) as i:
                    step(i * 2, 0, True)
                    step(i * 2 + 1, 1, True)
                step(B - 2, 0, False)
                sp.wait_ge(late_loaded, 8 * 16)
            NFIRST, NLOADED, NMLP = 3 * 16, 5 * 16, 6 * 16
            STAGES = [slice(0, 512), slice(512, 1536)]

            @block.gpsimd
            def _(pool):
                for t in (ident, identb, samedim, parts, partmask):
                    nc.gpsimd.memset(t[:], 0.0).then_inc(zeroed, 1)
                for t in (quads, ones4, lastmask, v0):
                    nc.gpsimd.memset(t[:], 1.0).then_inc(zeroed, 1)
                nc.gpsimd.memset(headmask1[:], D1 ** -0.5).then_inc(zeroed, 1)
                nc.gpsimd.memset(ctx[:, :, M:MP], 0.0).then_inc(padded, 1)
                nc.gpsimd.memset(negupper[:], -1.0).then_inc(zeroed, 1)
                nc.gpsimd.memset(negones[:], -1.0).then_inc(consts_ready, 1)
                nc.gpsimd.memset(half[:], -0.5).then_inc(consts_ready, 1)
                nc.gpsimd.memset(eps[:], EPS).then_inc(consts_ready, 1)
                pool.wait_ge(zeroed, 11)

                done = [0]

                def select(ap, pattern, base, op, fill, cm=1):
                    done[0] += 1
                    nc.gpsimd.affine_select(out=ap, in_=ap, compare_op=op, fill=fill, base=base, pattern=pattern,
                                            channel_multiplier=cm).then_inc(selected, 1)
                    pool.wait_ge(selected, done[0])

                for t in (ident, identb):
                    select(t[:], [[-1, 128]], 0, ALU.not_equal, 1.0)
                for off in (0, 64, -64):
                    select(samedim[:], [[-1, 128]], off, ALU.not_equal, 1.0 / 8)
                for off in (0, -32):
                    select(partmask[:], [[-1, 8]], off, ALU.not_equal, 1.0)
                for t, n in ((headmask1, 2), (ones4, 4)):
                    select(t[:], [[-128 // n, n]], 0, ALU.is_ge, 0.0)
                    select(t[:], [[128 // n, n]], 128 // n - 1, ALU.is_ge, 0.0, cm=-1)
                select(quads[:], [[-32, 4], [-16, 2]], 0, ALU.is_ge, 0.0)
                select(quads[:], [[32, 4], [16, 2]], 15, ALU.is_ge, 0.0, cm=-1)
                for i in range(2):
                    nc.gpsimd.tensor_tensor(quads[:, i, :], quads[:, i, :], quads[:, i + 2, :], ALU.add).then_inc(halves, 1)
                pool.wait_ge(halves, 2)
                nc.gpsimd.tensor_tensor(pairmask[:], quads[:, 0, :], quads[:, 1, :], ALU.add).then_inc(halves, 1)
                pool.wait_ge(halves, 3)
                select(negupper[:], [[0, 1]], -64, ALU.is_ge, 0.0)
                select(lastmask[:], [[0, 1]], -OVERLAP, ALU.is_ge, 0.0)
                select(v0[:, 2, :, :].rearrange("p h d -> p (h d)"), [[0, H0 * 32]], -OVERLAP, ALU.is_ge, 0.0)
                def root1(b):
                    pool.wait_ge(ln1_var, b + 1)
                    nc.gpsimd.tensor_tensor(vare[:, 0, :], mv[:, 0, 1:2], eps[:], ALU.add).then_inc(ln1_eps, 1)
                    pool.wait_ge(ln1_eps, b + 1)
                    nc.gpsimd.tensor_tensor(rstd[:, 0, :], vare[:, 0, :], half[0:S, :], ALU.pow).then_inc(ln1_rstd, 1)

                def bias_residual(b):
                    pool.wait_ge(xl1_ready, b + 1)
                    nc.gpsimd.tensor_tensor(xs[:, b, :], xs[:, b, :], gb2[:], ALU.add).then_inc(biased, 1)

                def mask_queries(b):
                    bk, n = ring("q", b - 1)
                    pool.wait_ge(ring_free[bk], n + 1)
                    nc.gpsimd.tensor_tensor(
                        qm[:], qT[:].unsqueeze(2).broadcast_to([128, 2, 2, S]),
                        pairmask[:].unsqueeze(1).unsqueeze(3).broadcast_to([128, 2, 2, S]), ALU.mult).then_inc(q_masked, 1)
                    pool.wait_ge(q_hi, b + 1)
                    nc.gpsimd.tensor_tensor(qlo[:], qm[:], qhi[:].bitcast(F32), ALU.subtract).then_inc(q_lo, 1)

                def step(b, p, attn, after, more):
                    if more:
                        root1(b + 1)
                        split_lo(pool, b + 1, ctx_hi, ctx_lo)
                    if after:
                        t = b - 1
                        pool.wait_ge(ln2_var, t + 1)
                        nc.gpsimd.tensor_tensor(vare[:, 1, :], mv[:, 1, 1:2], eps[:], ALU.add).then_inc(ln2_eps, 1)
                        pool.wait_ge(ln2_eps, t + 1)
                        nc.gpsimd.tensor_tensor(rstd[:, 1, :], vare[:, 1, :], half[0:S, :], ALU.pow).then_inc(ln2_rstd, 1)
                    if more:
                        bias_residual(b + 1)
                        mask_queries(b + 1)

                split_lo(pool, 0, ctx_hi, ctx_lo)
                root1(0)
                mask_queries(0)
                pool.wait_ge(loaded, NLOADED)
                pool.wait_ge(gates_ready, 1)
                nc.gpsimd.tensor_scalar(gb2[:], b2b[:], tgate[0:S, 0:1], None, ALU.mult).then_inc(consts_ready, 1)
                nc.gpsimd.tensor_scalar(gbo[:], bo1b[:], tgate[0:S, 1:2], None, ALU.mult).then_inc(consts_ready, 1)
                nc.gpsimd.tensor_scalar(bv0m[:], bv0b[:], lastmask[:], None, ALU.mult).then_inc(consts_ready, 1)
                pool.wait_ge(consts_ready, 6)
                bias_residual(0)
                steps(pool, step)

            @block.scalar
            def _(act):
                def round_weights(stage):
                    cols = STAGES[stage]
                    act.wait_ge(wstage_loaded[stage], 6 * 16)
                    nc.scalar.activation(wctx[:, 0, cols], wstage[:, 0, cols], ACT.Identity).then_inc(wparts_ready, 1)
                    nc.scalar.activation(wctx[:, 2, cols], wstage[:, 1, cols], ACT.Identity).then_inc(wparts_ready, 1)

                round_weights(0)
                act.wait_ge(padded, 1)

                def drain_tail(name, b, dst, src, func=ACT.Copy):
                    act.wait_ge(tail_full, tail(name, b) + 1)
                    nc.scalar.activation(dst, src, func).then_inc(tail_free, 1)

                def round_keys(b, c):
                    bk, n = ring(f"k{c}", b - 1)
                    act.wait_ge(ring_full[bk], n + 1)
                    nc.scalar.activation(khi[:, c, :], bank(bk, MP), ACT.Identity, bias=bk0s[:, c:c + 1]).then_inc(k_hi, 1)

                def drain_xT(b):
                    bk, n = ring("xT", b - 1)
                    act.wait_ge(ring_full[bk], n + 1)
                    nc.scalar.activation(xT[:], bank(bk, 2, S), ACT.Copy).then_inc(ring_free[bk], 1)

                def round_queries(b):
                    act.wait_ge(q_masked, b + 1)
                    nc.scalar.activation(qhi[:], qm[:], ACT.Identity).then_inc(q_hi, 1)

                def step(b, p, attn, after, more):
                    t = b - 1
                    if after:
                        drain_tail("oT", t, oT[:, 0:2, :], bank(7, 2, S))
                    if more:
                        bk, n = ring("v2", b)
                        act.wait_ge(ring_full[bk], n + 1)
                        split_hi(act, b + 1, ctx_loaded, ctx_hi)
                    if after:
                        drain_tail("hT", t, hT[:], bank(7, 4, S), ACT.Relu)
                    if more:
                        round_keys(b + 1, 0)
                        drain_xT(b + 1)
                        round_keys(b + 1, 1)
                    if after:
                        drain_tail("x2T", t, xT2[:], bank(7, 2, S))
                        drain_tail("down", t, hidden[:, t, :], bank(7, NEXP, parts=S))
                    def exponentials(*chunks):
                        for i in chunks:
                            sb_, n = stb(f"t{i}", b)
                            act.wait_ge(st_full[sb_], n + 1)
                            nc.scalar.activation(prob[:, i // 3 % 2, i % 3, :, :], bank(4 + sb_, 4, S), ACT.Exp,
                                                 scale=D0 ** -0.5).then_inc(st_free[sb_], 1)

                    if attn:
                        exponentials(0, 1)
                    if more:
                        round_queries(b + 1)
                    if attn:
                        exponentials(*range(2, 12))
                        act.wait_ge(o_full, b + 1)
                        nc.scalar.activation(oTp[:], bank(6, 4, S), ACT.Copy).then_inc(o_free, 1)
                    if isinstance(b, int) and b == 0:
                        round_weights(1)

                split_hi(act, 0, ctx_loaded, ctx_hi)
                act.wait_ge(first_loaded, NFIRST)
                for c in range(2):
                    round_keys(0, c)
                drain_xT(0)
                round_queries(0)
                act.wait_ge(loaded, NLOADED)
                nc.scalar.activation(tgate[:], gate[:], ACT.Tanh).then_inc(gates_ready, 1)
                steps(act, step)

            @block.vector
            def _(dve):
                def carry():
                    nc.vector.memset(scratch[:], 0.0)

                dve.wait_ge(x_loaded, 16)
                dve.wait_ge(consts_ready, 3)

                def weight_remainders(stage):
                    cols = STAGES[stage]
                    dve.wait_ge(wparts_ready, 4 * stage + 3)
                    nc.vector.tensor_tensor(wctx[:, 1, cols], wstage[:, 0, cols], wctx[:, 0, cols].bitcast(F32),
                                            ALU.subtract).then_inc(wparts_ready, 1)
                    nc.vector.tensor_tensor(wctx[0:64, 3, cols], wstage[0:64, 1, cols], wctx[0:64, 2, cols].bitcast(F32),
                                            ALU.subtract).then_inc(wparts_ready, 1)

                nc.vector.memset(wctx[64:128, 3, :].bitcast(F32), 0.0).then_inc(wparts_ready, 1)

                def norm(b, k, stat_sem, var_sem, rstd_sem, ready):
                    carry()
                    nc.vector.bn_stats(stat[:, k, :], xs[:, b, :]).then_inc(stat_sem, 1)
                    dve.wait_ge(stat_sem, b + 1)
                    carry()
                    nc.vector.bn_aggr(mv[:, k, :], stat[:, k, :]).then_inc(var_sem, 1)

                def norm_apply(b, k, rstd_sem, ready):
                    dve.wait_ge(rstd_sem, b + 1)
                    nc.vector.tensor_scalar(xl[:, k, :], xs[:, b, :], mv[:, k, 0:1], rstd[:, k, :], ALU.subtract,
                                            ALU.mult).then_inc(ready, 1)

                def key_remainder(b, c):
                    bk, n = ring(f"k{c}", b - 1)
                    dve.wait_ge(k_hi, 2 * b + c + 1)
                    nc.vector.scalar_tensor_tensor(klo[:, c, :], bank(bk, MP), bk0s[:, c:c + 1], khi[:, c, :].bitcast(F32),
                                                   ALU.add, ALU.subtract).then_inc(ring_free[bk], 1)

                def bias_queries(b):
                    bk, n = ring("q", b - 1)
                    dve.wait_ge(ring_full[bk], n + 1)
                    nc.vector.tensor_tensor(qT[:], bank(bk, 2, S), bq0s[:].unsqueeze(2).broadcast_to([128, 2, S]),
                                            ALU.add).then_inc(ring_free[bk], 1)

                def step(b, p, attn, after, more):
                    t = b - 1

                    def drain_values(mc):
                        bk, n = ring(f"v{mc}", b)
                        dve.wait_ge(ring_full[bk], n + 1)
                        src = bank(bk, H0, D0)
                        if mc < 2:
                            nc.vector.tensor_tensor(v0[:, mc, :, 0:D0], src, bv0b[:].rearrange("p (h d) -> p h d", h=H0),
                                                    ALU.add).then_inc(ring_free[bk], 1)
                        else:
                            nc.vector.scalar_tensor_tensor(v0[:, mc, :, 0:D0], src, lastmask[:],
                                                           bv0m[:].rearrange("p (h d) -> p h d", h=H0), ALU.mult,
                                                           ALU.add).then_inc(ring_free[bk], 1)

                    def maxima(i):
                        bk, n = ring(f"s{i}", b)
                        dve.wait_ge(ring_full[bk], n + 1)
                        nc.vector.reduce_max(mx[:, i:i + 1], bank(bk, M, parts=S), AX.X).then_inc(ring_free[bk], 1)

                    def split(c):
                        last_uses = dict(ring(f"s{8 * c + i}", b) for i in range(4, 8))
                        for bk, n in last_uses.items():
                            dve.wait_ge(ring_free[bk], n + 1)
                        nc.vector.tensor_copy(parts[:, c, 0:8], mx[:, 8 * c:8 * c + 8]).then_inc(parts_hi, 1)
                        dve.wait_ge(parts_hi, 2 * b + c + 1)
                        nc.vector.tensor_tensor(parts[:, c, 32:40], mx[:, 8 * c:8 * c + 8], parts[:, c, 0:8],
                                                ALU.subtract).then_inc(parts_ready, 1)

                    def spread(c):
                        k, n = stb(f"m{c}", b)
                        dve.wait_ge(st_full[k], n + 1)
                        nc.vector.tensor_tensor(mxb[:, c, :, :],
                                                bank(4 + k, S, parts=96, dt=BF16).unsqueeze(1).broadcast_to([96, 8, S]),
                                                partmask[:].unsqueeze(2).broadcast_to([96, 8, S]), ALU.mult).then_inc(st_free[k], 1)

                    if attn:
                        drain_values(0)
                    if after:
                        dve.wait_ge(tail_full, tail("nat", t) + 1)
                        nat = bank(7, H0, 32, parts=S)
                        nc.vector.reciprocal(rden[:], nat[:, :, D0]).then_inc(rden_ready, 1)
                        dve.wait_ge(rden_ready, t + 1)
                        nc.vector.tensor_tensor(o[:, 0:D].rearrange("p (h d) -> p h d", h=H0), nat[:, :, 0:D0],
                                                rden[:].unsqueeze(2).broadcast_to([S, H0, D0]), ALU.mult).then_inc(tail_free, 1)
                    if attn:
                        drain_values(1)
                        drain_values(2)
                    if more:
                        norm(b + 1, 0, ln1_stat, ln1_var, ln1_rstd, xl1_ready)
                    if attn:
                        maxima(0)
                        maxima(1)
                    if after:
                        dve.wait_ge(tail_full, tail("h", t) + 1)
                        nc.vector.tensor_tensor(h[:], bank(7, HID, parts=S), b1b[:], ALU.add).then_inc(tail_free, 1)
                    if more:
                        split_mix(dve, b + 1, ctx_hi, ctx_mix)
                        norm_apply(b + 1, 0, ln1_rstd, xl1_ready)
                    if attn:
                        maxima(2)
                    if attn:
                        bk, n = ring("prod", b)
                        dve.wait_ge(ring_full[bk], n + 1)
                        if isinstance(b, int) and b == 0:
                            nc.vector.tensor_copy(prod[:], bank(bk, 2, D)).then_inc(ring_free[bk], 1)
                        else:
                            nc.vector.tensor_tensor(prod[:], bank(bk, 2, D), prod[:], ALU.add).then_inc(ring_free[bk], 1)
                    if attn:
                        maxima(3)
                        maxima(4)
                    if more:
                        key_remainder(b + 1, 0)
                    if attn:
                        maxima(5)
                    if after:
                        dve.wait_ge(tail_full, tail("y", t) + 1)
                        dve.wait_ge(biased, t + 1)
                        nc.vector.scalar_tensor_tensor(xs[:, t, :], bank(7, D, parts=S), tgate[0:S, 0:1], xs[:, t, :],
                                                       ALU.mult, ALU.add).then_inc(tail_free, 1)
                        dve.wait_ge(tail_free, tail("y", t) + 1)
                        norm(t, 1, ln2_stat, ln2_var, ln2_rstd, xl2_ready)
                    if attn:
                        maxima(6)
                        maxima(7)
                        split(0)
                    if more:
                        key_remainder(b + 1, 1)
                    if after:
                        norm_apply(t, 1, ln2_rstd, xl2_ready)
                    if attn:
                        spread(0)
                    if more:
                        bias_queries(b + 1)
                    if attn:
                        maxima(8)
                        maxima(9)
                    if attn:
                        for i in range(10, 16):
                            maxima(i)
                        split(1)
                        spread(1)
                    if after:
                        dve.wait_ge(tail_full, tail("qf", t) + 1)
                        nc.vector.tensor_tensor(qall[:, :, bass.ts(t, S)], bank(7, 4, S), bqfs[:].unsqueeze(2).broadcast_to([128, 4, S]),
                                                ALU.add).then_inc(tail_free, 1)
                    if after:
                        dve.wait_ge(tail_free, tail("qf", t) + 1)
                        carry()
                        for c in range(4):
                            nc.vector.bn_stats(qstat[:, c, t, :], qall[:, c, bass.ts(t, S)]).then_inc(qstat_done, 1)
                    if isinstance(b, int) and b == 0:
                        weight_remainders(1)
                        dve.wait_ge(mlp_loaded, NMLP)
                        dve.wait_ge(rest_loaded, 16)

                norm(0, 0, ln1_stat, ln1_var, ln1_rstd, xl1_ready)
                weight_remainders(0)
                dve.wait_ge(selected, 16)
                split_mix(dve, 0, ctx_hi, ctx_mix)
                norm_apply(0, 0, ln1_rstd, xl1_ready)
                dve.wait_ge(first_loaded, NFIRST)
                for c in range(2):
                    key_remainder(0, c)
                bias_queries(0)
                dve.wait_ge(loaded, NLOADED)
                dve.wait_ge(consts_ready, 6)
                steps(dve, step)

            @block.tensor
            def _(pe):
                pe.wait_ge(consts_ready, 3)
                pe.wait_ge(selected, 16)
                pe.wait_ge(wparts_ready, 5)

                def project(name, b, dst, pairs):
                    bk, n = ring(name, b)
                    need(pe, ring_free[bk], n)
                    for j in range(len(pairs)):
                        lhs, rhs = pairs[j]
                        last = nc.tensor.matmul(dst(bk), lhs, rhs, start=j == 0, stop=j == len(pairs) - 1)
                    last.then_inc(ring_full[bk], 1)

                def keys(b, c):
                    pe.wait_ge(ctx_lo, b + 1)
                    pe.wait_ge(ctx_mix, b + 1)
                    cols = slice(KEY0.start + 128 * c, KEY0.start + 128 * c + 128)
                    project(f"k{c}", b - 1, lambda k: bank(k, MP), [(wctx[:, w, cols], cparts[:, x, :]) for w, x in PASSES])

                def transpose_x(b):
                    bk, n = ring("xT", b - 1)
                    need(pe, ring_free[bk], n)
                    pe.wait_ge(xl1_ready, b + 1)
                    for k in range(2):
                        last = nc.tensor.transpose(bank(bk, 2, S)[:, k, :], xl[:, 0, 128 * k:128 * k + 128], ident[0:S, 0:S])
                    last.then_inc(ring_full[bk], 1)

                def queries(b):
                    xbk, xn = ring("xT", b - 1)
                    bk, n = ring("q", b - 1)
                    need(pe, ring_free[bk], n)
                    pe.wait_ge(ring_free[xbk], xn + 1)
                    for mo in range(2):
                        for k in range(2):
                            last = nc.tensor.matmul(bank(bk, 2, S)[:, mo, :], wq0[:, k, 128 * mo:128 * mo + 128], xT[:, k, :],
                                                    start=k == 0, stop=k == 1)
                    last.then_inc(ring_full[bk], 1)

                def step(b, p, attn, after, more):
                    t = b - 1

                    def open_tail(name):
                        need(pe, tail_free, tail(name, t))

                    def scores(*heads):
                        for i in heads:
                            bk, n = ring(f"s{i}", b)
                            need(pe, ring_free[bk], n)
                            c, hd = divmod(i, 8)
                            if c == 0 and hd % 2 == 0:
                                pe.wait_ge(stack_loaded[hd // 2], 6 * 16 * (b + 1))
                            nc.tensor.matmul(bank(bk, MP, parts=S), qstack[:, p, c, hd // 2, hd % 2, :], kstack[:, p, c, hd // 2, :],
                                             start=True, stop=True).then_inc(ring_full[bk], 1)

                    def put_parts(c):
                        k, n = stb(f"m{c}", b)
                        need(pe, st_free[k], n)
                        pe.wait_ge(parts_ready, 2 * b + c + 1)
                        nc.tensor.transpose(bank(4 + k, S, parts=96, dt=BF16), parts[:, c, :], identb[0:S, 0:S]).then_inc(st_full[k], 1)

                    def tscores(i):
                        g, mc = divmod(i, 3)
                        c = g // 2
                        hs = slice(4 * (g % 2), 4 * (g % 2) + 4)
                        if mc == 0 and g % 2 == 0:
                            k, n = stb(f"m{c}", b)
                            pe.wait_ge(st_free[k], n + 1)
                        k, n = stb(f"t{i}", b)
                        need(pe, st_free[k], n)
                        dst = bank(4 + k, 4 * S)
                        nc.tensor.matmul(dst, negones[:], mxb[:, c, hs, :].rearrange("p h s -> p (h s)"), start=True, stop=False)
                        for a in range(2):
                            q = 2 * (g % 2) + a
                            last = nc.tensor.matmul(dst[:, 2 * S * a:2 * S * a + 2 * S], kstack[:, p, c, q, chunk[mc]],
                                                    qstack[:, p, c, q, :, :].rearrange("p a s -> p (a s)"), start=False, stop=a == 1)
                        last.then_inc(st_full[k], 1)

                    def values(i):
                        g, mc = divmod(i, 3)
                        if i == 0:
                            need(pe, o_free, b)
                        k, n = stb(f"t{i}", b)
                        pe.wait_ge(st_free[k], n + 1)
                        for j in range(4):
                            last = nc.tensor.matmul(psum[32 * j:32 * j + 32, 6, g * S:(g + 1) * S], v0[:, mc, 4 * g + j, :],
                                                    prob[:, g % 2, mc, j, :], start=mc == 0, stop=mc == 2)
                        if i == 11:
                            last.then_inc(o_full, 1)

                    def values_of(mc):
                        project(f"v{mc}", b, lambda k: bank(k, D), [(cparts[:, x, chunk[mc]], wctx[:, w, VAL0]) for w, x in PASSES])

                    def expert_product(mo):
                        bk, n = ring("prod", b)
                        if mo == 0:
                            pe.wait_ge(e_loaded, 32 * b + 32)
                            need(pe, ring_free[bk], n)
                        for k in range(4):
                            last = nc.tensor.matmul(bank(bk, 2, D)[:, mo, :], e1[:, k, 128 * mo:128 * mo + 128], e2[:, k, :],
                                                    start=k == 0, stop=k == 3)
                        if mo == 1:
                            last.then_inc(ring_full[bk], 1)

                    def product_queries(half_):
                        for mo in (2 * half_, 2 * half_ + 1):
                            for k in range(2):
                                last = nc.tensor.matmul(bank(7, 4, S)[:, mo, :], wqf[:, k, 128 * mo:128 * mo + 128], xT2[:, k, :],
                                                        start=k == 0, stop=k == 1)
                        return last

                    if attn:
                        values_of(0)
                    if after:
                        pe.wait_ge(o_free, t + 1)
                        open_tail("nat")
                        for g in range(4):
                            last = nc.tensor.transpose(bank(7, 4, 128, parts=S)[:, g, :], oTp[:, g, :], ident[:])
                        last.then_inc(tail_full, 1)
                    if attn:
                        values_of(1)
                        values_of(2)
                    if after:
                        open_tail("oT")
                        for k in range(2):
                            last = nc.tensor.transpose(bank(7, 2, S)[:, k, :], o[:, 128 * k:128 * k + 128], ident[0:S, 0:S])
                        last.then_inc(tail_full, 1)

                    if attn:
                        expert_product(0)
                        scores(0, 1)
                    if after:
                        open_tail("h")
                        for k in range(2):
                            last = nc.tensor.matmul(bank(7, HID, parts=S), oT[:, k, :], w1s[:, k, :], start=k == 0, stop=k == 1)
                        last.then_inc(tail_full, 1)
                    if attn:
                        scores(2)
                        expert_product(1)
                        scores(3)
                    if after:
                        open_tail("hT")
                        for k in range(4):
                            last = nc.tensor.transpose(bank(7, 4, S)[:, k, :], h[:, 128 * k:128 * k + 128], ident[0:S, 0:S])
                        last.then_inc(tail_full, 1)
                    if attn:
                        scores(4)
                    if more:
                        keys(b + 1, 0)
                    if attn:
                        scores(5)
                    if after:
                        open_tail("y")
                        for k in range(4):
                            last = nc.tensor.matmul(bank(7, D, parts=S), hT[:, k, :], w2s[:, k, :], start=k == 0, stop=k == 3)
                        last.then_inc(tail_full, 1)
                    if attn:
                        scores(6, 7)
                    if more:
                        transpose_x(b + 1)
                        keys(b + 1, 1)
                        queries(b + 1)
                    if attn:
                        put_parts(0)
                        scores(8, 9)
                    if after:
                        pe.wait_ge(xl2_ready, t + 1)
                        open_tail("x2T")
                        for k in range(2):
                            last = nc.tensor.transpose(bank(7, 2, S)[:, k, :], xl[:, 1, 128 * k:128 * k + 128], ident[0:S, 0:S])
                        last.then_inc(tail_full, 1)
                    if attn:
                        scores(10)
                    if after:
                        open_tail("down")
                        for k in range(2):
                            last = nc.tensor.matmul(bank(7, NEXP, parts=S), xT2[:, k, :], downs[:, k, :], start=k == 0, stop=k == 1)
                        last.then_inc(tail_full, 1)
                    if attn:
                        scores(11)
                        tscores(0)
                        tscores(1)
                        for mc in range(3):
                            bk, n = ring(f"v{mc}", b)
                            pe.wait_ge(ring_free[bk], n + 1)
                        for i in range(2, 6):
                            scores(10 + i)
                            tscores(i)
                            values(i - 2)
                        values(4)
                    if after:
                        open_tail("qf")
                        product_queries(0)
                    if attn:
                        put_parts(1)
                    if after:
                        product_queries(1).then_inc(tail_full, 1)
                    if attn:
                        values(5)
                        for i in range(6, 12):
                            tscores(i)
                            if i >= 8:
                                values(i - 2)
                        values(10)
                        values(11)
                    if isinstance(b, int) and b == 0:
                        pe.wait_ge(mlp_loaded, NMLP)

                for c in range(2):
                    keys(0, c)
                transpose_x(0)
                pe.wait_ge(first_loaded, NFIRST)
                queries(0)
                steps(pe, step)

        early.close()
        agg = sb("agg", [128, 4, 2]); mean = sb("mean", [128, 1]); dev = sb("dev", [128, 4]); spreads = sb("spreads", [128, 4])
        varq = sb("varq", [128, 1]); rstdq = sb("rstdq", [128, 1]); qscale = sb("qscale", [128, 1]); qshift = sb("qshift", [128, 1])
        keysq = sb("keysq", [128, NKEY]); keyn = sb("keyn", [128, 1]); keyr = sb("keyr", [128, 1])
        keyd = sb("keyd", [128, 128]); keyT = sb("keyT", [128, 128])
        ups = sb("ups", [128, 2, D]); wq1 = sb("wq1", [128, 2, HID]); wo1 = sb("wo1", [128, 4, D])
        weights_loaded = sem("weights_loaded"); agg_ready = sem("agg_ready"); mean_summed = sem("mean_summed"); bn_step = sem("bn_step")
        spread_summed = sem("spread_summed"); varq_ready = sem("varq_ready"); rstdq_ready = sem("rstdq_ready")
        rstdq_eps = sem("rstdq_eps"); keyn_ready = sem("keyn_ready"); keyr_ready = sem("keyr_ready"); keyd_ready = sem("keyd_ready")
        keyT_full = sem("keyT_full"); gelu_done = sem("gelu_done")

        with nc.Block() as block:
            @block.sync
            def _(sp):
                for w, src in ((ups, up), (wq1, Wq1), (wo1, Wo1)):
                    sp.dma_start(w[:], src.rearrange("(k p) n -> p k n", p=128)).then_inc(weights_loaded, 16)
                sp.wait_ge(weights_loaded, 3 * 16)

            @block.scalar
            def _(act):
                nc.scalar.activation(hidden[:], hidden[:], ACT.Gelu).then_inc(gelu_done, 1)
                act.wait_ge(gelu_done, 1)

            @block.tensor
            def _(pe):
                pe.wait_ge(agg_ready, 4)
                nc.tensor.matmul(bank(0, 4), samedim[:], agg[:, :, 0], start=True, stop=True).then_inc(mean_summed, 1)
                pe.wait_ge(bn_step, 4)
                nc.tensor.matmul(bank(1, 4), samedim[:], spreads[:], start=True, stop=True).then_inc(spread_summed, 1)
                pe.wait_ge(keyd_ready, 4)
                nc.tensor.transpose(bank(2, 128), keyd[:], ident[:]).then_inc(keyT_full, 1)

            @block.gpsimd
            def _(pool):
                pool.wait_ge(keyn_ready, 1)
                nc.gpsimd.tensor_tensor(keyr[:], keyn[:], half[:], ALU.pow).then_inc(keyr_ready, 1)
                pool.wait_ge(varq_ready, 1)
                nc.gpsimd.tensor_scalar(varq[:], varq[:], EPS, None, ALU.add).then_inc(rstdq_eps, 1)
                pool.wait_ge(rstdq_eps, 1)
                nc.gpsimd.tensor_tensor(rstdq[:], varq[:], half[:], ALU.pow).then_inc(rstdq_ready, 1)

            @block.vector
            def _(dve):
                done = [0]

                def then(instruction):
                    done[0] += 1
                    instruction.then_inc(bn_step, 1)
                    dve.wait_ge(bn_step, done[0])

                for c in range(4):
                    nc.vector.bn_aggr(agg[:, c, :], qstat[:, c, :, :].rearrange("p b s -> p (b s)")).then_inc(agg_ready, 1)
                dve.wait_ge(agg_ready, 4)
                dve.wait_ge(mean_summed, 1)
                then(nc.vector.reduce_sum(mean[:], bank(0, 4), AX.X))
                then(nc.vector.tensor_scalar(dev[:], agg[:, :, 0], mean[:], None, ALU.subtract))
                then(nc.vector.tensor_tensor(dev[:], dev[:], dev[:], ALU.mult))
                then(nc.vector.tensor_tensor(spreads[:], dev[:], agg[:, :, 1], ALU.add))
                then(nc.vector.tensor_tensor(keysq[:], keys[:], keys[:], ALU.mult))
                then(nc.vector.reduce_sum(keyn[:], keysq[:], AX.X))
                nc.vector.tensor_scalar(keyn[:], keyn[:], TINY, None, ALU.max).then_inc(keyn_ready, 1)
                then(nc.vector.memset(keyd[:], 0.0))
                dve.wait_ge(spread_summed, 1)
                nc.vector.reduce_sum(varq[:], bank(1, 4), AX.X).then_inc(varq_ready, 1)
                dve.wait_ge(keyr_ready, 1)
                for i in range(4):
                    q = slice(32 * i, 32 * i + 32)
                    nc.vector.tensor_scalar(keyd[q, q], keys[q, :], keyr[q, :], None, ALU.mult).then_inc(keyd_ready, 1)
                dve.wait_ge(rstdq_ready, 1)
                then(nc.vector.tensor_tensor(qscale[:], rstdq[:], gam[:], ALU.mult))
                then(nc.vector.tensor_tensor(mean[:], mean[:], qscale[:], ALU.mult))
                then(nc.vector.tensor_tensor(qshift[:], bet[:], mean[:], ALU.subtract))
                dve.wait_ge(keyT_full, 1)
                then(nc.vector.tensor_copy(keyT[:], bank(2, 128)))

        kT1 = sb("kT1", [128, 4, M]); v1 = sb("v1", [128, 3, H1, D1]); qz1 = sb("qz1", [128, 4, 2, S])
        negmax = sb("negmax", [S, H1]); den1 = sb("den1", [S, H1]); rden1 = sb("rden1", [S, H1])
        p1 = sb("p1", [S, H1, M]); pT1 = sb("pT1", [128, H1, 3, S])
        qn = sb("qn", [128, 4, S]); qsq = sb("qsq", [128, 4, S]); n2s = sb("n2s", [S, 16]); rn = sb("rn", [S, 16])
        FILL, TAKEN = -10.0, 10.0
        score = sb("score", [S, 16, NKEY + TOP]); top8 = sb("top8", [S, 16, 8]); marked = sb("marked", [S, 16, NKEY + TOP])
        expo = sb("expo", [S, 16, NKEY]); kept = sb("kept", [S, 16, NKEY]); den = sb("den", [S, 16]); rdn = sb("rdn", [S, 16])
        prb = sb("prb", [S, 8, 2, NKEY]); outer = sb("outer", [S, 8, NEXP]); wt = sb("wt", [S, NEXP]); beyond = sb("beyond", [S, 1])
        gw = sb("gw", [S, NEXP]); gT = sb("gT", [128, 2, S])
        ctx3_loaded = sem("ctx3_loaded"); ctx3_hi = sem("ctx3_hi"); ctx3_lo = sem("ctx3_lo"); ctx3_mix = sem("ctx3_mix")
        filled = sem("filled"); stored = sem("stored"); negmax_ready = sem("negmax_ready")
        a_full = [sem(f"a_full{i}") for i in range(4)]
        a_free = [sem(f"a_free{i}") for i in range(4)]
        t_full = sem("t_full"); t_free = sem("t_free"); pv_full = sem("pv_full"); pv_free = sem("pv_free")
        f_full = sem("f_full"); f_free = sem("f_free"); r_full = sem("r_full"); r_free = sem("r_free")
        ln3_stat = sem("ln3_stat"); ln3_var = sem("ln3_var"); ln3_eps = sem("ln3_eps"); ln3_rstd = sem("ln3_rstd"); xl3_ready = sem("xl3_ready")
        ln4_stat = sem("ln4_stat"); ln4_var = sem("ln4_var"); ln4_eps = sem("ln4_eps"); ln4_rstd = sem("ln4_rstd"); xl4_ready = sem("xl4_ready")
        biased3 = sem("biased3"); rden1_ready = sem("rden1_ready")
        qn_ready = sem("qn_ready"); qsq_ready = sem("qsq_ready"); rn_ready = sem("rn_ready"); expo_ready = sem("expo_ready")
        top_ready = sem("top_ready"); floor_set = sem("floor_set"); marked_ready = sem("marked_ready"); kept_ready = sem("kept_ready")
        den_ready = sem("den_ready"); rdn_ready = sem("rdn_ready"); prb_ready = sem("prb_ready"); outer_ready = sem("outer_ready")
        halved = sem("halved"); wt_ready = sem("wt_ready"); beyond_ready = sem("beyond_ready"); wt_whole = sem("wt_whole"); gw_ready = sem("gw_ready")

        A3 = {n: i for i, n in enumerate(["k0", "k1", "q", "k2", "k3", "v0", "v1", "v2"] + [f"s{i}" for i in range(H1)])}
        R3 = ["oT", "y", "x4T", "out"]
        F3 = ["n2", "gT", "y2", "sc", "x3T"]

        def a3(name, b):
            return A3[name] % 4, b * (len(A3) // 4) + A3[name] // 4

        def f3(name, b):
            if not isinstance(b, int):
                return 7 + 5 * b + F3.index(name)
            uses = [(s, n) for s in range(-2, B) for n in F3 if (s < B - 2 if n in ("n2", "sc") else -1 <= s < B - 1)]
            return uses.index((b, name))

        def r3(name, t):
            return t * len(R3) + R3.index(name)

        def steps(eng, step):
            step(-2, False, False, False, True)
            step(-1, False, False, True, True)
            step(0, True, False, True, True)
            with eng.Fori(1, B - 2) as b:
                step(b, True, True, True, True)
            step(B - 2, True, True, True, False)
            step(B - 1, True, True, False, False)
            step(B, False, True, False, False)

        with nc.Block() as block:
            @block.sync
            def _(sp):
                def store(t):
                    sp.wait_ge(r_free, r3("out", t) + 1)
                    sp.dma_start(out[t], xs[:, t, :]).then_inc(stored, 16)

                load_context(sp, 0, ctx3_loaded)

                def next_context(b):
                    sp.wait_ge(ctx3_lo, b)
                    sp.wait_ge(ctx3_mix, b)
                    load_context(sp, b, ctx3_loaded)

                next_context(1)
                with sp.Fori(1, B - 1) as b:
                    next_context(b + 1)
                    store(b - 1)
                store(B - 2)
                store(B - 1)
                sp.wait_ge(stored, 16 * B)

            @block.gpsimd
            def _(pool):
                nc.gpsimd.memset(score[:], FILL).then_inc(filled, 1)

                def root(b, k, var, eps_added, ready):
                    pool.wait_ge(var, b + 1)
                    nc.gpsimd.tensor_tensor(vare[:, k, :], mv[:, k, 1:2], eps[:], ALU.add).then_inc(eps_added, 1)
                    pool.wait_ge(eps_added, b + 1)
                    nc.gpsimd.tensor_tensor(rstd[:, k, :], vare[:, k, :], half[0:S, :], ALU.pow).then_inc(ready, 1)

                def step(b, attn, after, mix, choose):
                    t, m, f = b - 1, b + 1, b + 2
                    if choose:
                        pool.wait_ge(qn_ready, f + 1)
                        nc.gpsimd.tensor_tensor(qsq[:], qn[:], qn[:], ALU.mult).then_inc(qsq_ready, 1)
                    if attn:
                        pool.wait_ge(xl3_ready, b + 1)
                        nc.gpsimd.tensor_tensor(xs[:, b, :], xs[:, b, :], gbo[:], ALU.add).then_inc(biased3, 1)
                    if after:
                        root(t, 1, ln4_var, ln4_eps, ln4_rstd)
                    if mix:
                        pool.wait_ge(halved, 2 * m + 1)
                        nc.gpsimd.tensor_tensor(outer[:, 0:2, :], outer[:, 0:2, :], outer[:, 2:4, :], ALU.add).then_inc(halved, 1)
                        pool.wait_ge(halved, 2 * m + 2)
                        nc.gpsimd.tensor_tensor(wt[:], outer[:, 0, :], outer[:, 1, :], ALU.add).then_inc(wt_ready, 1)
                    if choose:
                        pool.wait_ge(f_free, f3("n2", b) + 1)
                        nc.gpsimd.tensor_tensor(rn[:], n2s[:], half[0:S, :].broadcast_to([S, 16]), ALU.pow).then_inc(rn_ready, 1)
                    if mix:
                        split_lo(pool, b + 1, ctx3_hi, ctx3_lo)
                        root(m, 0, ln3_var, ln3_eps, ln3_rstd)

                steps(pool, step)

            @block.scalar
            def _(act):
                def drain(name, b, dst, src, func=ACT.Copy, **kw):
                    k, n = a3(name, b)
                    act.wait_ge(a_full[k], n + 1)
                    nc.scalar.activation(dst, src(k), func, **kw).then_inc(a_free[k], 1)

                def step(b, attn, after, mix, choose):
                    t, m, f = b - 1, b + 1, b + 2
                    if choose:
                        nc.scalar.activation(qn[:], qall[:, :, bass.ts(f, S)], ACT.Identity, scale=qscale[:],
                                             bias=qshift[:]).then_inc(qn_ready, 1)
                    if attn:
                        for c in range(2):
                            drain(f"k{c}", b, kT1[:, c, :], lambda k: bank(k, M))
                    if after:
                        act.wait_ge(r_full, r3("oT", t) + 1)
                        nc.scalar.activation(oT[:], bank(7, 4, S), ACT.Copy).then_inc(r_free, 1)
                    if attn:
                        for c in range(2, 4):
                            drain(f"k{c}", b, kT1[:, c, :], lambda k: bank(k, M))
                        for mc in range(2):
                            drain(f"v{mc}", b, v1[:, mc, :, :], lambda k: bank(k, H1, D1), ACT.Identity)
                        drain("v2", b, v1[:, 2, :, :], lambda k: bank(k, H1, D1), ACT.Identity, scale=lastmask[:])
                    if mix:
                        split_hi(act, b + 1, ctx3_loaded, ctx3_hi)

                    def exponentials(*heads):
                        for h in heads:
                            if attn:
                                k, n = a3(f"s{h}", b)
                                act.wait_ge(negmax_ready, H1 * b + h + 1)
                                nc.scalar.activation(p1[:, h, :], bank(k, M, parts=S), ACT.Exp, bias=negmax[:, h:h + 1],
                                                     accum_out=den1[:, h:h + 1]).then_inc(a_free[k], 1)

                    def drain_transposed(*heads):
                        for h in heads:
                            if attn:
                                act.wait_ge(t_full, H1 * b + h + 1)
                                nc.scalar.activation(pT1[:, h, :, :], bank(4, 3, S), ACT.Copy).then_inc(t_free, 1)

                    exponentials(0, 1)
                    drain_transposed(0)
                    if after:
                        act.wait_ge(r_full, r3("x4T", t) + 1)
                        nc.scalar.activation(xT2[:], bank(7, 2, S), ACT.Copy).then_inc(r_free, 1)
                    exponentials(2)
                    if mix:
                        act.wait_ge(f_full, f3("gT", b) + 1)
                        nc.scalar.activation(gT[:], bank(6, 2, S), ACT.Copy).then_inc(f_free, 1)
                    exponentials(3)
                    for h in range(1, 5):
                        drain_transposed(h)
                        exponentials(h + 3)
                    drain_transposed(5, 6)
                    if mix:
                        act.wait_ge(f_full, f3("x3T", b) + 1)
                        nc.scalar.activation(xT[:], bank(6, 2, S), ACT.Copy).then_inc(f_free, 1)
                    drain_transposed(7)
                    if choose:
                        act.wait_ge(f_free, f3("sc", b) + 1)
                        nc.scalar.activation(expo[:], score[:, :, 0:NKEY], ACT.Exp).then_inc(expo_ready, 1)

                steps(act, step)

            @block.vector
            def _(dve):
                def carry():
                    nc.vector.memset(scratch[:], 0.0)

                dve.wait_ge(filled, 1)

                def norm(b, k, stat_sem, var_sem):
                    carry()
                    nc.vector.bn_stats(stat[:, k, :], xs[:, b, :]).then_inc(stat_sem, 1)
                    dve.wait_ge(stat_sem, b + 1)
                    carry()
                    nc.vector.bn_aggr(mv[:, k, :], stat[:, k, :]).then_inc(var_sem, 1)

                def norm_apply(b, k, rstd_sem, ready):
                    dve.wait_ge(rstd_sem, b + 1)
                    nc.vector.tensor_scalar(xl[:, k, :], xs[:, b, :], mv[:, k, 0:1], rstd[:, k, :], ALU.subtract,
                                            ALU.mult).then_inc(ready, 1)

                def step(b, attn, after, mix, choose):
                    t, m, f = b - 1, b + 1, b + 2
                    if after:
                        dve.wait_ge(pv_full, t + 1)
                        nc.vector.reciprocal(rden1[:], den1[:]).then_inc(rden1_ready, 1)
                        dve.wait_ge(rden1_ready, t + 1)
                        nc.vector.tensor_tensor(o[:].rearrange("p (h d) -> p h d", h=H1), bank(5, H1, D1, parts=S),
                                                rden1[:].unsqueeze(2).broadcast_to([S, H1, D1]), ALU.mult).then_inc(pv_free, 1)
                    if mix:
                        dve.wait_ge(marked_ready, 16 * m + 16)
                        dve.wait_ge(expo_ready, m + 1)
                        nc.vector.scalar_tensor_tensor(kept[:], marked[:, :, 0:NKEY], TAKEN / 2, expo[:], ALU.is_ge,
                                                       ALU.mult).then_inc(kept_ready, 1)
                        dve.wait_ge(kept_ready, m + 1)
                        nc.vector.reduce_sum(den[:], kept[:], AX.X).then_inc(den_ready, 1)
                        dve.wait_ge(den_ready, m + 1)
                        nc.vector.reciprocal(rdn[:], den[:]).then_inc(rdn_ready, 1)
                        dve.wait_ge(rdn_ready, m + 1)
                        nc.vector.tensor_tensor(prb[:].rearrange("p h s k -> p (h s) k"), kept[:], rdn[:].unsqueeze(2).broadcast_to([S, 16, NKEY]),
                                                ALU.mult).then_inc(prb_ready, 1)
                        dve.wait_ge(prb_ready, m + 1)
                    if attn:
                        k, n = a3("q", b)
                        dve.wait_ge(a_full[k], n + 1)
                        nc.vector.tensor_tensor(qz1[:], bank(k, 4, S).unsqueeze(2).broadcast_to([128, 4, 2, S]),
                                                headmask1[:].unsqueeze(1).unsqueeze(3).broadcast_to([128, 4, 2, S]),
                                                ALU.mult).then_inc(a_free[k], 1)
                    if mix:
                        nc.vector.tensor_tensor(outer[:].rearrange("p h (i j) -> p h i j", i=8),
                                                prb[:, :, 0, 0:8].unsqueeze(3).broadcast_to([S, 8, 8, NKEY]),
                                                prb[:, :, 1, :].unsqueeze(2).broadcast_to([S, 8, 8, NKEY]), ALU.mult).then_inc(outer_ready, 1)
                        nc.vector.reduce_sum(beyond[:], prb[:, :, 0, 8:NKEY], AX.XY).then_inc(beyond_ready, 1)
                    if after:
                        dve.wait_ge(r_full, r3("y", t) + 1)
                        dve.wait_ge(biased3, t + 1)
                        nc.vector.scalar_tensor_tensor(xs[:, t, :], bank(7, D, parts=S), tgate[0:S, 1:2], xs[:, t, :], ALU.mult,
                                                       ALU.add).then_inc(r_free, 1)
                        dve.wait_ge(r_free, r3("y", t) + 1)
                        norm(t, 1, ln4_stat, ln4_var)
                    if mix:
                        dve.wait_ge(outer_ready, m + 1)
                        nc.vector.tensor_tensor(outer[:, 0:4, :], outer[:, 0:4, :], outer[:, 4:8, :], ALU.add).then_inc(halved, 1)
                    if choose:
                        dve.wait_ge(f_full, f3("n2", b) + 1)
                        nc.vector.tensor_scalar(n2s[:], bank(6, 16, parts=S), TINY, None, ALU.max).then_inc(f_free, 1)
                    if after:
                        norm_apply(t, 1, ln4_rstd, xl4_ready)

                    def maxima(*heads):
                        for i in heads:
                            if attn:
                                k, n = a3(f"s{i}", b)
                                dve.wait_ge(a_full[k], n + 1)
                                nc.vector.tensor_reduce(negmax[:, i:i + 1], bank(k, M, parts=S), AX.X, ALU.max,
                                                        negate=True).then_inc(negmax_ready, 1)

                    def largest(groups):
                        for g in groups:
                            nc.vector.max(top8[:, g, :], score[:, g, :]).then_inc(top_ready, 1)

                    maxima(0, 1)
                    if mix:
                        dve.wait_ge(beyond_ready, m + 1)
                        dve.wait_ge(wt_ready, m + 1)
                        nc.vector.tensor_tensor(wt[:, NEXP - 1:NEXP], wt[:, NEXP - 1:NEXP], beyond[:], ALU.add).then_inc(wt_whole, 1)
                        dve.wait_ge(wt_whole, m + 1)
                        nc.vector.tensor_tensor(gw[:], wt[:], hidden[:, m, :], ALU.mult).then_inc(gw_ready, 1)
                    maxima(2, 3)
                    if mix:
                        dve.wait_ge(f_full, f3("y2", b) + 1)
                        nc.vector.scalar_tensor_tensor(xs[:, m, :], bank(6, D, parts=S), tgate[0:S, 2:3], xs[:, m, :], ALU.mult,
                                                       ALU.add).then_inc(f_free, 1)
                        dve.wait_ge(f_free, f3("y2", b) + 1)
                        norm(m, 0, ln3_stat, ln3_var)
                    maxima(4)
                    if choose:
                        dve.wait_ge(f_full, f3("sc", b) + 1)
                        dve.wait_ge(rn_ready, f + 1)
                        nc.vector.tensor_tensor(score[:, :, 0:NKEY], bank(6, 16, NKEY, parts=S), rn[:].unsqueeze(2).broadcast_to([S, 16, NKEY]),
                                                ALU.mult).then_inc(f_free, 1)
                    if mix:
                        norm_apply(m, 0, ln3_rstd, xl3_ready)
                    maxima(5)
                    if choose:
                        dve.wait_ge(f_free, f3("sc", b) + 1)
                        carry()
                        largest(range(8))
                    maxima(6)
                    if choose:
                        largest(range(8, 16))
                        dve.wait_ge(top_ready, 16 * f + 16)
                        nc.vector.memset(top8[:, :, TOP:8], FILL).then_inc(floor_set, 1)
                    maxima(7)
                    if mix:
                        split_mix(dve, b + 1, ctx3_hi, ctx3_mix)
                    if choose:
                        dve.wait_ge(floor_set, f + 1)
                        carry()
                        for g in range(16):
                            nc.vector.match_replace(marked[:, g, :], top8[:, g, :], score[:, g, :], TAKEN).then_inc(marked_ready, 1)
                    if after:
                        dve.wait_ge(r_full, r3("out", t) + 1)
                        nc.vector.scalar_tensor_tensor(xs[:, t, :], bank(7, D, parts=S), tgate[0:S, 3:4], xs[:, t, :], ALU.mult,
                                                       ALU.add).then_inc(r_free, 1)

                steps(dve, step)

            @block.tensor
            def _(pe):
                def step(b, attn, after, mix, choose):
                    t, m, f = b - 1, b + 1, b + 2

                    def project(name, dst, pairs):
                        k, n = a3(name, b)
                        need(pe, a_free[k], n)
                        for j in range(len(pairs)):
                            last = nc.tensor.matmul(dst(k), pairs[j][0], pairs[j][1], start=j == 0, stop=j == len(pairs) - 1)
                        last.then_inc(a_full[k], 1)

                    def keys_of(c):
                        project(f"k{c}", lambda k: bank(k, MP), [(wctx[:, w, KEY1.start + 128 * c:KEY1.start + 128 * c + 128], cparts[:, x, :]) for w, x in PASSES])

                    def values_of(mc):
                        project(f"v{mc}", lambda k: bank(k, HID), [(cparts[:, x, chunk[mc]], wctx[:, w, VAL1]) for w, x in PASSES])

                    def transposed(h):
                        if attn:
                            need(pe, t_free, H1 * b + h)
                            k, n = a3(f"s{h}", b)
                            pe.wait_ge(a_free[k], n + 1)
                            for mc in range(3):
                                last = nc.tensor.transpose(bank(4, 3, S)[:, mc, :], p1[:, h, chunk[mc]], ident[0:S, 0:S])
                            last.then_inc(t_full, 1)

                    def attend(h):
                        if attn:
                            if h == 0:
                                need(pe, pv_free, b)
                            pe.wait_ge(t_free, H1 * b + h + 1)
                            for mc in range(3):
                                last = nc.tensor.matmul(bank(5, H1, D1, parts=S)[:, h, :], pT1[:, h, mc, :], v1[:, mc, h, :],
                                                        start=mc == 0, stop=mc == 2)
                            if h == H1 - 1:
                                last.then_inc(pv_full, 1)

                    def scores(h):
                        if attn:
                            k, n = a3(f"s{h}", b)
                            need(pe, a_free[k], n)
                            nc.tensor.matmul(bank(k, M, parts=S), qz1[:, h // 2, h % 2, :], kT1[:, h // 2, :], start=True,
                                             stop=True).then_inc(a_full[k], 1)

                    if attn:
                        pe.wait_ge(ctx3_lo, b + 1)
                        pe.wait_ge(ctx3_mix, b + 1)
                        keys_of(0)
                        keys_of(1)
                    if after:
                        need(pe, r_free, r3("oT", t))
                        pe.wait_ge(pv_free, t + 1)
                        for k in range(4):
                            last = nc.tensor.transpose(bank(7, 4, S)[:, k, :], o[:, 128 * k:128 * k + 128], ident[0:S, 0:S])
                        last.then_inc(r_full, 1)
                    if attn:
                        k, n = a3("q", b)
                        need(pe, a_free[k], n)
                        pe.wait_ge(f_free, f3("x3T", b - 1) + 1)
                        for mo in range(4):
                            for j in range(2):
                                last = nc.tensor.matmul(bank(k, 4, S)[:, mo, :], wq1[:, j, 128 * mo:128 * mo + 128], xT[:, j, :],
                                                        start=j == 0, stop=j == 1)
                        last.then_inc(a_full[k], 1)
                        keys_of(2)
                        keys_of(3)
                    if after:
                        need(pe, r_free, r3("y", t))
                        for k in range(4):
                            last = nc.tensor.matmul(bank(7, D, parts=S), oT[:, k, :], wo1[:, k, :], start=k == 0, stop=k == 3)
                        last.then_inc(r_full, 1)
                    if choose:
                        need(pe, f_free, f3("n2", b))
                        pe.wait_ge(qsq_ready, f + 1)
                        for c in range(4):
                            last = nc.tensor.matmul(bank(6, 4, 4, parts=S)[:, c, :], qsq[:, c, :], ones4[:], start=True, stop=True)
                        last.then_inc(f_full, 1)
                    if attn:
                        values_of(0)
                        values_of(1)
                        values_of(2)
                    scores(0)
                    scores(1)
                    scores(2)
                    if after:
                        need(pe, r_free, r3("x4T", t))
                        pe.wait_ge(xl4_ready, t + 1)
                        for k in range(2):
                            last = nc.tensor.transpose(bank(7, 2, S)[:, k, :], xl[:, 1, 128 * k:128 * k + 128], ident[0:S, 0:S])
                        last.then_inc(r_full, 1)
                    transposed(0)
                    scores(3)
                    if mix:
                        need(pe, f_free, f3("gT", b))
                        pe.wait_ge(gw_ready, m + 1)
                        for k in range(2):
                            last = nc.tensor.transpose(bank(6, 2, S)[:, k, :], gw[:, 128 * k:128 * k + 128], ident[0:S, 0:S])
                        last.then_inc(f_full, 1)
                    transposed(1)
                    attend(0)
                    if mix:
                        need(pe, f_free, f3("y2", b))
                        for k in range(2):
                            last = nc.tensor.matmul(bank(6, D, parts=S), gT[:, k, :], ups[:, k, :], start=k == 0, stop=k == 1)
                        last.then_inc(f_full, 1)
                    scores(4)
                    transposed(2)
                    attend(1)
                    if choose:
                        need(pe, f_free, f3("sc", b))
                        for c in range(4):
                            last = nc.tensor.matmul(bank(6, 4, 128, parts=S)[:, c, :], qn[:, c, :], keyT[:], start=True, stop=True)
                        last.then_inc(f_full, 1)
                    scores(5)
                    transposed(3)
                    attend(2)
                    scores(6)
                    transposed(4)
                    attend(3)
                    scores(7)
                    transposed(5)
                    attend(4)
                    if after:
                        need(pe, r_free, r3("out", t))
                        for k in range(2):
                            last = nc.tensor.matmul(bank(7, D, parts=S), xT2[:, k, :], prod[:, k, :], start=k == 0, stop=k == 1)
                        last.then_inc(r_full, 1)
                    transposed(6)
                    attend(5)
                    if mix:
                        pe.wait_ge(xl3_ready, m + 1)
                        need(pe, f_free, f3("x3T", b))
                        for k in range(2):
                            last = nc.tensor.transpose(bank(6, 2, S)[:, k, :], xl[:, 0, 128 * k:128 * k + 128], ident[0:S, 0:S])
                        last.then_inc(f_full, 1)
                    transposed(7)
                    attend(6)
                    attend(7)

                steps(pe, step)



_INS = ["x", "ctxT", "g_xattn", "g_ffn", "L0_xattn_Wq", "L0_xattn_bq", "L0_xattn_Wk", "L0_xattn_bk", "L0_xattn_Wv", "L0_xattn_bv",
        "L0_xattn_W1", "L0_xattn_b1", "L0_xattn_W2", "L0_xattn_b2", "L0_ffn_Wq", "L0_ffn_bq", "L0_ffn_bn_gamma", "L0_ffn_bn_beta",
        "L0_ffn_sub_key0", "L0_ffn_sub_key1", "downT", "L0_ffn_expert_up", "L1_xattn_Wq", "L1_xattn_Wk", "L1_xattn_Wv",
        "L1_xattn_Wo", "L1_xattn_bo", "w1T", "w2"]


def kernel(**inputs):
    import numpy as _np
    import concourse.bacc as _bacc
    from concourse import mybir as _mybir
    from concourse.bass_utils import run_bass_kernel_spmd as _run

    laid = {n: _np.asarray(a) for n, a in inputs.items()}
    laid["ctxT"] = laid["ctx_768"].transpose(0, 2, 1)
    for n, k in (("L0_xattn_bq", 2), ("L0_xattn_bk", 2), ("L0_ffn_bq", 4)):
        laid[n] = laid[n].reshape(k, 128).T
    laid["downT"] = laid["L0_ffn_expert_down"].T
    laid["w1T"] = laid["L1_ffn_w1"].transpose(0, 2, 1).reshape(B, 128, 4, D)
    laid["w2"] = laid["L1_ffn_w2"].reshape(B, 128, 4, D)

    nc = _bacc.Bacc("TRN2", target_bir_lowering=False, num_devices=1)
    arrays, args = {}, []
    for name in _INS:
        a = _np.ascontiguousarray(laid[name])
        arrays[f"in_{name}"] = a
        args.append(nc.dram_tensor(f"in_{name}", a.shape, _mybir.dt.from_np(a.dtype), kind="ExternalInput").ap())
    args.append(nc.dram_tensor("out_0", (B, S, D), _mybir.dt.float32, kind="ExternalOutput").ap())
    program(nc, *args)
    r = _run(nc, [arrays], core_ids=[0])
    return r.results[0]["out_0"]
```
